# Optimizing a Trainium2 kernel written in Bass

```python
import numpy as np
import jax
import jax.numpy as jnp

def _softmax(x, axis=-1):
    return jax.nn.softmax(x, axis=axis)

def _gelu(x):
    return jax.nn.gelu(x, approximate=True)

def _silu(x):
    return jax.nn.silu(x)

def _sigmoid(x):
    return jax.nn.sigmoid(x)

def _layernorm(x, axis=-1, eps=1e-05):
    m = jnp.mean(x, axis=axis, keepdims=True)
    v = jnp.var(x, axis=axis, keepdims=True)
    return (x - m) / jnp.sqrt(v + eps)

def _scatter_add(tgt, idx, src, axis=0):
    return tgt.at[idx].add(src)

def _segment_sum(src, seg, n):
    return jax.ops.segment_sum(src, seg, n)
kernel_name = 'mk_adaln_d1_jaxref_r4_bb6126'

def setup_inputs(seed: int=0):
    np.random.seed(seed)
    _w = jnp.asarray

    def _L0_attn_setup():
        import jax, jax.numpy as jnp
        import numpy as np
        import math
        B, S, E = (2, 512, 256)
        H, DC, DR = (16, 64, 128)
        HD = E // H

        def _linear_params(key, din, dout):
            k1, k2 = jax.random.split(key)
            bound = 1.0 / math.sqrt(din)
            w = jax.random.uniform(k1, (din, dout), minval=-bound, maxval=bound, dtype=jnp.float32)
            b = jax.random.uniform(k2, (dout,), minval=-bound, maxval=bound, dtype=jnp.float32)
            return (w, b)

        def _gelu(x):
            return jax.nn.gelu(x, approximate=False)

        def _rope_cos_sin(seq_len, d_rope):
            inv_freq = 1.0 / 10000.0 ** (jnp.arange(0, d_rope, 2, dtype=jnp.float32) / d_rope)
            t = jnp.arange(seq_len, dtype=jnp.float32)
            freqs = t[:, None] * inv_freq[None, :]
            emb = jnp.concatenate([freqs, freqs], axis=-1)
            return (jnp.cos(emb), jnp.sin(emb))

        def _apply_rope(x, cos, sin):
            d = x.shape[-1]
            x1, x2 = (x[..., :d // 2], x[..., d // 2:])
            rot = jnp.concatenate([-x2, x1], axis=-1)
            return x * cos + rot * sin
        key = jax.random.key(seed)
        ks = jax.random.split(key, 10)
        x = jax.random.normal(ks[0], (B, S, E), dtype=jnp.float32)
        wq, bq = _linear_params(ks[1], E, DC)
        wqc, bqc = _linear_params(ks[2], DC, E - DR)
        wqr, bqr = _linear_params(ks[3], E, DR)
        wkv, bkv = _linear_params(ks[4], E, DC)
        wkr, bkr = _linear_params(ks[5], E, DR)
        wkc, bkc = _linear_params(ks[6], DC, E - DR)
        wv, bv = _linear_params(ks[7], DC, E)
        wo, bo = _linear_params(ks[8], E, E)
        return dict(x=x, wq=wq, bq=bq, wqc=wqc, bqc=bqc, wqr=wqr, bqr=bqr, wkv=wkv, bkv=bkv, wkr=wkr, bkr=bkr, wkc=wkc, bkc=bkc, wv=wv, bv=bv, wo=wo, bo=bo)
    _L0_attn_in = _L0_attn_setup()

    def _L0_ffn_setup():
        import jax, jax.numpy as jnp
        import numpy as np
        H = 256
        I = 128
        E = 8
        TOP_K = 2
        N_SHARED = 2
        SHARED_I = I * N_SHARED
        SCALE = 2.5
        NORM_TOPK = True
        B, S = (2, 256)

        def _swiglu(x, wg, wu, wd):
            g = x @ wg.T
            u = x @ wu.T
            return jax.nn.silu(g) * u @ wd.T
        key = jax.random.key(seed)
        ks = jax.random.split(key, 8)
        std = 0.02
        return {'hidden_states': jax.random.normal(ks[0], (B, S, H), jnp.float32), 'gate_weight': jax.random.normal(ks[1], (E, H), jnp.float32) * std, 'w_gate': jax.random.normal(ks[2], (E, I, H), jnp.float32) * std, 'w_up': jax.random.normal(ks[3], (E, I, H), jnp.float32) * std, 'w_down': jax.random.normal(ks[4], (E, H, I), jnp.float32) * std, 'ws_gate': jax.random.normal(ks[5], (SHARED_I, H), jnp.float32) * std, 'ws_up': jax.random.normal(ks[6], (SHARED_I, H), jnp.float32) * std, 'ws_down': jax.random.normal(ks[7], (H, SHARED_I), jnp.float32) * std}
    _L0_ffn_in = _L0_ffn_setup()
    _L0_c = _w((lambda *s: np.random.randn(*s).astype(np.float32) * 0.05)(4, 256))
    _L0_wmod = _w((lambda *s: np.random.randn(*s).astype(np.float32) * 0.05)(256, 6 * 256) * 256 ** (-0.5))
    _d = {'L0_attn_x': _L0_attn_in['x'], 'L0_attn_wq': _L0_attn_in['wq'], 'L0_attn_bq': _L0_attn_in['bq'], 'L0_attn_wqc': _L0_attn_in['wqc'], 'L0_attn_bqc': _L0_attn_in['bqc'], 'L0_attn_wqr': _L0_attn_in['wqr'], 'L0_attn_bqr': _L0_attn_in['bqr'], 'L0_attn_wkv': _L0_attn_in['wkv'], 'L0_attn_bkv': _L0_attn_in['bkv'], 'L0_attn_wkr': _L0_attn_in['wkr'], 'L0_attn_bkr': _L0_attn_in['bkr'], 'L0_attn_wkc': _L0_attn_in['wkc'], 'L0_attn_bkc': _L0_attn_in['bkc'], 'L0_attn_wv': _L0_attn_in['wv'], 'L0_attn_bv': _L0_attn_in['bv'], 'L0_attn_wo': _L0_attn_in['wo'], 'L0_attn_bo': _L0_attn_in['bo'], 'L0_ffn_gate_weight': _L0_ffn_in['gate_weight'], 'L0_ffn_w_gate': _L0_ffn_in['w_gate'], 'L0_ffn_w_up': _L0_ffn_in['w_up'], 'L0_ffn_w_down': _L0_ffn_in['w_down'], 'L0_ffn_ws_gate': _L0_ffn_in['ws_gate'], 'L0_ffn_ws_up': _L0_ffn_in['ws_up'], 'L0_ffn_ws_down': _L0_ffn_in['ws_down'], 'L0_c': _L0_c, 'L0_wmod': _L0_wmod}
    _x0 = _d['L0_attn_x']
    _d['L0_attn_x'] = jax.random.normal(jax.random.fold_in(jax.random.key(seed), 1), (4, 1024, 256), dtype=_x0.dtype)
    del _x0
    return _d

def reference(L0_attn_x, L0_attn_wq, L0_attn_bq, L0_attn_wqc, L0_attn_bqc, L0_attn_wqr, L0_attn_bqr, L0_attn_wkv, L0_attn_bkv, L0_attn_wkr, L0_attn_bkr, L0_attn_wkc, L0_attn_bkc, L0_attn_wv, L0_attn_bv, L0_attn_wo, L0_attn_bo, L0_ffn_gate_weight, L0_ffn_w_gate, L0_ffn_w_up, L0_ffn_w_down, L0_ffn_ws_gate, L0_ffn_ws_up, L0_ffn_ws_down, L0_c, L0_wmod):

    def _L0_attn_ref(x, wq, bq, wqc, bqc, wqr, bqr, wkv, bkv, wkr, bkr, wkc, bkc, wv, bv, wo, bo):
        import jax, jax.numpy as jnp
        import numpy as np
        import math
        B, S, E = (2, 512, 256)
        H, DC, DR = (16, 64, 128)
        HD = E // H

        def _linear_params(key, din, dout):
            k1, k2 = jax.random.split(key)
            bound = 1.0 / math.sqrt(din)
            w = jax.random.uniform(k1, (din, dout), minval=-bound, maxval=bound, dtype=jnp.float32)
            b = jax.random.uniform(k2, (dout,), minval=-bound, maxval=bound, dtype=jnp.float32)
            return (w, b)

        def _gelu(x):
            return jax.nn.gelu(x, approximate=False)

        def _rope_cos_sin(seq_len, d_rope):
            inv_freq = 1.0 / 10000.0 ** (jnp.arange(0, d_rope, 2, dtype=jnp.float32) / d_rope)
            t = jnp.arange(seq_len, dtype=jnp.float32)
            freqs = t[:, None] * inv_freq[None, :]
            emb = jnp.concatenate([freqs, freqs], axis=-1)
            return (jnp.cos(emb), jnp.sin(emb))

        def _apply_rope(x, cos, sin):
            d = x.shape[-1]
            x1, x2 = (x[..., :d // 2], x[..., d // 2:])
            rot = jnp.concatenate([-x2, x1], axis=-1)
            return x * cos + rot * sin
        b, s, _ = x.shape
        cq = _gelu(x @ wq + bq)
        q_c = cq @ wqc + bqc
        q_r = x @ wqr + bqr
        ckv = _gelu(x @ wkv + bkv)
        k_r = x @ wkr + bkr
        k_c = ckv @ wkc + bkc
        v = (ckv @ wv + bv).reshape(b, s, H, HD).transpose(0, 2, 1, 3)
        cos, sin = _rope_cos_sin(s, DR)
        q_r = _apply_rope(q_r, cos, sin)
        k_r = _apply_rope(k_r, cos, sin)
        q = _gelu(jnp.concatenate([q_c, q_r], axis=-1)).reshape(b, s, H, HD).transpose(0, 2, 1, 3)
        k = _gelu(jnp.concatenate([k_c, k_r], axis=-1)).reshape(b, s, H, HD).transpose(0, 2, 1, 3)
        scale = 1.0 / math.sqrt(HD)
        scores = jnp.einsum('bhqd,bhkd->bhqk', q, k) * scale
        causal = jnp.triu(jnp.ones((s, s), dtype=bool), k=1)
        scores = jnp.where(causal[None, None], -jnp.inf, scores)
        attn = jax.nn.softmax(scores, axis=-1)
        out = jnp.einsum('bhqk,bhkd->bhqd', attn, v)
        out = out.transpose(0, 2, 1, 3).reshape(b, s, E)
        return out @ wo + bo

    def _L0_ffn_ref(hidden_states, gate_weight, w_gate, w_up, w_down, ws_gate, ws_up, ws_down):
        import jax, jax.numpy as jnp
        import numpy as np
        H = 256
        I = 128
        E = 8
        TOP_K = 2
        N_SHARED = 2
        SHARED_I = I * N_SHARED
        SCALE = 2.5
        NORM_TOPK = True
        B, S = (2, 256)

        def _swiglu(x, wg, wu, wd):
            g = x @ wg.T
            u = x @ wu.T
            return jax.nn.silu(g) * u @ wd.T
        b, s, h = hidden_states.shape
        x = hidden_states.reshape(-1, h)
        shared_out = _swiglu(x, ws_gate, ws_up, ws_down)
        logits = x.astype(jnp.float32) @ gate_weight.astype(jnp.float32).T
        scores = jax.nn.sigmoid(logits)
        topk_w, topk_idx = jax.lax.top_k(scores, TOP_K)
        if TOP_K > 1 and NORM_TOPK:
            topk_w = topk_w / (topk_w.sum(-1, keepdims=True) + 1e-20)
        topk_w = topk_w * SCALE
        onehot = jax.nn.one_hot(topk_idx, E, dtype=topk_w.dtype)
        combine = jnp.einsum('tk,tke->te', topk_w, onehot)
        g = jnp.einsum('th,eih->tei', x, w_gate)
        u = jnp.einsum('th,eih->tei', x, w_up)
        hmid = jax.nn.silu(g) * u
        y = jnp.einsum('tei,ehi->teh', hmid, w_down)
        routed_out = jnp.einsum('te,teh->th', combine, y)
        out = (routed_out + shared_out).reshape(b, s, h)
        return out
    x = L0_attn_x
    mod = (_silu(L0_c) @ L0_wmod).reshape(L0_c.shape[0], 6, 1, -1)
    sa, ca, ga, sb, cb, gb = (mod[:, 0], mod[:, 1], mod[:, 2], mod[:, 3], mod[:, 4], mod[:, 5])
    ga = (2 * (ga >= 0) - 1) * jnp.maximum(jnp.abs(ga), 0.25)
    gb = (2 * (gb >= 0) - 1) * jnp.maximum(jnp.abs(gb), 0.25)
    h = _layernorm(x, axis=-1) * (1 + ca) + sa
    x = x + ga * _L0_attn_ref(h, L0_attn_wq, L0_attn_bq, L0_attn_wqc, L0_attn_bqc, L0_attn_wqr, L0_attn_bqr, L0_attn_wkv, L0_attn_bkv, L0_attn_wkr, L0_attn_bkr, L0_attn_wkc, L0_attn_bkc, L0_attn_wv, L0_attn_bv, L0_attn_wo, L0_attn_bo)
    h = _layernorm(x, axis=-1) * (1 + cb) + sb
    x = x + gb * _L0_ffn_ref(h, L0_ffn_gate_weight, L0_ffn_w_gate, L0_ffn_w_up, L0_ffn_w_down, L0_ffn_ws_gate, L0_ffn_ws_up, L0_ffn_ws_down)
    return x

_drawn_inputs = setup_inputs


def setup_inputs(seed=0):
    import zlib

    import numpy as np

    out = dict(_drawn_inputs(seed))
    spreads = {}
    factors = {'L0_attn_wq': 8.0,
     'L0_attn_bq': 8.0,
     'L0_attn_wqc': 8.0,
     'L0_attn_bqc': 8.0,
     'L0_attn_wqr': 8.0,
     'L0_attn_bqr': 8.0,
     'L0_attn_wkv': 8.0,
     'L0_attn_bkv': 8.0,
     'L0_attn_wkr': 8.0,
     'L0_attn_bkr': 8.0,
     'L0_attn_wkc': 8.0,
     'L0_attn_bkc': 8.0,
     'L0_attn_wv': 6.01,
     'L0_attn_bv': 5.205,
     'L0_attn_wo': 4.044,
     'L0_attn_bo': 6.166,
     'L0_ffn_gate_weight': 8.0,
     'L0_ffn_w_gate': 8.0,
     'L0_ffn_w_up': 8.0,
     'L0_ffn_w_down': 8.0,
     'L0_ffn_ws_gate': 8.0,
     'L0_ffn_ws_up': 8.0,
     'L0_ffn_ws_down': 8.0,
     'L0_c': 3.033,
     'L0_wmod': 3.11}
    for name, (base, spread) in spreads.items():
        noise = np.random.default_rng([zlib.crc32(name.encode()), seed]).standard_normal(out[name].shape)
        drawn = base * np.exp(spread * noise) if base else spread * noise
        out[name] = jnp.asarray(drawn.astype(out[name].dtype))
    for name, factor in factors.items():
        out[name] = (out[name] * factor).astype(out[name].dtype)
    return out
```

```python
from contextlib import ExitStack

import numpy as np
import concourse.bass as bass
from concourse import mybir

F32 = mybir.dt.float32
F32R = mybir.dt.float32r
BF16 = mybir.dt.bfloat16
ALU = mybir.AluOpType
ACT = mybir.ActivationFunctionType
AX = mybir.AxisListType

P = 128
B, S, E = 4, 1024, 256
H, HD = 16, 16
DR = 128
NT = S // P
BANK = 512
NC = S // BANK
CH = BANK
CT = CH // P
GH = 4
G = H // GH
SLOTS = 3
EPS = 1e-5
NEG = -3.0e38
NE, TOPK, HID = 8, 2, 128
NF = 2 + NE
ROUTE_SCALE = 2.5

ROWS = 96
ROWS_M = ROWS + 2

STEPS = [(c, j) for c in range(NC) for j in range((c + 1) * BANK // P)]
NS = len(STEPS)
UNITS = NS * GH
DIAG = [P * j >= BANK * c for c, j in STEPS]


def width(step):
    c, j = STEPS[step]
    return BANK * (c + 1) - max(BANK * c, P * j)


def first_query(step):
    c, j = STEPS[step]
    return max(BANK * c, P * j)


def share_max_tiles(steps):
    total = GH * sum(P * (i + 1) for i in range(NT))
    room = sum(width(s) for s in range(steps))
    out, tile, done, target = [], 0, 0, 0
    for s in range(NS):
        mine = []
        if s < steps:
            target += width(s) * total / room
            while tile < GH * NT and (done < target - 1 or s == steps - 1):
                mine.append(tile)
                done += P * (tile % NT + 1)
                tile += 1
        out.append(mine)
    assert tile == GH * NT
    return out


MAX_STEPS = 9
MAX_IN_STEP = share_max_tiles(MAX_STEPS)
TRANSPOSE_M_STEP = MAX_STEPS


class Counter:

    def __init__(self, ctx, nc, name, per_turn):
        self.sem = ctx.enter_context(nc.semaphore(name))
        self.per_turn = per_turn

    def at(self, turn, k):
        return turn * self.per_turn + (max(k, 0) + 1)

    def before(self, turn, k):
        return turn * self.per_turn + (k + 1)


def start_counters(nc, counters):
    with nc.Block() as block:
        @block.sync
        def _(sp):
            for c in counters:
                sp.sem_inc(c.sem, 1)


def stage_0(nc, d, gate_all, mod_all):
    with ExitStack() as ctx:
        sb = lambda n, s, t=F32: ctx.enter_context(nc.sbuf_tensor(n, s, t))
        sem = lambda n: ctx.enter_context(nc.semaphore(n))
        ps = ctx.enter_context(nc.psum_tensor("ps_mod", [P, 8, BANK], F32))
        wmod = sb("wmod", [P, 2, 6 * E])
        cT = sb("cT", [P, 2, B])
        sT = sb("sT", [P, 2, B])
        s_wide = sb("s_wide", [P, 2, B, P])
        mag = sb("mag", [P, 2, E])
        sign2 = sb("sign2", [P, 2, E])
        loaded, silu_ready, wide_ready = sem("mod_loaded"), sem("silu_ready"), sem("wide_ready")
        cols_ready, rows_ready, gate_chain = sem("cols_ready"), sem("rows_ready"), sem("gate_chain")
        block = ctx.enter_context(nc.Block())

        @block.sync
        def _(sp):
            sp.dma_start(wmod[:], d["wmod"].rearrange("(k p) n -> p k n", p=P)).then_inc(loaded, 16)
            sp.dma_start(cT[:], d["cT"].rearrange("(k p) b -> p k b", p=P)).then_inc(loaded, 16)

        @block.scalar
        def _(act):
            act.wait_ge(loaded, 32)
            nc.scalar.activation(sT[:], cT[:], ACT.Silu).then_inc(silu_ready, 1)

        @block.tensor
        def _(pe):
            pe.wait_ge(silu_ready, 1)
            for m, part in enumerate((0, 1, 3, 4)):
                for f in range(2):
                    for k in range(2):
                        o = part * E + f * P
                        last = nc.tensor.matmul(ps[:, 0, (m * 2 + f) * B:(m * 2 + f + 1) * B], wmod[:, k, o:o + P],
                                                sT[:, k, :], start=(k == 0), stop=(k == 1))
            last.then_inc(cols_ready, 1)
            pe.wait_ge(wide_ready, 1)
            for b in range(B):
                for g, part in enumerate((2, 5)):
                    for k in range(2):
                        last = nc.tensor.matmul(ps[:, 1 + b, g * E:(g + 1) * E], s_wide[:, k, b, :],
                                                wmod[:, k, part * E:(part + 1) * E], start=(k == 0), stop=(k == 1))
                last.then_inc(rows_ready, 1)

        @block.vector
        def _(dve):
            dve.wait_ge(silu_ready, 1)
            nc.vector.tensor_copy(s_wide[:], sT[:].unsqueeze(3).broadcast_to([P, 2, B, P])).then_inc(wide_ready, 1)
            dve.wait_ge(cols_ready, 1)
            for m in range(4):
                src = ps[:, 0, m * 2 * B:(m + 1) * 2 * B].rearrange("p (f b) -> p b f", b=B)
                nc.vector.tensor_scalar(mod_all[:, :, m, :], src, float(m % 2), None, ALU.add)
            for b in range(B):
                dve.wait_ge(rows_ready, b + 1)
                row = ps[:, 1 + b, :].rearrange("p (g n) -> p g n", g=2)
                nc.vector.tensor_scalar(mag[:], row, -1.0, 0.25, ALU.mult, ALU.max).then_inc(gate_chain, 1)
                nc.vector.tensor_scalar(sign2[:], row, 0.0, 2.0, ALU.is_ge, ALU.mult).then_inc(gate_chain, 1)
                dve.wait_ge(gate_chain, 4 * b + 2)
                nc.vector.tensor_tensor(mag[:], row, mag[:], ALU.max).then_inc(gate_chain, 1)
                dve.wait_ge(gate_chain, 4 * b + 3)
                nc.vector.scalar_tensor_tensor(gate_all[:, :, b, :], sign2[:], -1.0, mag[:], ALU.add,
                                               ALU.mult).then_inc(gate_chain, 1)
                dve.wait_ge(gate_chain, 4 * b + 4)


def stage_a(nc, d, ident, gate_all, mod_all):
    with ExitStack() as ctx:
        sb = lambda n, s, t=F32: ctx.enter_context(nc.sbuf_tensor(n, s, t))
        sem = lambda n: ctx.enter_context(nc.semaphore(n))
        counters = []

        def cnt(name, per_turn):
            counters.append(Counter(ctx, nc, name, per_turn))
            return counters[-1]

        ps = ctx.enter_context(nc.psum_tensor("ps_attn", [P, 8, BANK], F32))

        score_bank = lambda slot: 2 * slot
        ST_BANK, OUT_BANK = 4, 6

        w_lat = sb("w_lat", [P, 2, 2 * 64])
        w_qr, w_kr = sb("w_qr", [P, 2, DR]), sb("w_kr", [P, 2, DR])
        w_c = sb("w_c", [P, 2, P])
        w_v = sb("w_v", [P, E])
        w_o = sb("w_o", [P, 2, E])
        bias = sb("bias", [P, 5])
        bv_row, bo_row = sb("bv_row", [P, E]), sb("bo_row", [P, E])
        cos_t, sin_t = sb("cos_t", [P, S]), sb("sin_t", [P, S])
        causal = sb("causal", [P, P], BF16)
        causal_t = sb("causal_t", [P, P], BF16)
        ident_b = sb("ident_b", [P, P], BF16)
        neg_half = sb("neg_half", [P, NT])

        x = sb("x", [P, NT, E])
        out_nat = sb("out_nat", [P, NT, E])
        out_t = sb("out_t", [P, 2, S])
        probs = sb("probs", [P, 2, GH, BANK])
        v = sb("v", [P, NT, H, 2 * HD])
        op_q, op_k = sb("op_q", [P, SLOTS, GH, S], F32R), sb("op_k", [P, SLOTS, GH, S], F32R)
        parts = sb("parts", [P, 4, 2, BANK])
        out_raw = sb("out_raw", [P, BANK])
        inv_sum = sb("inv_sum", [P, CT * GH])
        stats, mean_var = sb("stats", [P, NT, 6]), sb("mean_var", [P, NT, 2])
        rstd = sb("rstd", [P, NT])
        neg_max, neg_max_parts = sb("neg_max", [P, GH * NT]), sb("neg_max_parts", [P, 2, GH * NT])
        max_rows = sb("max_rows", [2 * GH * NT, P])
        mod = sb("mod", [P, 4, 2])
        gate, gate_bias = sb("gate", [P, E]), sb("gate_bias", [P, E])
        proj = sb("proj", [P, E])

        h_t = out_nat[:].rearrange("p t e -> p (t e)").rearrange("p (f s) -> p f s", f=2)
        rope = out_t[:].rearrange("p r (a n) -> p r a n", a=2)
        x_hat = probs[:, 0, :, :].rearrange("p a n -> p (a n)").rearrange("p (t e) -> p t e", e=E)
        latent = probs[:, 1, 0:2, :].rearrange("p a n -> p (a n)")
        raw = probs[:, 1, 2:4, :]

        scratch = nc.dram_tensor("qk_parts", [2, 2, E, S], F32, kind="Internal").ap()

        w_loaded, w_set = sem("w_loaded"), sem("w_set")
        ticks = [sem(f"tick_a{i}") for i in range(4)]
        x_loaded, stats_chain = cnt("x_loaded", 16), cnt("stats_chain", 2)
        mod_ready = cnt("mod_ready", 2)
        var_ready, rstd_ready, xhat_ready = cnt("var_ready", 1), cnt("rstd_ready", 1), cnt("xhat_ready", NT)
        xt_done, ht_ready = cnt("xt_done", 4), cnt("ht_ready", 4)
        lat_done, lat_ready = cnt("lat_done", NC), cnt("lat_ready", NC)
        qk_done, raw_ready = cnt("qk_done", 8), cnt("raw_ready", 8)
        rope_terms, rope_ready = cnt("rope_terms", 8), cnt("rope_ready", 4)
        hi_ready, lo_ready = cnt("hi_ready", 8), cnt("lo_ready", 8)
        parts_stored = [cnt(f"parts_stored{i}", 32) for i in range(4)]
        ops_loaded = [[cnt(f"ops_loaded{s}_{h}", 64 * (2 if s == 0 else 1)) for h in range(GH)] for s in range(SLOTS)]
        v_done, v_ready = cnt("v_done", NT), cnt("v_ready", NT)
        score_done, max_done = cnt("score_done", G * GH * NT), cnt("max_done", G * GH * NT)
        m_chain, m_split = cnt("m_chain", G), cnt("m_split", G)
        mt_done, mt_ready, m_loaded = cnt("mt_done", G), cnt("mt_ready", G), cnt("m_loaded", 32 * G)
        st_done, prob_ready = cnt("st_done", G * UNITS), cnt("prob_ready", G * UNITS)
        pv_done = cnt("pv_done", G * NS)
        raw_out_ready, raw_out_turned = cnt("raw_out_ready", G * NC), cnt("raw_out_turned", G * NC)
        inv_ready, out_ready = cnt("inv_ready", G * NC), cnt("out_ready", G * NC)
        out_turned, out_t_ready = cnt("out_turned", 2 * NC), cnt("out_t_ready", 2 * NC)
        gate_bias_ready, xb_ready = cnt("gate_bias_ready", 1), cnt("xb_ready", 1)
        proj_done, proj_scaled, x1_ready = cnt("proj_done", NT), cnt("proj_scaled", NT), cnt("x1_ready", NT)
        x1_stored = cnt("x1_stored", 16)

        N_WLOAD = 8 + 2 + 4 + 2 + 2

        start_counters(nc, counters)
        block = ctx.enter_context(nc.Block())

        @block.sync
        def _(sp):
            sp.wait_ge(w_set, 1)

            def load(dst, src):
                sp.dma_start(dst, src).then_inc(w_loaded, 16)

            load(w_lat[:, :, 0:64], d["wq"].rearrange("(k p) n -> p k n", p=P))
            load(w_lat[:, :, 64:128], d["wkv"].rearrange("(k p) n -> p k n", p=P))
            load(w_qr[:], d["wqr"].rearrange("(k p) n -> p k n", p=P))
            load(w_kr[:], d["wkr"].rearrange("(k p) n -> p k n", p=P))
            load(w_c[0:64, 0, :], d["wqc"])
            load(w_c[64:128, 1, :], d["wkc"])
            load(w_v[64:128, :], d["wv"])
            load(w_o[:], d["wo"].rearrange("(k p) n -> p k n", p=P))
            load(bias[0:64, 0:1], d["bq"].unsqueeze(1))
            load(bias[64:128, 0:1], d["bkv"].unsqueeze(1))
            for i, n in enumerate(("bqc", "bkc", "bqr", "bkr")):
                load(bias[:, 1 + i:2 + i], d[n].unsqueeze(1))
            load(bv_row[:], d["bv"].unsqueeze(0).broadcast_to([P, E]))
            load(bo_row[:], d["bo"].unsqueeze(0).broadcast_to([P, E]))
            load(cos_t[:], d["cos"])
            load(sin_t[:], d["sin"])

            with sp.Fori(0, B) as b:
                sp.wait_ge(x1_stored.sem, x1_stored.at(b, 0))
                sp.sem_inc(ticks[2], 1)
                sp.dma_start(x[:], d["x"][bass.ds(b, 1)].rearrange("o (t p) e -> p (o t) e", p=P)).then_inc(
                    x_loaded.sem, 16)

                def store_parts(n):
                    kind, c = qk_item(n)
                    sp.wait_ge(hi_ready.sem, hi_ready.at(b, n + 1))
                    sp.sem_inc(ticks[2], 1)
                    sp.wait_ge(lo_ready.sem, lo_ready.at(b, n + 1))
                    sp.sem_inc(ticks[2], 1)
                    if n == 0:
                        for h in range(GH):
                            sp.wait_ge(ops_loaded[0][h].sem, ops_loaded[0][h].at(b, 0))
                    dst = scratch[kind % 2, :, P * (kind // 2):P * (kind // 2) + P, c * BANK:(c + 1) * BANK]
                    sp.dma_start(dst.rearrange("a p s -> p a s"), parts[:, n % 4]).then_inc(
                        parts_stored[n % 4].sem, 16)

                def load_operands(g):
                    slot = g % SLOTS
                    for h in range(GH):
                        f = (g * GH + h) * HD
                        for r in range(2):
                            q_src = scratch[0, r:r + 1, f:f + HD, :].broadcast_to([2, HD, S])
                            k_src = scratch[1, :, f:f + HD, :]
                            rows = slice(32 * r, 32 * r + 32)
                            sp.dma_start(op_q[rows, slot, h, :].bitcast(F32), q_src).then_inc(
                                ops_loaded[slot][h].sem, 16)
                            sp.dma_start(op_k[rows, slot, h, :].bitcast(F32), k_src).then_inc(
                                ops_loaded[slot][h].sem, 16)

                def load_max_rows(g):
                    sp.wait_ge(mt_ready.sem, mt_ready.at(b, g + 1))
                    slot = g % SLOTS
                    n = GH * NT
                    for r in range(2):
                        dst = op_q[ROWS + r:ROWS + r + 1, slot, :, :].bitcast(F32)
                        sp.dma_start(dst.rearrange("p h (t s) -> p (h t) s", s=P), max_rows[n * r:n * r + n, :]).then_inc(
                            m_loaded.sem, 16)

                for n in range(4):
                    store_parts(n)
                for i in range(4):
                    sp.wait_ge(parts_stored[i].sem, parts_stored[i].at(b, 16))
                    sp.sem_inc(ticks[2], 1)
                sp.wait_ge(st_done.sem, st_done.at(b, 0))
                load_operands(0)
                load_operands(1)
                for n in range(4, 8):
                    store_parts(n)
                for i in range(4):
                    sp.wait_ge(parts_stored[i].sem, parts_stored[i].at(b, 32))
                    sp.sem_inc(ticks[2], 1)
                load_operands(2)
                load_max_rows(0)
                load_max_rows(1)
                sp.wait_ge(st_done.sem, st_done.at(b, UNITS))
                sp.sem_inc(ticks[2], 1)
                sp.wait_ge(max_done.sem, max_done.at(b, GH * NT))
                load_operands(3)
                load_max_rows(2)
                load_max_rows(3)

                sp.wait_ge(x1_ready.sem, x1_ready.at(b, NT))
                sp.sem_inc(ticks[2], 1)
                sp.dma_start(d["x1"][bass.ds(b, 1)].rearrange("o (t p) e -> p (o t) e", p=P), x[:]).then_inc(
                    x1_stored.sem, 16)
            sp.wait_ge(x1_stored.sem, x1_stored.at(B, 0))

        @block.gpsimd
        def _(pool):
            pool.wait_ge(w_set, 1)
            with pool.Fori(0, B) as b:
                pool.wait_ge(var_ready.sem, var_ready.at(b, 1))
                nc.gpsimd.tensor_tensor(rstd[:], rstd[:], neg_half[:], ALU.pow).then_inc(rstd_ready.sem, 1)

                def lo_part(n):
                    pool.wait_ge(hi_ready.sem, hi_ready.at(b, n + 1))
                    nc.gpsimd.tensor_tensor(parts[:, n % 4, 1, :].bitcast(F32R), raw[:, n % 2, :], parts[:, n % 4, 0, :],
                                            ALU.subtract).then_inc(lo_ready.sem, 1)

                def rope_sum(r):
                    pool.wait_ge(rope_terms.sem, rope_terms.at(b, 2 * r + 2))
                    nc.gpsimd.tensor_tensor(rope[:, r % 2, 0, :], rope[:, r % 2, 0, :], rope[:, r % 2, 1, :],
                                            ALU.add).then_inc(rope_ready.sem, 1)

                for n in range(4):
                    lo_part(n)
                rope_sum(0)
                rope_sum(1)
                lo_part(4)
                rope_sum(2)
                lo_part(5)
                rope_sum(3)
                lo_part(6)
                lo_part(7)
                pool.wait_ge(mod_ready.sem, mod_ready.at(b, 2))
                nc.gpsimd.tensor_tensor(gate_bias[:], gate[:], bo_row[:], ALU.mult).then_inc(gate_bias_ready.sem, 1)
                pool.wait_ge(gate_bias_ready.sem, gate_bias_ready.at(b, 1))
                pool.wait_ge(xhat_ready.sem, xhat_ready.at(b, NT))
                nc.gpsimd.tensor_tensor(x[:], x[:], gate_bias[:].unsqueeze(1).broadcast_to([P, NT, E]),
                                        ALU.add).then_inc(xb_ready.sem, 1)

        @block.scalar
        def _(act):
            act.wait_ge(w_loaded, 16 * N_WLOAD)
            with act.Fori(0, B) as b:
                for c in range(NC):
                    act.wait_ge(lat_done.sem, lat_done.at(b, c + 1))
                    act.wait_ge(pv_done.sem, pv_done.at(b, 0))
                    nc.scalar.activation(latent[:, c * BANK:(c + 1) * BANK], ps[:, ST_BANK + c, :], ACT.Gelu,
                                         bias=bias[:, 0:1]).then_inc(lat_ready.sem, 1)
                for n in range(8):
                    if n >= 2:
                        act.wait_ge(lo_ready.sem, lo_ready.at(b, n - 1))
                        act.wait_ge(hi_ready.sem, hi_ready.at(b, n - 1))
                    kind, c = qk_item(n)
                    if n < 4:
                        act.wait_ge(qk_done.sem, qk_done.at(b, n + 1))
                        nc.scalar.activation(raw[:, n % 2, :], ps[:, n % 4, :], ACT.Gelu,
                                             bias=bias[:, 1 + kind:2 + kind]).then_inc(raw_ready.sem, 1)
                    else:
                        act.wait_ge(rope_ready.sem, rope_ready.at(b, n - 3))
                        nc.scalar.activation(raw[:, n % 2, :], rope[:, n % 2, 0, :], ACT.Gelu).then_inc(
                            raw_ready.sem, 1)
                act.wait_ge(lo_ready.sem, lo_ready.at(b, 8))
                act.wait_ge(hi_ready.sem, hi_ready.at(b, 8))
                act.wait_ge(v_done.sem, v_done.at(b, NT))

                def copy_out(g, c):
                    act.wait_ge(pv_done.sem, pv_done.at(b, g * NS + (CT if c == 0 else NS)))
                    act.wait_ge(raw_out_turned.sem, raw_out_turned.at(b, g * NC + c))
                    nc.scalar.activation(out_raw[:], ps[:, OUT_BANK + c, :], ACT.Copy).then_inc(raw_out_ready.sem, 1)

                for g in range(G):
                    for s in range(NS):
                        n = g * NS + s
                        for h in range(GH):
                            u = GH * n + h
                            act.wait_ge(st_done.sem, st_done.at(b, u + 1))
                            if h == 0 and n >= 2:
                                act.wait_ge(pv_done.sem, pv_done.at(b, n - 1))
                            w = width(s)
                            nc.scalar.activation(probs[:, n % 2, h, 0:w], ps[:, ST_BANK + u % 2, 0:w], ACT.Exp,
                                                 scale=float(HD) ** -0.5).then_inc(prob_ready.sem, 1)
                        if s == 1 and g > 0:
                            copy_out(g - 1, 1)
                        if s == 5:
                            copy_out(g, 0)
                copy_out(G - 1, 1)

        @block.vector
        def _(dve):
            for t in (w_c, w_v, op_q, op_k):
                nc.vector.memset(t[:].bitcast(F32) if t in (op_q, op_k) else t[:], 0.0)
            nc.vector.memset(v[:], 1.0)
            nc.vector.memset(neg_half[:], -0.5).then_inc(w_set, 1)
            dve.wait_ge(w_set, 1)
            nc.vector.memset(op_k[ROWS:ROWS_M].bitcast(F32), 1.0).then_inc(w_set, 1)
            nc.vector.tensor_copy(causal[:], d["causal_sb"][:, 0, :])
            nc.vector.tensor_copy(causal_t[:], d["causal_sb"][:, 1, :])
            nc.vector.tensor_copy(ident_b[:], ident[:]).then_inc(w_set, 1)
            dve.wait_ge(w_loaded, 16 * N_WLOAD)
            with dve.Fori(0, B) as b:
                nc.vector.tensor_copy(mod[:].unsqueeze(1), mod_all[:, bass.ds(b, 1), :, :]).then_inc(mod_ready.sem, 1)
                dve.wait_ge(xb_ready.sem, xb_ready.at(b, 0))
                nc.vector.tensor_copy(gate[:].unsqueeze(1), gate_all[:, 0, bass.ds(b, 1), :]).then_inc(
                    mod_ready.sem, 1)
                dve.wait_ge(x_loaded.sem, x_loaded.at(b, 16))
                for t in range(NT):
                    last = nc.vector.bn_stats(stats[:, t, :], x[:, t, :])
                last.then_inc(stats_chain.sem, 1)
                dve.wait_ge(stats_chain.sem, stats_chain.at(b, 1))
                dve.sem_inc(ticks[3], 1)
                for t in range(NT):
                    last = nc.vector.bn_aggr(mean_var[:, t, :], stats[:, t, :])
                last.then_inc(stats_chain.sem, 1)
                dve.wait_ge(stats_chain.sem, stats_chain.at(b, 2))
                nc.vector.tensor_scalar(rstd[:], mean_var[:, :, 1], EPS, None, ALU.add).then_inc(var_ready.sem, 1)
                dve.wait_ge(rstd_ready.sem, rstd_ready.at(b, 1))
                dve.wait_ge(pv_done.sem, pv_done.at(b, 0))
                for t in range(NT):
                    nc.vector.tensor_scalar(x_hat[:, t, :], x[:, t, :], mean_var[:, t, 0:1], rstd[:, t:t + 1],
                                            ALU.subtract, ALU.mult).then_inc(xhat_ready.sem, 1)
                dve.wait_ge(mod_ready.sem, mod_ready.at(b, 2))
                dve.wait_ge(out_turned.sem, out_turned.at(b, 0))
                dve.wait_ge(proj_done.sem, proj_done.at(b, 0))
                for c in range(NC):
                    for f in range(2):
                        dve.wait_ge(xt_done.sem, xt_done.at(b, 2 * c + f + 1))
                        nc.vector.tensor_scalar(h_t[:, f, c * BANK:(c + 1) * BANK], ps[:, 2 * c + f, :], mod[:, 1, f:f + 1],
                                                mod[:, 0, f:f + 1], ALU.mult, ALU.add).then_inc(ht_ready.sem, 1)

                def hi_part(n):
                    dve.wait_ge(raw_ready.sem, raw_ready.at(b, n + 1))
                    dve.wait_ge(parts_stored[n % 4].sem, parts_stored[n % 4].at(b, 16 * (n // 4)))
                    nc.vector.tensor_copy(parts[:, n % 4, 0, :].bitcast(F32R), raw[:, n % 2, :]).then_inc(
                        hi_ready.sem, 1)

                def rope_mult(r):
                    n = 4 + r
                    kind, c = qk_item(n)
                    dve.wait_ge(qk_done.sem, qk_done.at(b, n + 1))
                    if r >= 2:
                        dve.wait_ge(raw_ready.sem, raw_ready.at(b, n - 1))
                    cols = slice(c * BANK, (c + 1) * BANK)
                    y, bcol = ps[:, n % 4, :], bias[:, 1 + kind:2 + kind]
                    nc.vector.scalar_tensor_tensor(rope[:, r % 2, 0, :], y, bcol, cos_t[:, cols], ALU.add,
                                                   ALU.mult)
                    for lo, hi in ((0, 64), (64, 0)):
                        nc.vector.scalar_tensor_tensor(rope[hi:hi + 64, r % 2, 1, :], y[lo:lo + 64], bcol[lo:lo + 64],
                                                       sin_t[lo:lo + 64, cols], ALU.add,
                                                       ALU.mult).then_inc(rope_terms.sem, 1)

                for n in range(4):
                    hi_part(n)
                rope_mult(0)
                rope_mult(1)
                hi_part(4)
                rope_mult(2)
                hi_part(5)
                rope_mult(3)
                hi_part(6)
                hi_part(7)
                for t in range(NT):
                    dve.wait_ge(v_done.sem, v_done.at(b, t + 1))
                    src = ps[:, OUT_BANK + t % 2, 0:E].rearrange("p (h e) -> p h e", e=HD)
                    nc.vector.tensor_tensor(v[:, t, :, 0:HD], src, bv_row[:].rearrange("p (h e) -> p h e", e=HD),
                                            ALU.add).then_inc(v_ready.sem, 1)

                def row_max(g, tile):
                    t = g * GH * NT + tile
                    dve.wait_ge(score_done.sem, score_done.at(b, t + 1))
                    w = P * (tile % NT + 1)
                    bank = score_bank(tile % 2)
                    src = ps[:, bank:bank + 2, :].rearrange("p a n -> p (a n)")[:, 0:w]
                    nc.vector.tensor_reduce(neg_max[:, tile:tile + 1], src, AX.X, ALU.max,
                                            negate=True).then_inc(max_done.sem, 1)

                def split_max(g):
                    dve.wait_ge(max_done.sem, max_done.at(b, GH * NT * (g + 1)))
                    nc.vector.tensor_copy(neg_max_parts[:, 0, :].bitcast(F32R), neg_max[:]).then_inc(m_chain.sem, 1)
                    dve.wait_ge(m_chain.sem, m_chain.at(b, g + 1))
                    nc.vector.tensor_tensor(neg_max_parts[:, 1, :].bitcast(F32R), neg_max[:], neg_max_parts[:, 0, :],
                                            ALU.subtract).then_inc(m_split.sem, 1)

                def max_to_rows(g):
                    dve.wait_ge(mt_done.sem, mt_done.at(b, g + 1))
                    dve.wait_ge(m_loaded.sem, m_loaded.at(b, 32 * g))
                    nc.vector.tensor_copy(max_rows[:], ps[0:2 * GH * NT, 0, 0:P]).then_inc(mt_ready.sem, 1)

                def normalise(g, c):
                    n = g * NC + c
                    dve.wait_ge(raw_out_turned.sem, raw_out_turned.at(b, n + 1))
                    src = ps[:, OUT_BANK + c, :].rearrange("p (t h e) -> p t h e", h=GH, e=2 * HD)
                    inv = inv_sum[:].rearrange("p (t h) -> p t h", h=GH)
                    dve.wait_ge(out_ready.sem, out_ready.at(b, n))
                    nc.vector.reciprocal(inv, src[:, :, :, HD]).then_inc(inv_ready.sem, 1)
                    dve.wait_ge(inv_ready.sem, inv_ready.at(b, n + 1))
                    for t in range(CT):
                        dst = out_nat[:, c * CT + t, g * GH * HD:(g + 1) * GH * HD].rearrange("p (h e) -> p h e", e=HD)
                        last = nc.vector.tensor_tensor(dst, src[:, t, :, 0:HD],
                                                       inv[:, t, :].unsqueeze(2).broadcast_to([P, GH, HD]), ALU.mult)
                    last.then_inc(out_ready.sem, 1)

                for tile in range(GH * NT):
                    row_max(0, tile)
                split_max(0)
                max_to_rows(0)
                for g in range(G):
                    for s in range(NS):
                        if g + 1 < G:
                            for tile in MAX_IN_STEP[s]:
                                row_max(g + 1, tile)
                            if s == TRANSPOSE_M_STEP:
                                max_to_rows(g + 1)
                            if s + 1 == TRANSPOSE_M_STEP:
                                split_max(g + 1)
                        if s == 3 and g > 0:
                            normalise(g - 1, 1)
                        if s == 7:
                            normalise(g, 0)
                normalise(G - 1, 1)
                for c in range(NC):
                    for f in range(2):
                        dve.wait_ge(out_turned.sem, out_turned.at(b, 2 * c + f + 1))
                        nc.vector.tensor_copy(out_t[:, f, c * BANK:(c + 1) * BANK], ps[:, 2 * c + f, :]).then_inc(
                            out_t_ready.sem, 1)
                dve.wait_ge(xb_ready.sem, xb_ready.at(b, 1))
                for t in range(NT):
                    dve.wait_ge(proj_done.sem, proj_done.at(b, t + 1))
                    nc.vector.tensor_tensor(proj[:], ps[:, ST_BANK + t % 2, 0:E], gate[:], ALU.mult).then_inc(
                        proj_scaled.sem, 1)
                    dve.wait_ge(proj_scaled.sem, proj_scaled.at(b, t + 1))
                    nc.vector.tensor_tensor(x[:, t, :], x[:, t, :], proj[:], ALU.add).then_inc(x1_ready.sem, 1)
                    dve.wait_ge(x1_ready.sem, x1_ready.at(b, t + 1))

        @block.tensor
        def _(pe):
            pe.wait_ge(w_loaded, 16 * N_WLOAD)
            pe.wait_ge(w_set, 3)
            with pe.Fori(0, B) as b:
                pe.wait_ge(out_t_ready.sem, out_t_ready.at(b, 0))
                for t in range(NT):
                    pe.wait_ge(xhat_ready.sem, xhat_ready.at(b, t + 1))
                    for f in range(2):
                        c, o = t // 4, P * (t % 4)
                        last = nc.tensor.transpose(ps[:, 2 * c + f, o:o + P], x_hat[:, t, f * P:(f + 1) * P], ident[:])
                        if t % 4 == 3:
                            last.then_inc(xt_done.sem, 1)
                pe.wait_ge(x1_ready.sem, x1_ready.at(b, 0))
                for c in range(NC):
                    pe.wait_ge(ht_ready.sem, ht_ready.at(b, 2 * c + 2))
                    for f in range(2):
                        last = nc.tensor.matmul(ps[:, ST_BANK + c, :], w_lat[:, f, :], h_t[:, f, c * BANK:(c + 1) * BANK],
                                                start=(f == 0), stop=(f == 1))
                    last.then_inc(lat_done.sem, 1)
                for n in range(8):
                    kind, c = qk_item(n)
                    cols = slice(c * BANK, (c + 1) * BANK)
                    if n < 4:
                        pe.wait_ge(lat_ready.sem, lat_ready.at(b, c + 1))
                        pe.wait_ge(ht_ready.sem, ht_ready.at(b, 4))
                        last = nc.tensor.matmul(ps[:, n % 4, :], w_c[:, kind, :], latent[:, cols], start=True, stop=True)
                    else:
                        pe.wait_ge(raw_ready.sem, raw_ready.at(b, n - 3))
                        w = (w_qr, w_kr)[kind - 2]
                        for f in range(2):
                            last = nc.tensor.matmul(ps[:, n % 4, :], w[:, f, :], h_t[:, f, cols],
                                                    start=(f == 0), stop=(f == 1))
                    last.then_inc(qk_done.sem, 1)
                pe.wait_ge(out_ready.sem, out_ready.at(b, 0))
                for t in range(NT):
                    pe.wait_ge(v_ready.sem, v_ready.at(b, t - 1))
                    nc.tensor.matmul(ps[:, OUT_BANK + t % 2, 0:E], latent[:, t * P:(t + 1) * P], w_v[:],
                                     start=True, stop=True).then_inc(v_done.sem, 1)

                def scores(g, tile):
                    h, i, slot, t = tile // NT, tile % NT, g % SLOTS, g * GH * NT + tile
                    if i == 0:
                        pe.wait_ge(ops_loaded[slot][h].sem, ops_loaded[slot][h].at(b, 128 if g == 3 else 64))
                    if tile < 2:
                        if g == 0:
                            pe.wait_ge(rope_terms.sem, rope_terms.at(b, 8))
                        else:
                            pe.wait_ge(mt_ready.sem, mt_ready.at(b, g))
                    pe.wait_ge(max_done.sem, max_done.at(b, t - 1))
                    bank = score_bank(tile % 2)
                    q = op_q[0:ROWS, slot, h, i * P:(i + 1) * P]
                    for k0 in range(0, P * (i + 1), BANK):
                        k1 = min(k0 + BANK, P * (i + 1))
                        last_piece = k1 == P * (i + 1)
                        nc.tensor.matmul(ps[:, bank + k0 // BANK, 0:k1 - k0], q, op_k[0:ROWS, slot, h, k0:k1],
                                         start=True, stop=not last_piece)
                    o = P * i % BANK
                    nc.tensor.matmul(ps[:, bank + P * i // BANK, o:o + P], ident_b[:], causal[:], start=False,
                                     stop=True).then_inc(score_done.sem, 1)

                def transpose_max(g):
                    pe.wait_ge(m_split.sem, m_split.at(b, g + 1))
                    pe.sem_inc(ticks[1], 1)
                    nc.tensor.transpose(ps[0:2 * GH * NT, 0, 0:P],
                                        neg_max_parts[:].rearrange("p a n -> p (a n)"), ident[:]).then_inc(
                                            mt_done.sem, 1)

                def scores_t(g, s, h):
                    c, j = STEPS[s]
                    slot, u = g % SLOTS, (g * NS + s) * GH + h
                    if s == 0 and h == 0:
                        pe.wait_ge(m_loaded.sem, m_loaded.at(b, 32 * (g + 1)))
                        if g == 0:
                            pe.wait_ge(lat_ready.sem, lat_ready.at(b, 2))
                    pe.wait_ge(prob_ready.sem, prob_ready.at(b, u - 1))
                    q0, w = first_query(s), width(s)
                    last = nc.tensor.matmul(ps[:, ST_BANK + u % 2, 0:w], op_k[0:ROWS_M, slot, h, j * P:(j + 1) * P],
                                            op_q[0:ROWS_M, slot, h, q0:q0 + w], start=True, stop=not DIAG[s])
                    if DIAG[s]:
                        last = nc.tensor.matmul(ps[:, ST_BANK + u % 2, 0:P], ident_b[:], causal_t[:], start=False,
                                                stop=True)
                    last.then_inc(st_done.sem, 1)

                def weigh_values(g, s):
                    c, j = STEPS[s]
                    n = g * NS + s
                    pe.wait_ge(prob_ready.sem, prob_ready.at(b, GH * (n + 1)))
                    if j == 0:
                        pe.wait_ge(v_ready.sem, v_ready.at(b, NT))
                        pe.wait_ge(out_ready.sem, out_ready.at(b, (g - 1) * NC + c + 1))
                    o, w = first_query(s) - c * BANK, width(s)
                    for h in range(GH):
                        last = nc.tensor.matmul(ps[32 * h:32 * h + 32, OUT_BANK + c, o:o + w], v[:, j, g * GH + h, :],
                                                probs[:, n % 2, h, 0:w], start=(j == 0), stop=(o + P == BANK))
                    last.then_inc(pv_done.sem, 1)

                def turn_out(g, c):
                    pe.wait_ge(raw_out_ready.sem, raw_out_ready.at(b, g * NC + c + 1))
                    for t in range(CT):
                        last = nc.tensor.transpose(ps[:, OUT_BANK + c, t * P:(t + 1) * P], out_raw[:, t * P:(t + 1) * P],
                                                   ident[:])
                    last.then_inc(raw_out_turned.sem, 1)

                for tile in range(GH * NT):
                    scores(0, tile)
                transpose_max(0)
                for g in range(G):
                    for s in range(NS):
                        tiles = MAX_IN_STEP[s] if g + 1 < G else []
                        half = (len(tiles) + 1) // 2
                        scores_t(g, s, 0)
                        scores_t(g, s, 1)
                        for tile in tiles[:half]:
                            scores(g + 1, tile)
                        scores_t(g, s, 2)
                        scores_t(g, s, 3)
                        for tile in tiles[half:]:
                            scores(g + 1, tile)
                        if g + 1 < G and s == TRANSPOSE_M_STEP:
                            transpose_max(g + 1)
                        if s == 2 and g > 0:
                            turn_out(g - 1, 1)
                        if s == 6:
                            turn_out(g, 0)
                        if s > 0:
                            weigh_values(g, s - 1)
                        elif g > 0:
                            weigh_values(g - 1, NS - 1)
                weigh_values(G - 1, NS - 1)
                turn_out(G - 1, 1)
                pe.wait_ge(out_ready.sem, out_ready.at(b, G * NC))
                for c in range(NC):
                    for f in range(2):
                        for t in range(CT):
                            last = nc.tensor.transpose(ps[:, 2 * c + f, t * P:(t + 1) * P],
                                                       out_nat[:, c * CT + t, f * P:(f + 1) * P], ident[:])
                        last.then_inc(out_turned.sem, 1)
                pe.wait_ge(prob_ready.sem, prob_ready.at(b, G * UNITS))
                for t in range(NT):
                    pe.wait_ge(proj_scaled.sem, proj_scaled.at(b, t - 1))
                    if t % CT == 0:
                        pe.wait_ge(out_t_ready.sem, out_t_ready.at(b, 2 * (t // CT) + 2))
                    for f in range(2):
                        last = nc.tensor.matmul(ps[:, ST_BANK + t % 2, 0:E], out_t[:, f, t * P:(t + 1) * P], w_o[:, f, :],
                                                start=(f == 0), stop=(f == 1))
                    last.then_inc(proj_done.sem, 1)


def qk_item(n):
    return (n % 2 + (2 if n >= 4 else 0)), (n // 2) % 2


def stage_b(nc, d, ident, gate_all, mod_all, out):
    with ExitStack() as ctx:
        sb = lambda n, s, t=F32: ctx.enter_context(nc.sbuf_tensor(n, s, t))
        sem = lambda n: ctx.enter_context(nc.semaphore(n))
        counters = []

        def cnt(name, per_turn):
            counters.append(Counter(ctx, nc, name, per_turn))
            return counters[-1]

        ps = ctx.enter_context(nc.psum_tensor("ps_ffn", [P, 8, BANK], F32))
        OUT_BANK, FRONT_BANK = 4, 6

        w_in = sb("w_in", [P, 2, 2, NF * 2 * HID], F32R)
        w_out = sb("w_out", [P, 2, NF * E], F32R)
        staged = sb("staged", [P, 2, NF * HID])
        w_router = sb("w_router", [P, 2, NE])
        lower = sb("lower", [P, NE, NE])
        neg_half = sb("neg_half_b", [P, CT])
        x1 = sb("x1_b", [P, 2, CT, E])
        x_hat = sb("x_hat_b", [P, CT, E])
        h_t = sb("h_t", [P, 2, CH])
        h_parts = sb("h_parts", [P, 2, 2, 2, CH], F32R)
        stats, mean_var, rstd = sb("stats_b", [P, CT, 6]), sb("mean_var_b", [P, CT, 2]), sb("rstd_b", [P, CT])
        logits_t = sb("logits_t", [NE, CH])
        ex = sb("ex", [P, CT, NE])
        prob = sb("prob", [P, CT, NE])
        beats, ties = sb("beats", [P, CT, NE, NE]), sb("ties", [P, CT, NE, NE])
        rank = sb("rank", [P, CT, NE])
        combine = sb("combine", [P, CT, NE])
        total, inv = sb("total", [P, CT]), sb("inv", [P, CT])
        combine_t = sb("combine_t", [NE, CH])
        share = sb("share", [P, 2, NE, CH])
        act_g = sb("act_g", [P, 3, CH])
        hidden = sb("hidden", [P, 2, CH])
        hid_parts = sb("hid_parts", [P, 3, 2, CH], F32R)
        scaled = sb("scaled", [P, 2, BANK])
        y = sb("y", [P, 2, CT, E])
        mod = sb("mod_b", [P, 2, 4, 2])
        gate = sb("gate_b", [P, 2, E])
        combine_d = nc.dram_tensor("combine_d", [2, NE, CH], F32, kind="Internal").ap()

        NW = 5
        raw_loaded = [sem(f"raw_loaded{i}") for i in range(2)]
        small_loaded = sem("small_loaded")
        w_hi, w_lo = sem("w_hi"), sem("w_lo")
        ticks = [sem(f"tick_b{i}") for i in range(3)]
        x1_loaded = [cnt(f"x1_loaded{i}", 16) for i in range(2)]
        chain = cnt("chain_b", 2 * CHAIN)
        mod_ready = cnt("mod_ready_b", 2)
        var_ready, rstd_ready, xhat_ready = cnt("var_ready_b", 2), cnt("rstd_ready_b", 2), cnt("xhat_ready_b", 2 * CT)
        xt_done, ht_ready = cnt("xt_done_b", 4), cnt("ht_ready_b", 4)
        h_hi, h_lo = cnt("h_hi", 2), cnt("h_lo", 2)
        logit_done, logit_ready = cnt("logit_done", 2), cnt("logit_ready", 2)
        logit_t_done, exp_ready = cnt("logit_t_done", 2), cnt("exp_ready", 2)
        combine_ready, ct_done, ct_ready = cnt("combine_ready", 2), cnt("ct_done", 2), cnt("ct_ready", 2)
        combine_stored = cnt("combine_stored", 32)
        share_loaded = [cnt(f"share_loaded{i}", 16) for i in range(2)]
        gu_done, silu_ready, weighed = cnt("gu_done", 2 * NF), cnt("silu_ready_b", 2 * NF), cnt("weighed", 2 * NE)
        hid_ready, hid_hi, hid_lo = cnt("hid_ready", 2 * NF), cnt("hid_hi", 2 * NF), cnt("hid_lo", 2 * NF)
        down_done, scaled_ready = cnt("down_done", 2 * NF), cnt("scaled_ready", 4)
        y_ready = cnt("y_ready", 4)
        y_stored = [cnt(f"y_stored{i}", 16) for i in range(2)]

        def first(turn):
            return isinstance(turn, int) and turn == 0

        start_counters(nc, counters)
        block = ctx.enter_context(nc.Block())

        raw_src = [d["w_in_t"][k][:, i * 1280:(i + 1) * 1280] for k in range(2) for i in range(2)]
        raw_src += [d["w_out_t"][:, i * 1280:(i + 1) * 1280] for i in range(2)]
        parts_dst = [(w_in[:, k, 0, i * 1280:(i + 1) * 1280], w_in[:, k, 1, i * 1280:(i + 1) * 1280])
                     for k in range(2) for i in range(2)]
        parts_dst += [(w_out[:, 0, i * 1280:(i + 1) * 1280], w_out[:, 1, i * 1280:(i + 1) * 1280]) for i in range(2)]

        @block.sync
        def _(sp):
            sp.dma_start(w_router[:], d["gate_w_t"].rearrange("(k p) e -> p k e", p=P)).then_inc(small_loaded, 16)
            sp.dma_start(lower[:], d["lower"].unsqueeze(0).broadcast_to([P, NE, NE])).then_inc(small_loaded, 16)

            def front(turn, i):
                if not first(turn):
                    sp.wait_ge(y_ready.sem, y_ready.before(turn, 2 * (i + 1) - 4))
                sp.sem_inc(ticks[0], 1)
                sp.dma_start(x1[:, i], d["x1"][bass.ds(turn, 1), i * CH:(i + 1) * CH, :].rearrange(
                    "o (t p) e -> p (o t) e", p=P)).then_inc(x1_loaded[i].sem, 16)

            def combine_weights(turn, i):
                sp.wait_ge(ct_ready.sem, ct_ready.at(turn, i + 1))
                sp.dma_start(combine_d[i], combine_t[:]).then_inc(combine_stored.sem, 16)
                sp.wait_ge(combine_stored.sem, combine_stored.at(turn, 16 * (i + 1)))
                sp.sem_inc(ticks[0], 1)
                if not first(turn):
                    sp.wait_ge(weighed.sem, weighed.before(turn, NE * (i + 1) - 2 * NE))
                sp.dma_start(share[:, i], combine_d[i:i + 1].broadcast_to([P, NE, CH])).then_inc(
                    share_loaded[i].sem, 16)

            def store(turn, i):
                sp.wait_ge(y_ready.sem, y_ready.at(turn, 2 * i + 2))
                sp.sem_inc(ticks[0], 1)
                sp.dma_start(out[bass.ds(turn, 1), i * CH:(i + 1) * CH, :].rearrange("o (t p) e -> p (o t) e", p=P),
                             y[:, i]).then_inc(y_stored[i].sem, 16)

            front(0, 0)
            for n in range(6):
                if n >= 2:
                    sp.wait_ge(w_lo, n - 1)
                sp.dma_start(staged[:, n % 2, :], raw_src[n]).then_inc(raw_loaded[n % 2], 16)
            combine_weights(0, 0)

            def turn_body(turn, last):
                front(turn, 1)
                combine_weights(turn, 1)
                store(turn, 0)
                if not last:
                    front(turn + 1, 0)
                    combine_weights(turn + 1, 0)
                store(turn, 1)

            with sp.Fori(0, B - 1) as t:
                turn_body(t, False)
            turn_body(B - 1, True)
            for i in range(2):
                sp.wait_ge(y_stored[i].sem, y_stored[i].at(B, 0))

        @block.gpsimd
        def _(pool):
            def front_1(turn, i):
                pool.wait_ge(var_ready.sem, var_ready.at(turn, i + 1))
                nc.gpsimd.tensor_tensor(rstd[:], rstd[:], neg_half[:], ALU.pow).then_inc(rstd_ready.sem, 1)

            def front_2(turn, i):
                pool.wait_ge(h_hi.sem, h_hi.at(turn, i + 1))
                nc.gpsimd.tensor_tensor(h_parts[:, i, 1], h_t[:], h_parts[:, i, 0].bitcast(F32),
                                        ALU.subtract).then_inc(h_lo.sem, 1)

            def weigh(turn, i, e):
                n, x_ = i * NF + e, e - 2
                pool.wait_ge(silu_ready.sem, silu_ready.at(turn, n + 1))
                if x_ == 0:
                    pool.wait_ge(share_loaded[i].sem, share_loaded[i].at(turn, 16))
                nc.gpsimd.tensor_tensor(act_g[:, n % 3, :], act_g[:, n % 3, :], share[:, i, x_, :],
                                        ALU.mult).then_inc(weighed.sem, 1)

            def lo_part(turn, i, e):
                n = i * NF + e
                pool.wait_ge(hid_hi.sem, hid_hi.at(turn, n + 1))
                pool.wait_ge(down_done.sem, down_done.at(turn, n - 2))
                nc.gpsimd.tensor_tensor(hid_parts[:, n % 3, 1, :], hidden[:, n % 2, :],
                                        hid_parts[:, n % 3, 0, :].bitcast(F32), ALU.subtract).then_inc(hid_lo.sem, 1)

            for n in range(6):
                pool.wait_ge(w_hi, n + 1)
                hi, lo = parts_dst[n]
                nc.gpsimd.tensor_tensor(lo, staged[:, n % 2, :], hi.bitcast(F32), ALU.subtract).then_inc(w_lo, 1)
                if n == 1:
                    front_1(0, 0)
                if n == 3:
                    front_2(0, 0)

            def turn_body(turn, last):
                for i in range(2):
                    nxt = (turn, 1) if i == 0 else (turn + 1, 0)
                    for e in range(NF):
                        if e >= 2:
                            weigh(turn, i, e)
                        if e >= 1:
                            lo_part(turn, i, e - 1)
                        if not (i and last):
                            if e == FRONT_AT[0]:
                                front_1(*nxt)
                            if e == FRONT_AT[1]:
                                front_2(*nxt)
                    lo_part(turn, i, NF - 1)

            with pool.Fori(0, B - 1) as t:
                turn_body(t, False)
            turn_body(B - 1, True)

        @block.scalar
        def _(act):
            def router_exp(turn, i):
                act.wait_ge(logit_t_done.sem, logit_t_done.at(turn, i + 1))
                act.wait_ge(combine_ready.sem, combine_ready.at(turn, i))
                nc.scalar.activation(ex[:], ps[:, FRONT_BANK + 1, 0:CT * NE].rearrange("p (t e) -> p t e", e=NE),
                                     ACT.Exp, scale=-1.0).then_inc(exp_ready.sem, 1)

            router_exp(0, 0)

            def turn_body(turn, last):
                for i in range(2):
                    nxt = (turn, 1) if i == 0 else (turn + 1, 0)
                    for e in range(NF):
                        n = i * NF + e
                        act.wait_ge(gu_done.sem, gu_done.at(turn, n + 1))
                        act.wait_ge(hid_ready.sem, hid_ready.at(turn, n - 2))
                        nc.scalar.activation(act_g[:, n % 3, :], ps[:, 2 * (n % 2), :],
                                             ACT.Silu).then_inc(silu_ready.sem, 1)
                        if e == FRONT_AT[2] and not (i and last):
                            router_exp(*nxt)

            with act.Fori(0, B - 1) as t:
                turn_body(t, False)
            turn_body(B - 1, True)

        @block.vector
        def _(dve):
            nc.vector.memset(neg_half[:], -0.5)

            def front_1(turn, i):
                if i == 0:
                    dve.wait_ge(ht_ready.sem, ht_ready.at(turn, 0))
                src = mod_all[:, turn:turn + 1] if isinstance(turn, int) else mod_all[:, bass.ds(turn, 1)]
                gsrc = gate_all[:, 1, turn:turn + 1] if isinstance(turn, int) else gate_all[:, 1, bass.ds(turn, 1)]
                nc.vector.tensor_copy(mod[:, i:i + 1], src)
                nc.vector.tensor_copy(gate[:, i:i + 1], gsrc).then_inc(mod_ready.sem, 1)
                dve.wait_ge(x1_loaded[i].sem, x1_loaded[i].at(turn, 16))
                for t in range(CT):
                    last = nc.vector.bn_stats(stats[:, t, :], x1[:, i, t, :])
                last.then_inc(chain.sem, 1)
                dve.wait_ge(chain.sem, chain.at(turn, CHAIN * i + 1))
                dve.sem_inc(ticks[2], 1)
                for t in range(CT):
                    last = nc.vector.bn_aggr(mean_var[:, t, :], stats[:, t, :])
                last.then_inc(chain.sem, 1)
                dve.wait_ge(chain.sem, chain.at(turn, CHAIN * i + 2))
                nc.vector.tensor_scalar(rstd[:], mean_var[:, :, 1], EPS, None, ALU.add).then_inc(var_ready.sem, 1)

            def front_2(turn, i):
                dve.wait_ge(rstd_ready.sem, rstd_ready.at(turn, i + 1))
                dve.wait_ge(xt_done.sem, xt_done.at(turn, 2 * i))
                for t in range(CT):
                    nc.vector.tensor_scalar(x_hat[:, t, :], x1[:, i, t, :], mean_var[:, t, 0:1], rstd[:, t:t + 1],
                                            ALU.subtract, ALU.mult).then_inc(xhat_ready.sem, 1)

            def front_3(turn, i):
                dve.wait_ge(mod_ready.sem, mod_ready.at(turn, i + 1))
                dve.wait_ge(h_lo.sem, h_lo.at(turn, i))
                dve.wait_ge(logit_done.sem, logit_done.at(turn, i))
                dve.wait_ge(xt_done.sem, xt_done.at(turn, 2 * i + 2))
                for f in range(2):
                    nc.vector.tensor_scalar(h_t[:, f, :], ps[:, FRONT_BANK + f, :], mod[:, i, 3, f:f + 1],
                                            mod[:, i, 2, f:f + 1], ALU.mult, ALU.add).then_inc(ht_ready.sem, 1)
                dve.wait_ge(ht_ready.sem, ht_ready.at(turn, 2 * i + 2))
                if not first(turn):
                    dve.wait_ge(gu_done.sem, gu_done.before(turn, NF * (i + 1) - 2 * NF))
                nc.vector.tensor_copy(h_parts[:, i, 0], h_t[:]).then_inc(h_hi.sem, 1)

            def front_4(turn, i):
                dve.wait_ge(logit_done.sem, logit_done.at(turn, i + 1))
                nc.vector.tensor_copy(logits_t[:], ps[0:NE, FRONT_BANK, :]).then_inc(logit_ready.sem, 1)

            def front_5(turn, i):
                dve.wait_ge(exp_ready.sem, exp_ready.at(turn, i + 1))
                nc.vector.tensor_scalar(prob[:], ex[:], 1.0, None, ALU.add).then_inc(chain.sem, 1)
                dve.wait_ge(chain.sem, chain.at(turn, CHAIN * i + 3))
                nc.vector.reciprocal(prob[:], prob[:]).then_inc(chain.sem, 1)
                dve.wait_ge(chain.sem, chain.at(turn, CHAIN * i + 4))
                mine = prob[:].unsqueeze(3).broadcast_to([P, CT, NE, NE])
                other = prob[:].unsqueeze(2).broadcast_to([P, CT, NE, NE])
                nc.vector.tensor_tensor(beats[:], other, mine, ALU.is_gt)
                nc.vector.tensor_tensor(ties[:], other, mine, ALU.is_equal).then_inc(chain.sem, 1)
                dve.wait_ge(chain.sem, chain.at(turn, CHAIN * i + 5))
                nc.vector.tensor_tensor(ties[:], ties[:], lower[:].unsqueeze(1).broadcast_to([P, CT, NE, NE]),
                                        ALU.mult).then_inc(chain.sem, 1)
                dve.wait_ge(chain.sem, chain.at(turn, CHAIN * i + 6))
                nc.vector.tensor_tensor(beats[:], beats[:], ties[:], ALU.add).then_inc(chain.sem, 1)
                dve.wait_ge(chain.sem, chain.at(turn, CHAIN * i + 7))
                nc.vector.tensor_reduce(rank[:], beats[:], AX.X, ALU.add).then_inc(chain.sem, 1)
                dve.wait_ge(chain.sem, chain.at(turn, CHAIN * i + 8))
                nc.vector.scalar_tensor_tensor(combine[:], rank[:], TOPK - 0.5, prob[:], ALU.is_lt, ALU.mult).then_inc(
                    chain.sem, 1)
                dve.wait_ge(chain.sem, chain.at(turn, CHAIN * i + 9))
                nc.vector.tensor_reduce(total[:], combine[:], AX.X, ALU.add).then_inc(chain.sem, 1)
                dve.wait_ge(chain.sem, chain.at(turn, CHAIN * i + 10))
                nc.vector.tensor_scalar(total[:], total[:], 1e-20, None, ALU.add).then_inc(chain.sem, 1)
                dve.wait_ge(chain.sem, chain.at(turn, CHAIN * i + 11))
                nc.vector.reciprocal(inv[:], total[:]).then_inc(chain.sem, 1)
                dve.wait_ge(chain.sem, chain.at(turn, CHAIN * i + 12))
                nc.vector.tensor_scalar(inv[:], inv[:], ROUTE_SCALE, None, ALU.mult).then_inc(chain.sem, 1)
                dve.wait_ge(chain.sem, chain.at(turn, CHAIN * i + 13))
                nc.vector.tensor_tensor(combine[:], combine[:], inv[:].unsqueeze(2).broadcast_to([P, CT, NE]),
                                        ALU.mult).then_inc(combine_ready.sem, 1)

            def front_6(turn, i):
                dve.wait_ge(ct_done.sem, ct_done.at(turn, i + 1))
                dve.wait_ge(combine_stored.sem, combine_stored.at(turn, 16 * i))
                nc.vector.tensor_copy(combine_t[:], ps[0:NE, FRONT_BANK, :]).then_inc(ct_ready.sem, 1)

            def hidden_tile(turn, i, e):
                n = i * NF + e
                dve.wait_ge(silu_ready.sem, silu_ready.at(turn, n + 1))
                dve.wait_ge(gu_done.sem, gu_done.at(turn, n + 1))
                if e >= 2:
                    dve.wait_ge(weighed.sem, weighed.at(turn, i * NE + e - 1))
                dve.wait_ge(hid_lo.sem, hid_lo.at(turn, n - 1))
                nc.vector.tensor_tensor(hidden[:, n % 2, :], ps[:, 2 * (n % 2) + 1, :], act_g[:, n % 3, :],
                                        ALU.mult).then_inc(hid_ready.sem, 1)
                dve.wait_ge(hid_ready.sem, hid_ready.at(turn, n + 1))
                dve.wait_ge(down_done.sem, down_done.at(turn, n - 2))
                nc.vector.tensor_copy(hid_parts[:, n % 3, 0, :], hidden[:, n % 2, :]).then_inc(hid_hi.sem, 1)

            def residual(turn, i):
                dve.wait_ge(down_done.sem, down_done.at(turn, NF * (i + 1)))
                dve.wait_ge(y_stored[i].sem, y_stored[i].at(turn, 0))
                for q in range(2):
                    k = 2 * i + q
                    dve.wait_ge(y_ready.sem, y_ready.at(turn, k))
                    nc.vector.tensor_tensor(scaled[:, q, :].rearrange("p (t e) -> p t e", e=E),
                                            ps[:, OUT_BANK + q, :].rearrange("p (t e) -> p t e", e=E),
                                            gate[:, i].unsqueeze(1).broadcast_to([P, 2, E]),
                                            ALU.mult).then_inc(scaled_ready.sem, 1)
                    dve.wait_ge(scaled_ready.sem, scaled_ready.at(turn, k + 1))
                    nc.vector.tensor_tensor(y[:, i, 2 * q:2 * q + 2, :], x1[:, i, 2 * q:2 * q + 2, :],
                                            scaled[:, q, :].rearrange("p (t e) -> p t e", e=E),
                                            ALU.add).then_inc(y_ready.sem, 1)

            dve.wait_ge(small_loaded, 32)
            front_1(0, 0)
            for n in range(6):
                dve.wait_ge(raw_loaded[n % 2], 16 * (n // 2 + 1))
                nc.vector.tensor_copy(parts_dst[n][0], staged[:, n % 2, :]).then_inc(w_hi, 1)
                if n == 2:
                    front_2(0, 0)
                    front_3(0, 0)
            front_4(0, 0)
            front_5(0, 0)
            front_6(0, 0)

            def turn_body(turn, last):
                for i in range(2):
                    nxt = (turn, 1) if i == 0 else (turn + 1, 0)
                    for e in range(NF):
                        if not (i and last):
                            if e == FRONT_AT[0]:
                                front_1(*nxt)
                            if e == FRONT_AT[0] + 1:
                                front_2(*nxt)
                            if e == FRONT_AT[1]:
                                front_3(*nxt)
                            if e == FRONT_AT[1] + 1:
                                front_4(*nxt)
                            if e == FRONT_AT[2] + 1:
                                front_5(*nxt)
                            if e == FRONT_AT[3]:
                                front_6(*nxt)
                        hidden_tile(turn, i, e)
                    residual(turn, i)

            with dve.Fori(0, B - 1) as t:
                turn_body(t, False)
            turn_body(B - 1, True)

        @block.tensor
        def _(pe):
            pe.wait_ge(small_loaded, 32)

            def front_transpose(turn, i):
                pe.wait_ge(ct_ready.sem, ct_ready.at(turn, i))
                for f in range(2):
                    for t in range(CT):
                        pe.wait_ge(xhat_ready.sem, xhat_ready.at(turn, CT * i + t + 1))
                        last = nc.tensor.transpose(ps[:, FRONT_BANK + f, t * P:(t + 1) * P],
                                                   x_hat[:, t, f * P:(f + 1) * P], ident[:])
                    last.then_inc(xt_done.sem, 1)

            def front_router(turn, i):
                pe.wait_ge(ht_ready.sem, ht_ready.at(turn, 2 * i + 2))
                for f in range(2):
                    last = nc.tensor.matmul(ps[0:NE, FRONT_BANK, :], w_router[:, f, :], h_t[:, f, :],
                                            start=(f == 0), stop=(f == 1))
                last.then_inc(logit_done.sem, 1)

            def front_logits(turn, i):
                pe.wait_ge(logit_ready.sem, logit_ready.at(turn, i + 1))
                pe.sem_inc(ticks[1], 1)
                for t in range(CT):
                    last = nc.tensor.transpose(ps[:, FRONT_BANK + 1, t * NE:(t + 1) * NE], logits_t[:, t * P:(t + 1) * P],
                                               ident[0:NE, 0:NE])
                last.then_inc(logit_t_done.sem, 1)

            def front_combine(turn, i):
                pe.wait_ge(combine_ready.sem, combine_ready.at(turn, i + 1))
                for t in range(CT):
                    last = nc.tensor.transpose(ps[0:NE, FRONT_BANK, t * P:(t + 1) * P], combine[:, t, :], ident[:])
                last.then_inc(ct_done.sem, 1)

            def products(dst, stationary, moving, start, stop):
                for k, (a, c) in enumerate(((0, 0), (0, 1), (1, 0))):
                    last = nc.tensor.matmul(dst, stationary(a), moving(c), start=start and k == 0, stop=stop and k == 2,
                                            skip_group_check=True)
                return last

            def gate_up(turn, i, e):
                n = i * NF + e
                if e == 0:
                    pe.wait_ge(h_hi.sem, h_hi.at(turn, i + 1))
                    pe.wait_ge(h_lo.sem, h_lo.at(turn, i + 1))
                pe.wait_ge(hid_ready.sem, hid_ready.at(turn, n - 1))
                for u in range(2):
                    for f in range(2):
                        o = (2 * e + u) * HID
                        last = products(ps[:, 2 * (n % 2) + u, :], lambda a: w_in[:, f, a, o:o + HID],
                                        lambda c: h_parts[:, i, c, f, :], f == 0, f == 1)
                last.then_inc(gu_done.sem, 1)

            def down(turn, i, e):
                n = i * NF + e
                if e == 0:
                    pe.wait_ge(scaled_ready.sem, scaled_ready.at(turn, 2 * i))
                pe.wait_ge(hid_hi.sem, hid_hi.at(turn, n + 1))
                pe.wait_ge(hid_lo.sem, hid_lo.at(turn, n + 1))
                for t in range(CT):
                    last = products(ps[:, OUT_BANK + t // 2, (t % 2) * E:(t % 2 + 1) * E],
                                    lambda a: hid_parts[:, n % 3, a, t * P:(t + 1) * P],
                                    lambda c: w_out[:, c, e * E:(e + 1) * E], e == 0 and t % 2 == 0,
                                    e == NF - 1)
                last.then_inc(down_done.sem, 1)

            front_transpose(0, 0)
            front_router(0, 0)
            front_logits(0, 0)
            front_combine(0, 0)
            pe.wait_ge(w_hi, 6)
            pe.wait_ge(w_lo, 6)

            def turn_body(turn, last):
                for i in range(2):
                    nxt = (turn, 1) if i == 0 else (turn + 1, 0)
                    for e in range(NF):
                        gate_up(turn, i, e)
                        if not (i and last):
                            if e == FRONT_AT[0] + 1:
                                front_transpose(*nxt)
                            if e == FRONT_AT[1]:
                                front_router(*nxt)
                            if e == FRONT_AT[2]:
                                front_logits(*nxt)
                            if e == FRONT_AT[3]:
                                front_combine(*nxt)
                        if e >= LAG:
                            down(turn, i, e - LAG)
                    for e in range(NF - LAG, NF):
                        down(turn, i, e)

            with pe.Fori(0, B - 1) as t:
                turn_body(t, False)
            turn_body(B - 1, True)


LAG = 2
CHAIN = 13
FRONT_AT = (0, 3, 5, 8)


def build(nc, ins, out):
    with ExitStack() as ctx:
        sb = lambda n, s, t=F32: ctx.enter_context(nc.sbuf_tensor(n, s, t))
        ident, causal_sb = sb("ident", [P, P]), sb("causal_sb", [P, 2, P])
        gate_all, mod_all = sb("gate_all", [P, 2, B, E]), sb("mod_all", [P, B, 4, 2])
        const_loaded = ctx.enter_context(nc.semaphore("const_loaded"))
        d = dict(ins)
        d["x1"] = nc.dram_tensor("x1", [B, S, E], F32, kind="Internal").ap()
        d["causal_sb"] = causal_sb
        with nc.Block() as block:
            @block.sync
            def _(sp):
                sp.dma_start(ident[:], d["ident"]).then_inc(const_loaded, 16)
                sp.dma_start(causal_sb[:], d["causal"].rearrange("a p n -> p a n")).then_inc(const_loaded, 16)
                sp.wait_ge(const_loaded, 32)
        stage_0(nc, d, gate_all, mod_all)
        stage_a(nc, d, ident, gate_all, mod_all)
        stage_b(nc, d, ident, gate_all, mod_all, out)


def kernel(**inputs):
    import concourse.bacc as bacc
    from concourse.bass_utils import run_bass_kernel_spmd

    a = {k.removeprefix("L0_").removeprefix("attn_").removeprefix("ffn_"): np.asarray(t) for k, t in inputs.items()}
    put = {n: a[n] for n in ("x", "wq", "bq", "wqc", "bqc", "wqr", "bqr", "wkv", "bkv", "wkr", "bkr", "wkc", "bkc",
                             "wv", "bv", "wo", "bo", "wmod")}
    put["cT"] = a["c"].T
    put["gate_w_t"] = a["gate_weight"].T
    w_g = np.concatenate([a["ws_gate"].reshape(2, HID, E), a["w_gate"]])
    w_u = np.concatenate([a["ws_up"].reshape(2, HID, E), a["w_up"]])
    w_in = np.stack([w_g, w_u], axis=1).transpose(3, 0, 1, 2).reshape(2, P, NF * 2 * HID)
    put["w_in_t"] = w_in
    w_d = np.concatenate([a["ws_down"].reshape(E, 2, HID).transpose(1, 2, 0), a["w_down"].transpose(0, 2, 1)])
    put["w_out_t"] = w_d.transpose(1, 0, 2).reshape(HID, NF * E)
    inv_freq = (np.float32(1) / np.float32(10000) ** (np.arange(0, DR, 2, dtype=np.float32) / np.float32(DR)))
    angle = (np.arange(S, dtype=np.float32)[:, None] * inv_freq[None, :]).T
    angle = np.concatenate([angle, angle]).astype(np.float32)
    put["cos"] = np.cos(angle)
    put["sin"] = np.sin(angle) * np.where(np.arange(DR) < DR // 2, 1, -1).astype(np.float32)[:, None]
    put["ident"] = np.eye(P, dtype=np.float32)
    later = np.arange(P)[None, :] > np.arange(P)[:, None]
    put["causal"] = np.where(np.stack([later, later.T]), np.float32(NEG), np.float32(0))
    put["lower"] = (np.arange(NE)[None, :] < np.arange(NE)[:, None]).astype(np.float32)

    nc = bacc.Bacc("TRN2", target_bir_lowering=False, num_devices=1)
    ins, arrays = {}, {}
    for n, t in put.items():
        t = np.ascontiguousarray(t)
        arrays["in_" + n] = t
        ins[n] = nc.dram_tensor("in_" + n, t.shape, mybir.dt.from_np(t.dtype), kind="ExternalInput").ap()
    out = nc.dram_tensor("out", [B, S, E], F32, kind="ExternalOutput").ap()
    build(nc, ins, out)
    r = run_bass_kernel_spmd(nc, [arrays], core_ids=[0])
    return np.asarray(r.results[0]["out"])
```

```python
from contextlib import ExitStack

import numpy as np
import concourse.bass as bass
from concourse import mybir

F32 = mybir.dt.float32
F32R = mybir.dt.float32r
BF16 = mybir.dt.bfloat16
ALU = mybir.AluOpType
ACT = mybir.ActivationFunctionType
AX = mybir.AxisListType

P = 128
B, S, E = 4, 1024, 256
H, HD = 16, 16
DR = 128
NT = S // P
BANK = 512
NC = S // BANK
CH = BANK
CT = CH // P
GH = 4
G = H // GH
SLOTS = 3
EPS = 1e-5
NEG = -3.0e38
NE, TOPK, HID = 8, 2, 128
NF = 2 + NE
ROUTE_SCALE = 2.5

PARTS = 4 * HD
ROWS = 96
ROWS_M = ROWS + 2

STEPS = [(c, j) for c in range(NC) for j in range((c + 1) * BANK // P)]
NS = len(STEPS)
UNITS = NS * GH
DIAG = [P * j >= BANK * c for c, j in STEPS]


def width(step):
    c, j = STEPS[step]
    return BANK * (c + 1) - max(BANK * c, P * j)


def first_query(step):
    c, j = STEPS[step]
    return max(BANK * c, P * j)


MAX_STEPS = 9


def share_max_tiles():
    total = GH * sum(P * (i + 1) for i in range(NT))
    out = [[[] for _ in range(NS)] for _ in range(G)]
    for group in range(1, G):
        places = [(group - 2, s) for s in range(MAX_STEPS, NS)] if group > 1 else []
        places += [(group - 1, s) for s in range(MAX_STEPS)]
        room = sum(width(s) for _, s in places)
        tile, done, target = 0, 0, 0
        for g, s in places:
            target += width(s) * total / room
            while tile < GH * NT and (done < target - 1 or (g, s) == places[-1]):
                out[g][s].append((group, tile))
                done += P * (tile % NT + 1)
                tile += 1
    return out


MAX_IN_STEP = share_max_tiles()


class Counter:

    def __init__(self, ctx, nc, name, per_turn):
        self.sem = ctx.enter_context(nc.semaphore(name))
        self.per_turn = per_turn

    def at(self, turn, k):
        return turn * self.per_turn + (max(k, 0) + 1)

    def before(self, turn, k):
        return turn * self.per_turn + (k + 1)


def start_counters(nc, counters):
    with nc.Block() as block:
        @block.sync
        def _(sp):
            for c in counters:
                sp.sem_inc(c.sem, 1)


def stage_0(nc, d, gate_all, mod_all):
    with ExitStack() as ctx:
        sb = lambda n, s, t=F32: ctx.enter_context(nc.sbuf_tensor(n, s, t))
        sem = lambda n: ctx.enter_context(nc.semaphore(n))
        ps = ctx.enter_context(nc.psum_tensor("ps_mod", [P, 8, BANK], F32))
        wmod = sb("wmod", [P, 2, 6 * E])
        cT = sb("cT", [P, 2, B])
        sT = sb("sT", [P, 2, B])
        s_wide = sb("s_wide", [P, 2, B, P])
        mag = sb("mag", [P, 2, E])
        sign2 = sb("sign2", [P, 2, E])
        loaded, silu_ready, wide_ready = sem("mod_loaded"), sem("silu_ready"), sem("wide_ready")
        cols_ready, rows_ready, gate_chain = sem("cols_ready"), sem("rows_ready"), sem("gate_chain")
        block = ctx.enter_context(nc.Block())

        @block.sync
        def _(sp):
            sp.dma_start(wmod[:], d["wmod"].rearrange("(k p) n -> p k n", p=P)).then_inc(loaded, 16)
            sp.dma_start(cT[:], d["cT"].rearrange("(k p) b -> p k b", p=P)).then_inc(loaded, 16)

        @block.scalar
        def _(act):
            act.wait_ge(loaded, 32)
            nc.scalar.activation(sT[:], cT[:], ACT.Silu).then_inc(silu_ready, 1)

        @block.tensor
        def _(pe):
            pe.wait_ge(silu_ready, 1)
            for m, part in enumerate((0, 1, 3, 4)):
                for f in range(2):
                    for k in range(2):
                        o = part * E + f * P
                        last = nc.tensor.matmul(ps[:, 0, (m * 2 + f) * B:(m * 2 + f + 1) * B], wmod[:, k, o:o + P],
                                                sT[:, k, :], start=(k == 0), stop=(k == 1))
            last.then_inc(cols_ready, 1)
            pe.wait_ge(wide_ready, 1)
            for b in range(B):
                for g, part in enumerate((2, 5)):
                    for k in range(2):
                        last = nc.tensor.matmul(ps[:, 1 + b, g * E:(g + 1) * E], s_wide[:, k, b, :],
                                                wmod[:, k, part * E:(part + 1) * E], start=(k == 0), stop=(k == 1))
                last.then_inc(rows_ready, 1)

        @block.vector
        def _(dve):
            dve.wait_ge(silu_ready, 1)
            nc.vector.tensor_copy(s_wide[:], sT[:].unsqueeze(3).broadcast_to([P, 2, B, P])).then_inc(wide_ready, 1)
            dve.wait_ge(cols_ready, 1)
            for m in range(4):
                src = ps[:, 0, m * 2 * B:(m + 1) * 2 * B].rearrange("p (f b) -> p b f", b=B)
                nc.vector.tensor_scalar(mod_all[:, :, m, :], src, float(m % 2), None, ALU.add)
            for b in range(B):
                dve.wait_ge(rows_ready, b + 1)
                row = ps[:, 1 + b, :].rearrange("p (g n) -> p g n", g=2)
                nc.vector.tensor_scalar(mag[:], row, -1.0, 0.25, ALU.mult, ALU.max).then_inc(gate_chain, 1)
                nc.vector.tensor_scalar(sign2[:], row, 0.0, 2.0, ALU.is_ge, ALU.mult).then_inc(gate_chain, 1)
                dve.wait_ge(gate_chain, 4 * b + 2)
                nc.vector.tensor_tensor(mag[:], row, mag[:], ALU.max).then_inc(gate_chain, 1)
                dve.wait_ge(gate_chain, 4 * b + 3)
                nc.vector.scalar_tensor_tensor(gate_all[:, :, b, :], sign2[:], -1.0, mag[:], ALU.add,
                                               ALU.mult).then_inc(gate_chain, 1)
                dve.wait_ge(gate_chain, 4 * b + 4)


def stage_a(nc, d, ident, gate_all, mod_all):
    with ExitStack() as ctx:
        sb = lambda n, s, t=F32: ctx.enter_context(nc.sbuf_tensor(n, s, t))
        sem = lambda n: ctx.enter_context(nc.semaphore(n))
        counters = []

        def cnt(name, per_turn):
            counters.append(Counter(ctx, nc, name, per_turn))
            return counters[-1]

        ps = ctx.enter_context(nc.psum_tensor("ps_attn", [P, 8, BANK], F32))

        score_bank = lambda slot: 2 * slot
        ST_BANK, OUT_BANK = 4, 6

        w_lat = sb("w_lat", [P, 2, 2 * 64])
        w_qr, w_kr = sb("w_qr", [P, 2, DR]), sb("w_kr", [P, 2, DR])
        w_c = sb("w_c", [P, 2, P])
        w_v = sb("w_v", [P, E])
        w_o = sb("w_o", [P, 2, E])
        bias = sb("bias", [P, 5])
        bv_row, bo_row = sb("bv_row", [P, E]), sb("bo_row", [P, E])
        cos_t, sin_t = sb("cos_t", [P, S]), sb("sin_t", [P, S])
        causal = sb("causal", [P, P], BF16)
        causal_t = sb("causal_t", [P, P], BF16)
        ident_b = sb("ident_b", [P, P], BF16)
        neg_half = sb("neg_half", [P, NT])
        pad = sb("pad", [P, 1])

        x = sb("x", [P, NT, E])
        x_hat = sb("x_hat", [P, NT, E])
        out_nat = sb("out_nat", [P, NT, E])
        out_t = sb("out_t", [P, 2, S])
        probs = sb("probs", [P, 2, GH, BANK])
        v = sb("v", [P, NT, H, 2 * HD])
        op_q, op_k = sb("op_q", [P, SLOTS, GH, S], F32R), sb("op_k", [P, SLOTS, GH, S], F32R)
        parts = sb("parts", [P, 2, 2, BANK])
        out_raw = sb("out_raw", [P, BANK])
        inv_sum = sb("inv_sum", [P, CT * GH])
        stats, mean_var = sb("stats", [P, NT, 6]), sb("mean_var", [P, NT, 2])
        rstd = sb("rstd", [P, NT])
        neg_max, neg_max_parts = sb("neg_max", [P, GH * NT]), sb("neg_max_parts", [P, 2, GH * NT])
        max_rows = sb("max_rows", [2 * GH * NT, P])
        mod = sb("mod", [P, 4, 2])
        gate, gate_bias = sb("gate", [P, E]), sb("gate_bias", [P, E])
        proj = sb("proj", [P, E])

        h_t = out_nat[:].rearrange("p t e -> p (t e)").rearrange("p (f s) -> p f s", f=2)
        rope = out_t[:].rearrange("p r (a n) -> p r a n", a=2)
        latent = probs[:, 1, 0:2, :].rearrange("p a n -> p (a n)")
        raw = probs[:, 1, 2:4, :]

        scratch = nc.dram_tensor("qk_parts", [2, 2, E, S], F32, kind="Internal").ap()

        w_loaded, w_set = sem("w_loaded"), sem("w_set")
        pads_set = sem("pads_set")
        pool_set = sem("pool_set")
        ticks = [sem(f"tick_a{i}") for i in range(4)]
        res_loaded = cnt("res_loaded", 16)
        x_loaded, stats_chain = cnt("x_loaded", 16), cnt("stats_chain", 2)
        mod_ready = cnt("mod_ready", 2)
        var_ready, rstd_ready, xhat_ready = cnt("var_ready", 1), cnt("rstd_ready", 1), cnt("xhat_ready", NT)
        xt_done, ht_ready = cnt("xt_done", 4), cnt("ht_ready", 4)
        lat_done, lat_ready = cnt("lat_done", NC), cnt("lat_ready", NC)
        qk_done, raw_ready = cnt("qk_done", 8), cnt("raw_ready", 8)
        rope_terms, rope_ready = cnt("rope_terms", 8), cnt("rope_ready", 4)
        lo_ready = cnt("lo_ready", 8)
        parts_stored = [cnt(f"parts_stored{i}", 64) for i in range(2)]
        ops_loaded = [[cnt(f"ops_loaded{s}_{h}", 64 * (2 if s == 0 else 1)) for h in range(GH)] for s in range(SLOTS)]
        v_done, v_ready = cnt("v_done", NT), cnt("v_ready", NT)
        score_done, max_done = cnt("score_done", G * GH * NT), cnt("max_done", G * GH * NT)
        m_chain, m_split = cnt("m_chain", G), cnt("m_split", G)
        mt_done, mt_ready, m_loaded = cnt("mt_done", G), cnt("mt_ready", G), cnt("m_loaded", 32 * G)
        st_done, prob_ready = cnt("st_done", G * UNITS), cnt("prob_ready", G * UNITS)
        pv_done = cnt("pv_done", G * NS)
        raw_out_ready, raw_out_turned = cnt("raw_out_ready", G * NC), cnt("raw_out_turned", G * NC)
        inv_ready, out_ready = cnt("inv_ready", G * NC), cnt("out_ready", G * NC)
        out_turned, out_t_ready = cnt("out_turned", 2 * NC), cnt("out_t_ready", 2 * NC)
        gate_bias_ready, xb_ready = cnt("gate_bias_ready", 1), cnt("xb_ready", 1)
        proj_done, proj_scaled, x1_ready = cnt("proj_done", NT), cnt("proj_scaled", NT), cnt("x1_ready", NT)
        x1_stored = cnt("x1_stored", 16)

        N_WLOAD = 8 + 2 + 4 + 2 + 2

        start_counters(nc, counters)
        block = ctx.enter_context(nc.Block())

        @block.sync
        def _(sp):
            sp.wait_ge(w_set, 1)

            def load(dst, src):
                sp.dma_start(dst, src).then_inc(w_loaded, 16)

            load(w_lat[:, :, 0:64], d["wq"].rearrange("(k p) n -> p k n", p=P))
            load(w_lat[:, :, 64:128], d["wkv"].rearrange("(k p) n -> p k n", p=P))
            load(w_qr[:], d["wqr"].rearrange("(k p) n -> p k n", p=P))
            load(w_kr[:], d["wkr"].rearrange("(k p) n -> p k n", p=P))
            load(w_c[0:64, 0, :], d["wqc"])
            load(w_c[64:128, 1, :], d["wkc"])
            load(w_v[64:128, :], d["wv"])
            load(w_o[:], d["wo"].rearrange("(k p) n -> p k n", p=P))
            load(bias[0:64, 0:1], d["bq"].unsqueeze(1))
            load(bias[64:128, 0:1], d["bkv"].unsqueeze(1))
            for i, n in enumerate(("bqc", "bkc", "bqr", "bkr")):
                load(bias[:, 1 + i:2 + i], d[n].unsqueeze(1))
            load(bv_row[:], d["bv"].unsqueeze(0).broadcast_to([P, E]))
            load(bo_row[:], d["bo"].unsqueeze(0).broadcast_to([P, E]))
            load(cos_t[:], d["cos"])
            load(sin_t[:], d["sin"])

            sp.dma_start(x_hat[:], d["x"][0:1].rearrange("o (t p) e -> p (o t) e", p=P)).then_inc(x_loaded.sem, 16)
            with sp.Fori(0, B) as b:

                def store_parts(n):
                    kind, c = qk_item(n)
                    sp.wait_ge(lo_ready.sem, lo_ready.at(b, n + 1))
                    sp.sem_inc(ticks[2], 1)
                    if n == 0:
                        for h in range(GH):
                            sp.wait_ge(ops_loaded[0][h].sem, ops_loaded[0][h].at(b, 0))
                    dst = scratch[kind % 2, :, P * (kind // 2):P * (kind // 2) + P, c * BANK:(c + 1) * BANK]
                    sp.dma_start(dst.rearrange("a p s -> p a s"), parts[:, n % 2]).then_inc(
                        parts_stored[n % 2].sem, 16)

                def load_operands(g):
                    slot = g % SLOTS
                    for h in range(GH):
                        f = (g * GH + h) * HD
                        for r in range(2):
                            q_src = scratch[0, r:r + 1, f:f + HD, :].broadcast_to([2, HD, S])
                            k_src = scratch[1, :, f:f + HD, :]
                            rows = slice(32 * r, 32 * r + 32)
                            sp.dma_start(op_q[rows, slot, h, :].bitcast(F32), q_src).then_inc(
                                ops_loaded[slot][h].sem, 16)
                            sp.dma_start(op_k[rows, slot, h, :].bitcast(F32), k_src).then_inc(
                                ops_loaded[slot][h].sem, 16)

                def load_max_rows(g):
                    sp.wait_ge(mt_ready.sem, mt_ready.at(b, g + 1))
                    slot = g % SLOTS
                    n = GH * NT
                    for r in range(2):
                        dst = op_q[ROWS + r:ROWS + r + 1, slot, :, :].bitcast(F32)
                        sp.dma_start(dst.rearrange("p h (t s) -> p (h t) s", s=P), max_rows[n * r:n * r + n, :]).then_inc(
                            m_loaded.sem, 16)

                for n in range(4):
                    store_parts(n)
                for i in range(2):
                    sp.wait_ge(parts_stored[i].sem, parts_stored[i].at(b, 32))
                    sp.sem_inc(ticks[2], 1)
                sp.wait_ge(st_done.sem, st_done.at(b, 0))
                load_operands(0)
                for n in range(4, 8):
                    store_parts(n)
                load_operands(1)
                for i in range(2):
                    sp.wait_ge(parts_stored[i].sem, parts_stored[i].at(b, 64))
                    sp.sem_inc(ticks[2], 1)
                sp.wait_ge(x1_stored.sem, x1_stored.at(b, 0))
                sp.sem_inc(ticks[2], 1)
                sp.dma_start(x[:], d["x"][bass.ds(b, 1)].rearrange("o (t p) e -> p (o t) e", p=P)).then_inc(
                    res_loaded.sem, 16)
                load_max_rows(0)
                load_operands(2)
                load_max_rows(1)
                sp.wait_ge(xt_done.sem, xt_done.at(b, 4))
                sp.sem_inc(ticks[2], 1)
                sp.dma_start(x_hat[:], d["x"][bass.ds((b + 1) % B, 1)].rearrange(
                    "o (t p) e -> p (o t) e", p=P)).then_inc(x_loaded.sem, 16)
                sp.wait_ge(st_done.sem, st_done.at(b, UNITS))
                sp.sem_inc(ticks[2], 1)
                sp.wait_ge(max_done.sem, max_done.at(b, GH * NT))
                load_operands(3)
                load_max_rows(2)
                load_max_rows(3)

                sp.wait_ge(x1_ready.sem, x1_ready.at(b, NT))
                sp.sem_inc(ticks[2], 1)
                sp.dma_start(d["x1"][bass.ds(b, 1)].rearrange("o (t p) e -> p (o t) e", p=P), x[:]).then_inc(
                    x1_stored.sem, 16)
            sp.wait_ge(x1_stored.sem, x1_stored.at(B, 0))
            sp.wait_ge(x_loaded.sem, x_loaded.at(B, 16))

        @block.gpsimd
        def _(pool):
            nc.gpsimd.memset(op_q[PARTS:ROWS, 0].bitcast(F32), 0.0).then_inc(pool_set, 1)
            pool.wait_ge(pool_set, 1)
            nc.gpsimd.memset(v[:], 1.0).then_inc(pool_set, 1)
            pool.wait_ge(pool_set, 2)
            pool.wait_ge(w_set, 1)

            def inverse_deviation(turn):
                pool.wait_ge(var_ready.sem, var_ready.at(turn, 1))
                nc.gpsimd.tensor_tensor(rstd[:], rstd[:], neg_half[:], ALU.pow).then_inc(rstd_ready.sem, 1)

            inverse_deviation(0)
            with pool.Fori(0, B) as b:
                def lo_part(n):
                    pool.wait_ge(raw_ready.sem, raw_ready.at(b, n + 1))
                    nc.gpsimd.tensor_tensor(parts[:, n % 2, 1, :].bitcast(F32R), raw[:, n % 2, :], parts[:, n % 2, 0, :],
                                            ALU.subtract).then_inc(lo_ready.sem, 1)

                def rope_sum(r):
                    pool.wait_ge(rope_terms.sem, rope_terms.at(b, 2 * r + 2))
                    nc.gpsimd.tensor_tensor(rope[:, r % 2, 0, :], rope[:, r % 2, 0, :], rope[:, r % 2, 1, :],
                                            ALU.add).then_inc(rope_ready.sem, 1)

                for n in range(4):
                    lo_part(n)
                rope_sum(0)
                rope_sum(1)
                lo_part(4)
                rope_sum(2)
                lo_part(5)
                rope_sum(3)
                lo_part(6)
                lo_part(7)
                pool.wait_ge(mod_ready.sem, mod_ready.at(b, 2))
                nc.gpsimd.tensor_tensor(gate_bias[:], gate[:], bo_row[:], ALU.mult).then_inc(gate_bias_ready.sem, 1)
                pool.wait_ge(gate_bias_ready.sem, gate_bias_ready.at(b, 1))
                pool.wait_ge(res_loaded.sem, res_loaded.at(b, 16))
                nc.gpsimd.tensor_tensor(x[:], x[:], gate_bias[:].unsqueeze(1).broadcast_to([P, NT, E]),
                                        ALU.add).then_inc(xb_ready.sem, 1)
                inverse_deviation(b + 1)

        @block.scalar
        def _(act):
            act.wait_ge(w_set, 2)
            n = SLOTS * GH * S
            nc.scalar.activation(op_k[PARTS:ROWS_M].rearrange("p a h s -> p (a h s)"),
                                 pad[PARTS:ROWS_M].broadcast_to([ROWS_M - PARTS, n]), ACT.Copy).then_inc(pads_set, 1)
            n = (SLOTS - 1) * GH * S
            nc.scalar.activation(op_q[PARTS:ROWS, 1:SLOTS].rearrange("p a h s -> p (a h s)"),
                                 pad[PARTS:ROWS].broadcast_to([ROWS - PARTS, n]), ACT.Copy).then_inc(pads_set, 1)
            act.wait_ge(w_loaded, 16 * N_WLOAD)
            with act.Fori(0, B) as b:
                act.wait_ge(mod_ready.sem, mod_ready.at(b, 2))
                act.wait_ge(out_turned.sem, out_turned.at(b, 0))
                for c in range(NC):
                    for f in range(2):
                        act.wait_ge(xt_done.sem, xt_done.at(b, 2 * c + f + 1))
                        nc.scalar.activation(h_t[:, f, c * BANK:(c + 1) * BANK], ps[:, 2 * c + f, :], ACT.Identity,
                                             bias=mod[:, 0, f:f + 1], scale=mod[:, 1, f:f + 1]).then_inc(ht_ready.sem, 1)
                for c in range(NC):
                    act.wait_ge(lat_done.sem, lat_done.at(b, c + 1))
                    act.wait_ge(pv_done.sem, pv_done.at(b, 0))
                    nc.scalar.activation(latent[:, c * BANK:(c + 1) * BANK], ps[:, ST_BANK + c, :], ACT.Gelu,
                                         bias=bias[:, 0:1]).then_inc(lat_ready.sem, 1)
                for n in range(8):
                    kind, c = qk_item(n)
                    if n < 4:
                        act.wait_ge(qk_done.sem, qk_done.at(b, n + 1))
                        src, col = ps[:, n % 4, :], bias[:, 1 + kind:2 + kind]
                    else:
                        act.wait_ge(rope_ready.sem, rope_ready.at(b, n - 3))
                        src, col = rope[:, n % 2, 0, :], 0.0
                    act.wait_ge(parts_stored[n % 2].sem, parts_stored[n % 2].at(b, 16 * (n // 2)))
                    nc.scalar.activation(parts[:, n % 2, 0, :].bitcast(F32R), src, ACT.Gelu, bias=col)
                    if n >= 2:
                        act.wait_ge(lo_ready.sem, lo_ready.at(b, n - 1))
                    nc.scalar.activation(raw[:, n % 2, :], src, ACT.Gelu, bias=col).then_inc(raw_ready.sem, 1)
                act.wait_ge(lo_ready.sem, lo_ready.at(b, 8))
                act.wait_ge(v_done.sem, v_done.at(b, NT))

                def copy_out(g, c):
                    act.wait_ge(pv_done.sem, pv_done.at(b, g * NS + (CT if c == 0 else NS)))
                    act.wait_ge(raw_out_turned.sem, raw_out_turned.at(b, g * NC + c))
                    nc.scalar.activation(out_raw[:], ps[:, OUT_BANK + c, :], ACT.Copy).then_inc(raw_out_ready.sem, 1)

                for g in range(G):
                    for s in range(NS):
                        n = g * NS + s
                        for h in range(GH):
                            u = GH * n + h
                            act.wait_ge(st_done.sem, st_done.at(b, u + 1))
                            if h == 0 and n >= 2:
                                act.wait_ge(pv_done.sem, pv_done.at(b, n - 1))
                            w = width(s)
                            nc.scalar.activation(probs[:, n % 2, h, 0:w], ps[:, ST_BANK + u % 2, 0:w], ACT.Exp,
                                                 scale=float(HD) ** -0.5).then_inc(prob_ready.sem, 1)
                        if s == 1 and g > 0:
                            copy_out(g - 1, 1)
                        if s == 5:
                            copy_out(g, 0)
                copy_out(G - 1, 1)
                for c in range(NC):
                    for f in range(2):
                        act.wait_ge(out_turned.sem, out_turned.at(b, 2 * c + f + 1))
                        nc.scalar.activation(out_t[:, f, c * BANK:(c + 1) * BANK], ps[:, 2 * c + f, :],
                                             ACT.Copy).then_inc(out_t_ready.sem, 1)

        @block.vector
        def _(dve):
            nc.vector.memset(w_c[:], 0.0)
            nc.vector.memset(w_v[:], 0.0)
            nc.vector.memset(neg_half[:], -0.5)
            nc.vector.memset(pad[:], 0.0).then_inc(w_set, 1)
            dve.wait_ge(w_set, 1)
            nc.vector.memset(pad[ROWS:ROWS_M], 1.0).then_inc(w_set, 1)

            def layer_norm(turn):
                dve.wait_ge(x_loaded.sem, x_loaded.at(turn, 16))
                for t in range(NT):
                    last = nc.vector.bn_stats(stats[:, t, :], x_hat[:, t, :])
                last.then_inc(stats_chain.sem, 1)
                dve.wait_ge(stats_chain.sem, stats_chain.at(turn, 1))
                dve.sem_inc(ticks[3], 1)
                for t in range(NT):
                    last = nc.vector.bn_aggr(mean_var[:, t, :], stats[:, t, :])
                last.then_inc(stats_chain.sem, 1)
                dve.wait_ge(stats_chain.sem, stats_chain.at(turn, 2))
                nc.vector.tensor_scalar(rstd[:], mean_var[:, :, 1], EPS, None, ALU.add).then_inc(var_ready.sem, 1)

            def normalise_input(turn):
                dve.wait_ge(rstd_ready.sem, rstd_ready.at(turn, 1))
                for t in range(NT):
                    nc.vector.tensor_scalar(x_hat[:, t, :], x_hat[:, t, :], mean_var[:, t, 0:1], rstd[:, t:t + 1],
                                            ALU.subtract, ALU.mult).then_inc(xhat_ready.sem, 1)

            layer_norm(0)
            nc.vector.tensor_copy(causal[:], d["causal_sb"][:, 0, :])
            nc.vector.tensor_copy(causal_t[:], d["causal_sb"][:, 1, :])
            nc.vector.tensor_copy(ident_b[:], ident[:]).then_inc(w_set, 1)
            normalise_input(0)
            dve.wait_ge(w_loaded, 16 * N_WLOAD)
            with dve.Fori(0, B) as b:
                dve.wait_ge(ht_ready.sem, ht_ready.at(b, 0))
                nc.vector.tensor_copy(mod[:].unsqueeze(1), mod_all[:, bass.ds(b, 1), :, :]).then_inc(mod_ready.sem, 1)
                dve.wait_ge(xb_ready.sem, xb_ready.at(b, 0))
                nc.vector.tensor_copy(gate[:].unsqueeze(1), gate_all[:, 0, bass.ds(b, 1), :]).then_inc(mod_ready.sem, 1)
                dve.wait_ge(proj_done.sem, proj_done.at(b, 0))

                def rope_mult(r):
                    n = 4 + r
                    kind, c = qk_item(n)
                    dve.wait_ge(qk_done.sem, qk_done.at(b, n + 1))
                    if r >= 2:
                        dve.wait_ge(raw_ready.sem, raw_ready.at(b, n - 1))
                    cols = slice(c * BANK, (c + 1) * BANK)
                    y, bcol = ps[:, n % 4, :], bias[:, 1 + kind:2 + kind]
                    nc.vector.scalar_tensor_tensor(rope[:, r % 2, 0, :], y, bcol, cos_t[:, cols], ALU.add,
                                                   ALU.mult)
                    for lo, hi in ((0, 64), (64, 0)):
                        nc.vector.scalar_tensor_tensor(rope[hi:hi + 64, r % 2, 1, :], y[lo:lo + 64], bcol[lo:lo + 64],
                                                       sin_t[lo:lo + 64, cols], ALU.add,
                                                       ALU.mult).then_inc(rope_terms.sem, 1)

                for r in range(4):
                    rope_mult(r)
                for t in range(NT):
                    dve.wait_ge(v_done.sem, v_done.at(b, t + 1))
                    src = ps[:, OUT_BANK + t % 2, 0:E].rearrange("p (h e) -> p h e", e=HD)
                    nc.vector.tensor_tensor(v[:, t, :, 0:HD], src, bv_row[:].rearrange("p (h e) -> p h e", e=HD),
                                            ALU.add).then_inc(v_ready.sem, 1)

                def row_max(g, tile):
                    t = g * GH * NT + tile
                    dve.wait_ge(score_done.sem, score_done.at(b, t + 1))
                    w = P * (tile % NT + 1)
                    bank = score_bank(tile % 2)
                    src = ps[:, bank:bank + 2, :].rearrange("p a n -> p (a n)")[:, 0:w]
                    nc.vector.tensor_reduce(neg_max[:, tile:tile + 1], src, AX.X, ALU.max,
                                            negate=True).then_inc(max_done.sem, 1)

                def split_max(g):
                    dve.wait_ge(max_done.sem, max_done.at(b, GH * NT * (g + 1)))
                    nc.vector.tensor_copy(neg_max_parts[:, 0, :].bitcast(F32R), neg_max[:]).then_inc(m_chain.sem, 1)
                    dve.wait_ge(m_chain.sem, m_chain.at(b, g + 1))
                    nc.vector.tensor_tensor(neg_max_parts[:, 1, :].bitcast(F32R), neg_max[:], neg_max_parts[:, 0, :],
                                            ALU.subtract).then_inc(m_split.sem, 1)

                def max_to_rows(g):
                    dve.wait_ge(mt_done.sem, mt_done.at(b, g + 1))
                    dve.wait_ge(m_loaded.sem, m_loaded.at(b, 32 * g))
                    nc.vector.tensor_copy(max_rows[:], ps[0:2 * GH * NT, 0, 0:P]).then_inc(mt_ready.sem, 1)

                def normalise(g, c):
                    n = g * NC + c
                    dve.wait_ge(raw_out_turned.sem, raw_out_turned.at(b, n + 1))
                    src = ps[:, OUT_BANK + c, :].rearrange("p (t h e) -> p t h e", h=GH, e=2 * HD)
                    inv = inv_sum[:].rearrange("p (t h) -> p t h", h=GH)
                    dve.wait_ge(out_ready.sem, out_ready.at(b, n))
                    nc.vector.reciprocal(inv, src[:, :, :, HD]).then_inc(inv_ready.sem, 1)
                    dve.wait_ge(inv_ready.sem, inv_ready.at(b, n + 1))
                    for t in range(CT):
                        dst = out_nat[:, c * CT + t, g * GH * HD:(g + 1) * GH * HD].rearrange("p (h e) -> p h e", e=HD)
                        last = nc.vector.tensor_tensor(dst, src[:, t, :, 0:HD],
                                                       inv[:, t, :].unsqueeze(2).broadcast_to([P, GH, HD]), ALU.mult)
                    last.then_inc(out_ready.sem, 1)

                for tile in range(GH * NT):
                    row_max(0, tile)
                split_max(0)
                max_to_rows(0)
                for g in range(G):
                    for s in range(NS):
                        if g + 1 < G and s == MAX_STEPS:
                            max_to_rows(g + 1)
                        for group, tile in MAX_IN_STEP[g][s]:
                            row_max(group, tile)
                        if g + 1 < G and s + 1 == MAX_STEPS:
                            split_max(g + 1)
                        if g == G - 1 and s == 1:
                            layer_norm(b + 1)
                        if g == G - 1 and s == 4:
                            normalise_input(b + 1)
                        if s == 3 and g > 0:
                            normalise(g - 1, 1)
                        if s == 7:
                            normalise(g, 0)
                normalise(G - 1, 1)
                dve.wait_ge(xb_ready.sem, xb_ready.at(b, 1))
                for t in range(NT):
                    dve.wait_ge(proj_done.sem, proj_done.at(b, t + 1))
                    nc.vector.tensor_tensor(proj[:], ps[:, ST_BANK + t % 2, 0:E], gate[:], ALU.mult).then_inc(
                        proj_scaled.sem, 1)
                    dve.wait_ge(proj_scaled.sem, proj_scaled.at(b, t + 1))
                    nc.vector.tensor_tensor(x[:, t, :], x[:, t, :], proj[:], ALU.add).then_inc(x1_ready.sem, 1)
                    dve.wait_ge(x1_ready.sem, x1_ready.at(b, t + 1))

        @block.tensor
        def _(pe):
            pe.wait_ge(w_loaded, 16 * N_WLOAD)
            pe.wait_ge(w_set, 3)
            pe.wait_ge(pads_set, 2)
            pe.wait_ge(pool_set, 2)
            with pe.Fori(0, B) as b:
                pe.wait_ge(out_t_ready.sem, out_t_ready.at(b, 0))
                for t in range(NT):
                    pe.wait_ge(xhat_ready.sem, xhat_ready.at(b, t + 1))
                    for f in range(2):
                        c, o = t // 4, P * (t % 4)
                        last = nc.tensor.transpose(ps[:, 2 * c + f, o:o + P], x_hat[:, t, f * P:(f + 1) * P], ident[:])
                        if t % 4 == 3:
                            last.then_inc(xt_done.sem, 1)
                pe.wait_ge(x1_ready.sem, x1_ready.at(b, 0))
                for c in range(NC):
                    pe.wait_ge(ht_ready.sem, ht_ready.at(b, 2 * c + 2))
                    for f in range(2):
                        last = nc.tensor.matmul(ps[:, ST_BANK + c, :], w_lat[:, f, :], h_t[:, f, c * BANK:(c + 1) * BANK],
                                                start=(f == 0), stop=(f == 1))
                    last.then_inc(lat_done.sem, 1)
                for n in range(8):
                    kind, c = qk_item(n)
                    cols = slice(c * BANK, (c + 1) * BANK)
                    if n < 4:
                        pe.wait_ge(lat_ready.sem, lat_ready.at(b, c + 1))
                        pe.wait_ge(ht_ready.sem, ht_ready.at(b, 4))
                        last = nc.tensor.matmul(ps[:, n % 4, :], w_c[:, kind, :], latent[:, cols], start=True, stop=True)
                    else:
                        pe.wait_ge(raw_ready.sem, raw_ready.at(b, n - 3))
                        w = (w_qr, w_kr)[kind - 2]
                        for f in range(2):
                            last = nc.tensor.matmul(ps[:, n % 4, :], w[:, f, :], h_t[:, f, cols],
                                                    start=(f == 0), stop=(f == 1))
                    last.then_inc(qk_done.sem, 1)
                pe.wait_ge(out_ready.sem, out_ready.at(b, 0))
                for t in range(NT):
                    pe.wait_ge(v_ready.sem, v_ready.at(b, t - 1))
                    nc.tensor.matmul(ps[:, OUT_BANK + t % 2, 0:E], latent[:, t * P:(t + 1) * P], w_v[:],
                                     start=True, stop=True).then_inc(v_done.sem, 1)

                def scores(g, tile):
                    h, i, slot, t = tile // NT, tile % NT, g % SLOTS, g * GH * NT + tile
                    if i == 0:
                        pe.wait_ge(ops_loaded[slot][h].sem, ops_loaded[slot][h].at(b, 128 if g == 3 else 64))
                    if tile < 2:
                        if g == 0:
                            pe.wait_ge(rope_terms.sem, rope_terms.at(b, 8))
                        else:
                            pe.wait_ge(mt_ready.sem, mt_ready.at(b, g))
                    pe.wait_ge(max_done.sem, max_done.at(b, t - 1))
                    bank = score_bank(tile % 2)
                    q = op_q[0:ROWS, slot, h, i * P:(i + 1) * P]
                    for k0 in range(0, P * (i + 1), BANK):
                        k1 = min(k0 + BANK, P * (i + 1))
                        last_piece = k1 == P * (i + 1)
                        nc.tensor.matmul(ps[:, bank + k0 // BANK, 0:k1 - k0], q, op_k[0:ROWS, slot, h, k0:k1],
                                         start=True, stop=not last_piece)
                    o = P * i % BANK
                    nc.tensor.matmul(ps[:, bank + P * i // BANK, o:o + P], ident_b[:], causal[:], start=False,
                                     stop=True).then_inc(score_done.sem, 1)

                def transpose_max(g):
                    pe.wait_ge(m_split.sem, m_split.at(b, g + 1))
                    pe.sem_inc(ticks[1], 1)
                    nc.tensor.transpose(ps[0:2 * GH * NT, 0, 0:P],
                                        neg_max_parts[:].rearrange("p a n -> p (a n)"), ident[:]).then_inc(
                                            mt_done.sem, 1)

                def scores_t(g, s, h):
                    c, j = STEPS[s]
                    slot, u = g % SLOTS, (g * NS + s) * GH + h
                    if s == 0 and h == 0:
                        pe.wait_ge(m_loaded.sem, m_loaded.at(b, 32 * (g + 1)))
                        if g == 0:
                            pe.wait_ge(lat_ready.sem, lat_ready.at(b, 2))
                    pe.wait_ge(prob_ready.sem, prob_ready.at(b, u - 1))
                    q0, w = first_query(s), width(s)
                    last = nc.tensor.matmul(ps[:, ST_BANK + u % 2, 0:w], op_k[0:ROWS_M, slot, h, j * P:(j + 1) * P],
                                            op_q[0:ROWS_M, slot, h, q0:q0 + w], start=True, stop=not DIAG[s])
                    if DIAG[s]:
                        last = nc.tensor.matmul(ps[:, ST_BANK + u % 2, 0:P], ident_b[:], causal_t[:], start=False,
                                                stop=True)
                    last.then_inc(st_done.sem, 1)

                def weigh_values(g, s):
                    c, j = STEPS[s]
                    n = g * NS + s
                    pe.wait_ge(prob_ready.sem, prob_ready.at(b, GH * (n + 1)))
                    if j == 0:
                        pe.wait_ge(v_ready.sem, v_ready.at(b, NT))
                        pe.wait_ge(out_ready.sem, out_ready.at(b, (g - 1) * NC + c + 1))
                    o, w = first_query(s) - c * BANK, width(s)
                    for h in range(GH):
                        last = nc.tensor.matmul(ps[32 * h:32 * h + 32, OUT_BANK + c, o:o + w], v[:, j, g * GH + h, :],
                                                probs[:, n % 2, h, 0:w], start=(j == 0), stop=(o + P == BANK))
                    last.then_inc(pv_done.sem, 1)

                def turn_out(g, c):
                    pe.wait_ge(raw_out_ready.sem, raw_out_ready.at(b, g * NC + c + 1))
                    for t in range(CT):
                        last = nc.tensor.transpose(ps[:, OUT_BANK + c, t * P:(t + 1) * P], out_raw[:, t * P:(t + 1) * P],
                                                   ident[:])
                    last.then_inc(raw_out_turned.sem, 1)

                for tile in range(GH * NT):
                    scores(0, tile)
                transpose_max(0)
                for g in range(G):
                    for s in range(NS):
                        tiles = MAX_IN_STEP[g][s]
                        half = len(tiles) // 2
                        scores_t(g, s, 0)
                        scores_t(g, s, 1)
                        if s != MAX_STEPS:
                            for tile in tiles[:half]:
                                scores(*tile)
                        if s > 0:
                            weigh_values(g, s - 1)
                        elif g > 0:
                            weigh_values(g - 1, NS - 1)
                        scores_t(g, s, 2)
                        scores_t(g, s, 3)
                        if s == MAX_STEPS:
                            if g + 1 < G:
                                transpose_max(g + 1)
                            half = 0
                        for tile in tiles[half:]:
                            scores(*tile)
                        if s == 2 and g > 0:
                            turn_out(g - 1, 1)
                        if s == 6:
                            turn_out(g, 0)
                weigh_values(G - 1, NS - 1)
                turn_out(G - 1, 1)
                pe.wait_ge(out_ready.sem, out_ready.at(b, G * NC))
                for c in range(NC):
                    for f in range(2):
                        for t in range(CT):
                            last = nc.tensor.transpose(ps[:, 2 * c + f, t * P:(t + 1) * P],
                                                       out_nat[:, c * CT + t, f * P:(f + 1) * P], ident[:])
                        last.then_inc(out_turned.sem, 1)
                pe.wait_ge(prob_ready.sem, prob_ready.at(b, G * UNITS))
                for t in range(NT):
                    pe.wait_ge(proj_scaled.sem, proj_scaled.at(b, t - 1))
                    if t % CT == 0:
                        pe.wait_ge(out_t_ready.sem, out_t_ready.at(b, 2 * (t // CT) + 2))
                    for f in range(2):
                        last = nc.tensor.matmul(ps[:, ST_BANK + t % 2, 0:E], out_t[:, f, t * P:(t + 1) * P], w_o[:, f, :],
                                                start=(f == 0), stop=(f == 1))
                    last.then_inc(proj_done.sem, 1)


def qk_item(n):
    return (n % 2 + (2 if n >= 4 else 0)), (n // 2) % 2


def stage_b(nc, d, ident, gate_all, mod_all, out):
    with ExitStack() as ctx:
        sb = lambda n, s, t=F32: ctx.enter_context(nc.sbuf_tensor(n, s, t))
        sem = lambda n: ctx.enter_context(nc.semaphore(n))
        counters = []

        def cnt(name, per_turn):
            counters.append(Counter(ctx, nc, name, per_turn))
            return counters[-1]

        ps = ctx.enter_context(nc.psum_tensor("ps_ffn", [P, 8, BANK], F32))
        OUT_BANK, FRONT_BANK = 4, 6

        w_in = sb("w_in", [P, 2, 2, NF * 2 * HID], F32R)
        w_out = sb("w_out", [P, 2, NF * E], F32R)
        staged = sb("staged", [P, 4, 3, E])
        w_router = sb("w_router", [P, 2, NE])
        lower = sb("lower", [P, NE, NE])
        neg_half = sb("neg_half_b", [P, CT])
        x1 = sb("x1_b", [P, 2, CT, E])
        res = sb("res", [P, 2, CT, E])
        x_hat = sb("x_hat_b", [P, CT, E])
        h_t = sb("h_t", [P, 2, CH])
        h_parts = sb("h_parts", [P, 2, 2, 2, CH], F32R)
        stats, mean_var, rstd = sb("stats_b", [P, CT, 6]), sb("mean_var_b", [P, CT, 2]), sb("rstd_b", [P, CT])
        logits_t = sb("logits_t", [NE, CH])
        ex = sb("ex", [P, CT, NE])
        prob = sb("prob", [P, CT, NE])
        beats, ties = sb("beats", [P, CT, NE, NE]), sb("ties", [P, CT, NE, NE])
        rank = sb("rank", [P, CT, NE])
        combine = sb("combine", [P, CT, NE])
        total, inv = sb("total", [P, CT]), sb("inv", [P, CT])
        combine_t = sb("combine_t", [NE, CH])
        share = sb("share", [P, 2, NE, CH])
        act_g = sb("act_g", [P, 3, CH])
        hidden = sb("hidden", [P, 2, CH])
        hid_parts = sb("hid_parts", [P, 3, 2, CH], F32R)
        scaled = sb("scaled", [P, 2, BANK])
        y = sb("y", [P, 2, CT, E])
        mod = sb("mod_b", [P, 2, 4, 2])
        gate = sb("gate_b", [P, 2, E])
        combine_d = nc.dram_tensor("combine_d", [2, NE, CH], F32, kind="Internal").ap()

        raw_loaded = [sem(f"raw_loaded{i}") for i in range(4)]
        small_loaded = sem("small_loaded")
        w_hi, w_lo = sem("w_hi"), sem("w_lo")
        ticks = [sem(f"tick_b{i}") for i in range(3)]
        x1_loaded = [cnt(f"x1_loaded{i}", 16) for i in range(2)]
        res_loaded = [cnt(f"res_loaded_b{i}", 16) for i in range(2)]
        chain = cnt("chain_b", 2 * CHAIN)
        mod_ready = cnt("mod_ready_b", 2)
        var_ready, rstd_ready, xhat_ready = cnt("var_ready_b", 2), cnt("rstd_ready_b", 2), cnt("xhat_ready_b", 2 * CT)
        xt_done, ht_ready = cnt("xt_done_b", 4), cnt("ht_ready_b", 4)
        h_hi, h_lo = cnt("h_hi", 2), cnt("h_lo", 2)
        logit_done, logit_ready = cnt("logit_done", 2), cnt("logit_ready", 2)
        logit_t_done, exp_ready = cnt("logit_t_done", 2), cnt("exp_ready", 2)
        combine_ready, ct_done, ct_ready = cnt("combine_ready", 2), cnt("ct_done", 2), cnt("ct_ready", 2)
        combine_stored = cnt("combine_stored", 32)
        share_loaded = [cnt(f"share_loaded{i}", 16) for i in range(2)]
        gu_done, silu_ready, weighed = cnt("gu_done", 2 * NF), cnt("silu_ready_b", 2 * NF), cnt("weighed", 2 * NE)
        hid_ready, hid_hi, hid_lo = cnt("hid_ready", 2 * NF), cnt("hid_hi", 2 * NF), cnt("hid_lo", 2 * NF)
        down_done, scaled_ready = cnt("down_done", 2 * NF), cnt("scaled_ready", 4)
        y_ready = cnt("y_ready", 4)
        y_stored = [cnt(f"y_stored{i}", 16) for i in range(2)]

        def first(turn):
            return isinstance(turn, int) and turn == 0

        start_counters(nc, counters)
        block = ctx.enter_context(nc.Block())

        def parts_of(e, half):
            o = 2 * HID * e
            return w_in[:, :, half, o:o + 2 * HID], w_out[:, half, e * E:(e + 1) * E]

        @block.sync
        def _(sp):
            sp.dma_start(w_router[:], d["gate_w_t"].rearrange("(k p) e -> p k e", p=P)).then_inc(small_loaded, 16)
            sp.dma_start(lower[:], d["lower"].unsqueeze(0).broadcast_to([P, NE, NE])).then_inc(small_loaded, 16)

            def chunk_of_x1(turn, i):
                return d["x1"][bass.ds(turn, 1), i * CH:(i + 1) * CH, :].rearrange("o (t p) e -> p (o t) e", p=P)

            def front(turn, i):
                if not first(turn):
                    sp.wait_ge(xhat_ready.sem, xhat_ready.before(turn, CT * (i + 1) - 2 * CT))
                sp.sem_inc(ticks[0], 1)
                sp.dma_start(x1[:, i], chunk_of_x1(turn, i)).then_inc(x1_loaded[i].sem, 16)

            def load_residual(turn, i):
                sp.wait_ge(y_ready.sem, y_ready.at(turn, 2 * i))
                sp.sem_inc(ticks[0], 1)
                sp.dma_start(res[:, i], chunk_of_x1(turn, i)).then_inc(res_loaded[i].sem, 16)

            def combine_weights(turn, i):
                sp.wait_ge(ct_ready.sem, ct_ready.at(turn, i + 1))
                sp.dma_start(combine_d[i], combine_t[:]).then_inc(combine_stored.sem, 16)
                sp.wait_ge(combine_stored.sem, combine_stored.at(turn, 16 * (i + 1)))
                sp.sem_inc(ticks[0], 1)
                if not first(turn):
                    sp.wait_ge(weighed.sem, weighed.before(turn, NE * (i + 1) - 2 * NE))
                sp.dma_start(share[:, i], combine_d[i:i + 1].broadcast_to([P, NE, CH])).then_inc(
                    share_loaded[i].sem, 16)

            def store(turn, i):
                sp.wait_ge(y_ready.sem, y_ready.at(turn, 2 * i + 2))
                sp.sem_inc(ticks[0], 1)
                sp.dma_start(out[bass.ds(turn, 1), i * CH:(i + 1) * CH, :].rearrange("o (t p) e -> p (o t) e", p=P),
                             y[:, i]).then_inc(y_stored[i].sem, 16)

            front(0, 0)
            for e in range(NF):
                if e >= 4:
                    sp.wait_ge(w_lo, e - 3)
                o = 2 * HID * e
                sp.dma_start(staged[:, e % 4, 0:2, :], d["w_in_t"][:, :, o:o + 2 * HID].rearrange(
                    "k p n -> p k n")).then_inc(raw_loaded[e % 4], 16)
                sp.dma_start(staged[:, e % 4, 2, :], d["w_out_t"][:, e * E:(e + 1) * E]).then_inc(raw_loaded[e % 4], 16)
                if e == 0:
                    front(0, 1)
            combine_weights(0, 0)

            def turn_body(turn, last):
                load_residual(turn, 0)
                if not last:
                    front(turn + 1, 0)
                combine_weights(turn, 1)
                store(turn, 0)
                load_residual(turn, 1)
                if not last:
                    front(turn + 1, 1)
                    combine_weights(turn + 1, 0)
                store(turn, 1)

            with sp.Fori(0, B - 1) as t:
                turn_body(t, False)
            turn_body(B - 1, True)
            for i in range(2):
                sp.wait_ge(y_stored[i].sem, y_stored[i].at(B, 0))

        @block.gpsimd
        def _(pool):
            def front_1(turn, i):
                pool.wait_ge(var_ready.sem, var_ready.at(turn, i + 1))
                nc.gpsimd.tensor_tensor(rstd[:], rstd[:], neg_half[:], ALU.pow).then_inc(rstd_ready.sem, 1)

            def front_2(turn, i):
                pool.wait_ge(h_hi.sem, h_hi.at(turn, i + 1))
                nc.gpsimd.tensor_tensor(h_parts[:, i, 1], h_t[:], h_parts[:, i, 0].bitcast(F32),
                                        ALU.subtract).then_inc(h_lo.sem, 1)

            def weigh(turn, i, e):
                n, x_ = i * NF + e, e - 2
                pool.wait_ge(silu_ready.sem, silu_ready.at(turn, n + 1))
                if x_ == 0:
                    pool.wait_ge(share_loaded[i].sem, share_loaded[i].at(turn, 16))
                nc.gpsimd.tensor_tensor(act_g[:, n % 3, :], act_g[:, n % 3, :], share[:, i, x_, :],
                                        ALU.mult).then_inc(weighed.sem, 1)

            def lo_part(turn, i, e):
                n = i * NF + e
                pool.wait_ge(hid_hi.sem, hid_hi.at(turn, n + 1))
                pool.wait_ge(down_done.sem, down_done.at(turn, n - 2))
                nc.gpsimd.tensor_tensor(hid_parts[:, n % 3, 1, :], hidden[:, n % 2, :],
                                        hid_parts[:, n % 3, 0, :].bitcast(F32), ALU.subtract).then_inc(hid_lo.sem, 1)

            for e in range(NF):
                pool.wait_ge(w_hi, e + 1)
                for lo, hi, raw in ((parts_of(e, 1)[0], parts_of(e, 0)[0], staged[:, e % 4, 0:2, :]),
                                    (parts_of(e, 1)[1], parts_of(e, 0)[1], staged[:, e % 4, 2, :])):
                    last = nc.gpsimd.tensor_tensor(lo, raw, hi.bitcast(F32), ALU.subtract)
                last.then_inc(w_lo, 1)
                if e == 0:
                    front_1(0, 0)
                if e == 2:
                    front_2(0, 0)

            def turn_body(turn, last):
                for i in range(2):
                    nxt = (turn, 1) if i == 0 else (turn + 1, 0)
                    for e in range(NF):
                        if e >= 2:
                            weigh(turn, i, e)
                        if e >= 1:
                            lo_part(turn, i, e - 1)
                        if not (i and last):
                            if e == FRONT_AT[0]:
                                front_1(*nxt)
                            if e == FRONT_AT[1]:
                                front_2(*nxt)
                    lo_part(turn, i, NF - 1)

            with pool.Fori(0, B - 1) as t:
                turn_body(t, False)
            turn_body(B - 1, True)

        @block.scalar
        def _(act):
            def router_exp(turn, i):
                act.wait_ge(logit_t_done.sem, logit_t_done.at(turn, i + 1))
                act.wait_ge(combine_ready.sem, combine_ready.at(turn, i))
                nc.scalar.activation(ex[:], ps[:, FRONT_BANK + 1, 0:CT * NE].rearrange("p (t e) -> p t e", e=NE),
                                     ACT.Exp, scale=-1.0).then_inc(exp_ready.sem, 1)

            router_exp(0, 0)

            def turn_body(turn, last):
                for i in range(2):
                    nxt = (turn, 1) if i == 0 else (turn + 1, 0)
                    for e in range(NF):
                        n = i * NF + e
                        act.wait_ge(gu_done.sem, gu_done.at(turn, n + 1))
                        act.wait_ge(hid_ready.sem, hid_ready.at(turn, n - 2))
                        nc.scalar.activation(act_g[:, n % 3, :], ps[:, 2 * (n % 2), :],
                                             ACT.Silu).then_inc(silu_ready.sem, 1)
                        if e == FRONT_AT[2] and not (i and last):
                            router_exp(*nxt)

            with act.Fori(0, B - 1) as t:
                turn_body(t, False)
            turn_body(B - 1, True)

        @block.vector
        def _(dve):
            nc.vector.memset(neg_half[:], -0.5)

            def front_1(turn, i):
                if i == 0:
                    dve.wait_ge(ht_ready.sem, ht_ready.at(turn, 0))
                src = mod_all[:, turn:turn + 1] if isinstance(turn, int) else mod_all[:, bass.ds(turn, 1)]
                gsrc = gate_all[:, 1, turn:turn + 1] if isinstance(turn, int) else gate_all[:, 1, bass.ds(turn, 1)]
                nc.vector.tensor_copy(mod[:, i:i + 1], src)
                nc.vector.tensor_copy(gate[:, i:i + 1], gsrc).then_inc(mod_ready.sem, 1)
                dve.wait_ge(x1_loaded[i].sem, x1_loaded[i].at(turn, 16))
                for t in range(CT):
                    last = nc.vector.bn_stats(stats[:, t, :], x1[:, i, t, :])
                last.then_inc(chain.sem, 1)
                dve.wait_ge(chain.sem, chain.at(turn, CHAIN * i + 1))
                dve.sem_inc(ticks[2], 1)
                for t in range(CT):
                    last = nc.vector.bn_aggr(mean_var[:, t, :], stats[:, t, :])
                last.then_inc(chain.sem, 1)
                dve.wait_ge(chain.sem, chain.at(turn, CHAIN * i + 2))
                nc.vector.tensor_scalar(rstd[:], mean_var[:, :, 1], EPS, None, ALU.add).then_inc(var_ready.sem, 1)

            def front_2(turn, i):
                dve.wait_ge(rstd_ready.sem, rstd_ready.at(turn, i + 1))
                dve.wait_ge(xt_done.sem, xt_done.at(turn, 2 * i))
                for t in range(CT):
                    nc.vector.tensor_scalar(x_hat[:, t, :], x1[:, i, t, :], mean_var[:, t, 0:1], rstd[:, t:t + 1],
                                            ALU.subtract, ALU.mult).then_inc(xhat_ready.sem, 1)

            def front_3(turn, i):
                dve.wait_ge(mod_ready.sem, mod_ready.at(turn, i + 1))
                dve.wait_ge(h_lo.sem, h_lo.at(turn, i))
                dve.wait_ge(logit_done.sem, logit_done.at(turn, i))
                dve.wait_ge(xt_done.sem, xt_done.at(turn, 2 * i + 2))
                for f in range(2):
                    nc.vector.tensor_scalar(h_t[:, f, :], ps[:, FRONT_BANK + f, :], mod[:, i, 3, f:f + 1],
                                            mod[:, i, 2, f:f + 1], ALU.mult, ALU.add).then_inc(ht_ready.sem, 1)
                dve.wait_ge(ht_ready.sem, ht_ready.at(turn, 2 * i + 2))
                if not first(turn):
                    dve.wait_ge(gu_done.sem, gu_done.before(turn, NF * (i + 1) - 2 * NF))
                nc.vector.tensor_copy(h_parts[:, i, 0], h_t[:]).then_inc(h_hi.sem, 1)

            def front_4(turn, i):
                dve.wait_ge(logit_done.sem, logit_done.at(turn, i + 1))
                nc.vector.tensor_copy(logits_t[:], ps[0:NE, FRONT_BANK, :]).then_inc(logit_ready.sem, 1)

            def front_5(turn, i):
                dve.wait_ge(exp_ready.sem, exp_ready.at(turn, i + 1))
                nc.vector.tensor_scalar(prob[:], ex[:], 1.0, None, ALU.add).then_inc(chain.sem, 1)
                dve.wait_ge(chain.sem, chain.at(turn, CHAIN * i + 3))
                nc.vector.reciprocal(prob[:], prob[:]).then_inc(chain.sem, 1)
                dve.wait_ge(chain.sem, chain.at(turn, CHAIN * i + 4))
                mine = prob[:].unsqueeze(3).broadcast_to([P, CT, NE, NE])
                other = prob[:].unsqueeze(2).broadcast_to([P, CT, NE, NE])
                nc.vector.tensor_tensor(beats[:], other, mine, ALU.is_gt)
                nc.vector.tensor_tensor(ties[:], other, mine, ALU.is_equal).then_inc(chain.sem, 1)
                dve.wait_ge(chain.sem, chain.at(turn, CHAIN * i + 5))
                nc.vector.tensor_tensor(ties[:], ties[:], lower[:].unsqueeze(1).broadcast_to([P, CT, NE, NE]),
                                        ALU.mult).then_inc(chain.sem, 1)
                dve.wait_ge(chain.sem, chain.at(turn, CHAIN * i + 6))
                nc.vector.tensor_tensor(beats[:], beats[:], ties[:], ALU.add).then_inc(chain.sem, 1)
                dve.wait_ge(chain.sem, chain.at(turn, CHAIN * i + 7))
                nc.vector.tensor_reduce(rank[:], beats[:], AX.X, ALU.add).then_inc(chain.sem, 1)
                dve.wait_ge(chain.sem, chain.at(turn, CHAIN * i + 8))
                nc.vector.scalar_tensor_tensor(combine[:], rank[:], TOPK - 0.5, prob[:], ALU.is_lt, ALU.mult).then_inc(
                    chain.sem, 1)
                dve.wait_ge(chain.sem, chain.at(turn, CHAIN * i + 9))
                nc.vector.tensor_reduce(total[:], combine[:], AX.X, ALU.add).then_inc(chain.sem, 1)
                dve.wait_ge(chain.sem, chain.at(turn, CHAIN * i + 10))
                nc.vector.tensor_scalar(total[:], total[:], 1e-20, None, ALU.add).then_inc(chain.sem, 1)
                dve.wait_ge(chain.sem, chain.at(turn, CHAIN * i + 11))
                nc.vector.reciprocal(inv[:], total[:]).then_inc(chain.sem, 1)
                dve.wait_ge(chain.sem, chain.at(turn, CHAIN * i + 12))
                nc.vector.tensor_scalar(inv[:], inv[:], ROUTE_SCALE, None, ALU.mult).then_inc(chain.sem, 1)
                dve.wait_ge(chain.sem, chain.at(turn, CHAIN * i + 13))
                nc.vector.tensor_tensor(combine[:], combine[:], inv[:].unsqueeze(2).broadcast_to([P, CT, NE]),
                                        ALU.mult).then_inc(combine_ready.sem, 1)

            def front_6(turn, i):
                dve.wait_ge(ct_done.sem, ct_done.at(turn, i + 1))
                dve.wait_ge(combine_stored.sem, combine_stored.at(turn, 16 * i))
                nc.vector.tensor_copy(combine_t[:], ps[0:NE, FRONT_BANK, :]).then_inc(ct_ready.sem, 1)

            def hidden_tile(turn, i, e):
                n = i * NF + e
                dve.wait_ge(silu_ready.sem, silu_ready.at(turn, n + 1))
                dve.wait_ge(gu_done.sem, gu_done.at(turn, n + 1))
                if e >= 2:
                    dve.wait_ge(weighed.sem, weighed.at(turn, i * NE + e - 1))
                dve.wait_ge(hid_lo.sem, hid_lo.at(turn, n - 1))
                nc.vector.tensor_tensor(hidden[:, n % 2, :], ps[:, 2 * (n % 2) + 1, :], act_g[:, n % 3, :],
                                        ALU.mult).then_inc(hid_ready.sem, 1)
                dve.wait_ge(hid_ready.sem, hid_ready.at(turn, n + 1))
                dve.wait_ge(down_done.sem, down_done.at(turn, n - 2))
                nc.vector.tensor_copy(hid_parts[:, n % 3, 0, :], hidden[:, n % 2, :]).then_inc(hid_hi.sem, 1)

            def residual(turn, i):
                dve.wait_ge(down_done.sem, down_done.at(turn, NF * (i + 1)))
                dve.wait_ge(y_stored[i].sem, y_stored[i].at(turn, 0))
                dve.wait_ge(res_loaded[i].sem, res_loaded[i].at(turn, 16))
                for q in range(2):
                    k = 2 * i + q
                    dve.wait_ge(y_ready.sem, y_ready.at(turn, k))
                    nc.vector.tensor_tensor(scaled[:, q, :].rearrange("p (t e) -> p t e", e=E),
                                            ps[:, OUT_BANK + q, :].rearrange("p (t e) -> p t e", e=E),
                                            gate[:, i].unsqueeze(1).broadcast_to([P, 2, E]),
                                            ALU.mult).then_inc(scaled_ready.sem, 1)
                    dve.wait_ge(scaled_ready.sem, scaled_ready.at(turn, k + 1))
                    nc.vector.tensor_tensor(y[:, i, 2 * q:2 * q + 2, :], res[:, i, 2 * q:2 * q + 2, :],
                                            scaled[:, q, :].rearrange("p (t e) -> p t e", e=E),
                                            ALU.add).then_inc(y_ready.sem, 1)

            dve.wait_ge(small_loaded, 32)
            def split_weights(e):
                dve.wait_ge(raw_loaded[e % 4], 32 * (e // 4 + 1))
                w_in_hi, w_out_hi = parts_of(e, 0)
                nc.vector.tensor_copy(w_in_hi, staged[:, e % 4, 0:2, :])
                nc.vector.tensor_copy(w_out_hi, staged[:, e % 4, 2, :]).then_inc(w_hi, 1)

            front_1(0, 0)
            split_weights(0)
            front_2(0, 0)
            split_weights(1)
            front_3(0, 0)
            split_weights(2)
            front_4(0, 0)
            split_weights(3)
            front_5(0, 0)
            front_6(0, 0)
            for e in range(4, NF):
                split_weights(e)

            def turn_body(turn, last):
                for i in range(2):
                    nxt = (turn, 1) if i == 0 else (turn + 1, 0)
                    for e in range(NF):
                        if not (i and last):
                            if e == FRONT_AT[0]:
                                front_1(*nxt)
                            if e == FRONT_AT[0] + 1:
                                front_2(*nxt)
                            if e == FRONT_AT[1]:
                                front_3(*nxt)
                            if e == FRONT_AT[1] + 1:
                                front_4(*nxt)
                            if e == FRONT_AT[2] + 1:
                                front_5(*nxt)
                            if e == FRONT_AT[3] + 1:
                                front_6(*nxt)
                        hidden_tile(turn, i, e)
                        if i == 1 and e == LAG - 1:
                            residual(turn, 0)
                residual(turn, 1)

            with dve.Fori(0, B - 1) as t:
                turn_body(t, False)
            turn_body(B - 1, True)

        @block.tensor
        def _(pe):
            pe.wait_ge(small_loaded, 32)

            def front_transpose(turn, i):
                pe.wait_ge(ct_ready.sem, ct_ready.at(turn, i))
                for f in range(2):
                    for t in range(CT):
                        pe.wait_ge(xhat_ready.sem, xhat_ready.at(turn, CT * i + t + 1))
                        last = nc.tensor.transpose(ps[:, FRONT_BANK + f, t * P:(t + 1) * P],
                                                   x_hat[:, t, f * P:(f + 1) * P], ident[:])
                    last.then_inc(xt_done.sem, 1)

            def front_router(turn, i):
                pe.wait_ge(ht_ready.sem, ht_ready.at(turn, 2 * i + 2))
                for f in range(2):
                    last = nc.tensor.matmul(ps[0:NE, FRONT_BANK, :], w_router[:, f, :], h_t[:, f, :],
                                            start=(f == 0), stop=(f == 1))
                last.then_inc(logit_done.sem, 1)

            def front_logits(turn, i):
                pe.wait_ge(logit_ready.sem, logit_ready.at(turn, i + 1))
                pe.sem_inc(ticks[1], 1)
                for t in range(CT):
                    last = nc.tensor.transpose(ps[:, FRONT_BANK + 1, t * NE:(t + 1) * NE], logits_t[:, t * P:(t + 1) * P],
                                               ident[0:NE, 0:NE])
                last.then_inc(logit_t_done.sem, 1)

            def front_combine(turn, i):
                pe.wait_ge(combine_ready.sem, combine_ready.at(turn, i + 1))
                for t in range(CT):
                    last = nc.tensor.transpose(ps[0:NE, FRONT_BANK, t * P:(t + 1) * P], combine[:, t, :], ident[:])
                last.then_inc(ct_done.sem, 1)

            def products(dst, stationary, moving, start, stop):
                for k, (a, c) in enumerate(((0, 0), (0, 1), (1, 0))):
                    last = nc.tensor.matmul(dst, stationary(a), moving(c), start=start and k == 0, stop=stop and k == 2,
                                            skip_group_check=True)
                return last

            def gate_up(turn, i, e):
                n = i * NF + e
                if i == 0:
                    pe.wait_ge(w_lo, e + 1)
                if e == 0:
                    pe.wait_ge(h_hi.sem, h_hi.at(turn, i + 1))
                    pe.wait_ge(h_lo.sem, h_lo.at(turn, i + 1))
                pe.wait_ge(hid_ready.sem, hid_ready.at(turn, n - 1))
                for u in range(2):
                    for f in range(2):
                        o = (2 * e + u) * HID
                        last = products(ps[:, 2 * (n % 2) + u, :], lambda a: w_in[:, f, a, o:o + HID],
                                        lambda c: h_parts[:, i, c, f, :], f == 0, f == 1)
                last.then_inc(gu_done.sem, 1)

            def down(turn, i, e):
                n = i * NF + e
                if e == 0:
                    pe.wait_ge(scaled_ready.sem, scaled_ready.at(turn, 2 * i))
                pe.wait_ge(hid_hi.sem, hid_hi.at(turn, n + 1))
                pe.wait_ge(hid_lo.sem, hid_lo.at(turn, n + 1))
                for t in range(CT):
                    last = products(ps[:, OUT_BANK + t // 2, (t % 2) * E:(t % 2 + 1) * E],
                                    lambda a: hid_parts[:, n % 3, a, t * P:(t + 1) * P],
                                    lambda c: w_out[:, c, e * E:(e + 1) * E], e == 0 and t % 2 == 0,
                                    e == NF - 1)
                last.then_inc(down_done.sem, 1)

            front_transpose(0, 0)
            front_router(0, 0)
            front_logits(0, 0)
            front_combine(0, 0)

            def turn_body(turn, last):
                for i in range(2):
                    nxt = (turn, 1) if i == 0 else (turn + 1, 0)
                    for e in range(NF):
                        gate_up(turn, i, e)
                        if not (i and last):
                            if e == FRONT_AT[0] + 1:
                                front_transpose(*nxt)
                            if e == FRONT_AT[1]:
                                front_router(*nxt)
                            if e == FRONT_AT[2]:
                                front_logits(*nxt)
                            if e == FRONT_AT[3]:
                                front_combine(*nxt)
                        if e >= LAG:
                            down(turn, i, e - LAG)
                        elif i == 1:
                            down(turn, 0, NF - LAG + e)
                for e in range(NF - LAG, NF):
                    down(turn, 1, e)

            with pe.Fori(0, B - 1) as t:
                turn_body(t, False)
            turn_body(B - 1, True)


LAG = 2
CHAIN = 13
FRONT_AT = (2, 4, 6, 8)


def build(nc, ins, out):
    with ExitStack() as ctx:
        sb = lambda n, s, t=F32: ctx.enter_context(nc.sbuf_tensor(n, s, t))
        ident, causal_sb = sb("ident", [P, P]), sb("causal_sb", [P, 2, P])
        gate_all, mod_all = sb("gate_all", [P, 2, B, E]), sb("mod_all", [P, B, 4, 2])
        const_loaded = ctx.enter_context(nc.semaphore("const_loaded"))
        d = dict(ins)
        d["x1"] = nc.dram_tensor("x1", [B, S, E], F32, kind="Internal").ap()
        d["causal_sb"] = causal_sb
        with nc.Block() as block:
            @block.sync
            def _(sp):
                sp.dma_start(ident[:], d["ident"]).then_inc(const_loaded, 16)
                sp.dma_start(causal_sb[:], d["causal"].rearrange("a p n -> p a n")).then_inc(const_loaded, 16)
                sp.wait_ge(const_loaded, 32)
        stage_0(nc, d, gate_all, mod_all)
        stage_a(nc, d, ident, gate_all, mod_all)
        stage_b(nc, d, ident, gate_all, mod_all, out)


def kernel(**inputs):
    import concourse.bacc as bacc
    from concourse.bass_utils import run_bass_kernel_spmd

    a = {k.removeprefix("L0_").removeprefix("attn_").removeprefix("ffn_"): np.asarray(t) for k, t in inputs.items()}
    put = {n: a[n] for n in ("x", "wq", "bq", "wqc", "bqc", "wqr", "bqr", "wkv", "bkv", "wkr", "bkr", "wkc", "bkc",
                             "wv", "bv", "wo", "bo", "wmod")}
    put["cT"] = a["c"].T
    put["gate_w_t"] = a["gate_weight"].T
    w_g = np.concatenate([a["ws_gate"].reshape(2, HID, E), a["w_gate"]])
    w_u = np.concatenate([a["ws_up"].reshape(2, HID, E), a["w_up"]])
    w_in = np.stack([w_g, w_u], axis=1).transpose(3, 0, 1, 2).reshape(2, P, NF * 2 * HID)
    put["w_in_t"] = w_in
    w_d = np.concatenate([a["ws_down"].reshape(E, 2, HID).transpose(1, 2, 0), a["w_down"].transpose(0, 2, 1)])
    put["w_out_t"] = w_d.transpose(1, 0, 2).reshape(HID, NF * E)
    inv_freq = (np.float32(1) / np.float32(10000) ** (np.arange(0, DR, 2, dtype=np.float32) / np.float32(DR)))
    angle = (np.arange(S, dtype=np.float32)[:, None] * inv_freq[None, :]).T
    angle = np.concatenate([angle, angle]).astype(np.float32)
    put["cos"] = np.cos(angle)
    put["sin"] = np.sin(angle) * np.where(np.arange(DR) < DR // 2, 1, -1).astype(np.float32)[:, None]
    put["ident"] = np.eye(P, dtype=np.float32)
    later = np.arange(P)[None, :] > np.arange(P)[:, None]
    put["causal"] = np.where(np.stack([later, later.T]), np.float32(NEG), np.float32(0))
    put["lower"] = (np.arange(NE)[None, :] < np.arange(NE)[:, None]).astype(np.float32)

    nc = bacc.Bacc("TRN2", target_bir_lowering=False, num_devices=1)
    ins, arrays = {}, {}
    for n, t in put.items():
        t = np.ascontiguousarray(t)
        arrays["in_" + n] = t
        ins[n] = nc.dram_tensor("in_" + n, t.shape, mybir.dt.from_np(t.dtype), kind="ExternalInput").ap()
    out = nc.dram_tensor("out", [B, S, E], F32, kind="ExternalOutput").ap()
    build(nc, ins, out)
    r = run_bass_kernel_spmd(nc, [arrays], core_ids=[0])
    return np.asarray(r.results[0]["out"])
```

```python
from contextlib import ExitStack

import numpy as np
import concourse.bass as bass
from concourse import mybir

F32 = mybir.dt.float32
F32R = mybir.dt.float32r
BF16 = mybir.dt.bfloat16
ALU = mybir.AluOpType
ACT = mybir.ActivationFunctionType
AX = mybir.AxisListType

P = 128
B, S, E = 4, 1024, 256
H, HD = 16, 16
DR = 128
NT = S // P
BANK = 512
NC = S // BANK
CH = BANK
CT = CH // P
GH = 4
G = H // GH
SLOTS = 2
EPS = 1e-5
NEG = -3.0e38
NE, TOPK, HID = 8, 2, 128
NF = 2 + NE
ROUTE_SCALE = 2.5

PARTS = 4 * HD
ROWS = 96
ROWS_M = ROWS + 2

STEPS = [(c, j) for c in range(NC) for j in range((c + 1) * BANK // P)]
NS = len(STEPS)
UNITS = NS * GH
DIAG = [P * j >= BANK * c for c, j in STEPS]


def width(step):
    c, j = STEPS[step]
    return BANK * (c + 1) - max(BANK * c, P * j)


def first_query(step):
    c, j = STEPS[step]
    return max(BANK * c, P * j)


MAX_STEPS = 9
MAX_FROM = 3
XT_AT = ((G - 2, NS - 2),) * 2
HT_AT = ((G - 2, NS - 2),) * 2
LAT_AT, GELU_LAT_AT = (G - 2, NS - 1), (G - 1, 0)
QK_AT = [(G - 1, s) for s in (1, 1, 2, 3, 4, 5, 6, 7)]
GELU_QK_AT = [(G - 1, s) for s in (2, 2, 4, 4)]
ROPE_AT = [(G - 1, s) for s in (4, 5, 6, 7)]
LN_AT = ((1, MAX_STEPS + 1), (G - 2, 2))
LEAD = (4, 10)


def share_max_tiles():
    total = GH * sum(P * (i + 1) for i in range(NT))
    out = [[[] for _ in range(NS)] for _ in range(G)]
    for g in range(G - 1):
        steps = range(MAX_FROM if g else 0, MAX_STEPS)
        room = sum(width(s) for s in steps)
        tile, done, target = 0, 0, 0
        for s in steps:
            target += width(s) * total / room
            while tile < GH * NT and (done < target - 1 or s == steps[-1]):
                out[g][s].append(tile)
                done += P * (tile % NT + 1)
                tile += 1
    return out


MAX_IN_STEP = share_max_tiles()


def tiles_beside(t):
    rest = GH * NT - LEAD[1]
    return range(LEAD[1] + rest * t // NT, LEAD[1] + rest * (t + 1) // NT)


class Counter:

    def __init__(self, ctx, nc, name, per_turn):
        self.sem = ctx.enter_context(nc.semaphore(name))
        self.per_turn = per_turn

    def at(self, turn, k):
        return turn * self.per_turn + (max(k, 0) + 1)

    def before(self, turn, k):
        return turn * self.per_turn + (k + 1)


def start_counters(nc, counters):
    with nc.Block() as block:
        @block.sync
        def _(sp):
            for c in counters:
                sp.sem_inc(c.sem, 1)


def stage_0(nc, d, gate_all, mod_all):
    with ExitStack() as ctx:
        sb = lambda n, s, t=F32: ctx.enter_context(nc.sbuf_tensor(n, s, t))
        sem = lambda n: ctx.enter_context(nc.semaphore(n))
        ps = ctx.enter_context(nc.psum_tensor("ps_mod", [P, 8, BANK], F32))
        wmod = sb("wmod", [P, 2, 6 * E])
        cT = sb("cT", [P, 2, B])
        sT = sb("sT", [P, 2, B])
        s_wide = sb("s_wide", [P, 2, B, P])
        mag = sb("mag", [P, 2, E])
        sign2 = sb("sign2", [P, 2, E])
        loaded, silu_ready, wide_ready = sem("mod_loaded"), sem("silu_ready"), sem("wide_ready")
        cols_ready, rows_ready, gate_chain = sem("cols_ready"), sem("rows_ready"), sem("gate_chain")
        block = ctx.enter_context(nc.Block())

        @block.sync
        def _(sp):
            sp.dma_start(wmod[:], d["wmod"].rearrange("(k p) n -> p k n", p=P)).then_inc(loaded, 16)
            sp.dma_start(cT[:], d["cT"].rearrange("(k p) b -> p k b", p=P)).then_inc(loaded, 16)

        @block.scalar
        def _(act):
            act.wait_ge(loaded, 32)
            nc.scalar.activation(sT[:], cT[:], ACT.Silu).then_inc(silu_ready, 1)

        @block.tensor
        def _(pe):
            pe.wait_ge(silu_ready, 1)
            for m, part in enumerate((0, 1, 3, 4)):
                for f in range(2):
                    for k in range(2):
                        o = part * E + f * P
                        last = nc.tensor.matmul(ps[:, 0, (m * 2 + f) * B:(m * 2 + f + 1) * B], wmod[:, k, o:o + P],
                                                sT[:, k, :], start=(k == 0), stop=(k == 1))
            last.then_inc(cols_ready, 1)
            pe.wait_ge(wide_ready, 1)
            for b in range(B):
                for g, part in enumerate((2, 5)):
                    for k in range(2):
                        last = nc.tensor.matmul(ps[:, 1 + b, g * E:(g + 1) * E], s_wide[:, k, b, :],
                                                wmod[:, k, part * E:(part + 1) * E], start=(k == 0), stop=(k == 1))
                last.then_inc(rows_ready, 1)

        @block.vector
        def _(dve):
            dve.wait_ge(silu_ready, 1)
            nc.vector.tensor_copy(s_wide[:], sT[:].unsqueeze(3).broadcast_to([P, 2, B, P])).then_inc(wide_ready, 1)
            dve.wait_ge(cols_ready, 1)
            for m in range(4):
                src = ps[:, 0, m * 2 * B:(m + 1) * 2 * B].rearrange("p (f b) -> p b f", b=B)
                nc.vector.tensor_scalar(mod_all[:, :, m, :], src, float(m % 2), None, ALU.add)
            for b in range(B):
                dve.wait_ge(rows_ready, b + 1)
                row = ps[:, 1 + b, :].rearrange("p (g n) -> p g n", g=2)
                nc.vector.tensor_scalar(mag[:], row, -1.0, 0.25, ALU.mult, ALU.max).then_inc(gate_chain, 1)
                nc.vector.tensor_scalar(sign2[:], row, 0.0, 2.0, ALU.is_ge, ALU.mult).then_inc(gate_chain, 1)
                dve.wait_ge(gate_chain, 4 * b + 2)
                nc.vector.tensor_tensor(mag[:], row, mag[:], ALU.max).then_inc(gate_chain, 1)
                dve.wait_ge(gate_chain, 4 * b + 3)
                nc.vector.scalar_tensor_tensor(gate_all[:, :, b, :], sign2[:], -1.0, mag[:], ALU.add,
                                               ALU.mult).then_inc(gate_chain, 1)
                dve.wait_ge(gate_chain, 4 * b + 4)


def stage_a(nc, d, ident, gate_all, mod_all):
    with ExitStack() as ctx:
        sb = lambda n, s, t=F32: ctx.enter_context(nc.sbuf_tensor(n, s, t))
        sem = lambda n: ctx.enter_context(nc.semaphore(n))
        counters = []

        def cnt(name, per_turn):
            counters.append(Counter(ctx, nc, name, per_turn))
            return counters[-1]

        ps = ctx.enter_context(nc.psum_tensor("ps_attn", [P, 8, BANK], F32))

        score_bank = lambda slot: 2 * slot
        ST_BANK, OUT_BANK = 4, 6

        w_lat = sb("w_lat", [P, 2, 2 * 64])
        w_qr, w_kr = sb("w_qr", [P, 2, DR]), sb("w_kr", [P, 2, DR])
        w_c = sb("w_c", [P, 2, P])
        w_v = sb("w_v", [P, E])
        w_o = sb("w_o", [P, 2, E])
        bias = sb("bias", [P, 5])
        bv_row, bo_row = sb("bv_row", [P, E]), sb("bo_row", [P, E])
        cos_t, sin_t = sb("cos_t", [P, S]), sb("sin_t", [P, S])
        causal = sb("causal", [P, P], BF16)
        causal_t = sb("causal_t", [P, P], BF16)
        ident_b = sb("ident_b", [P, P], BF16)
        neg_half = sb("neg_half", [P, NT])
        pad = sb("pad", [P, 1])

        x = sb("x", [P, NT, E])
        x_hat = sb("x_hat", [P, NT, E])
        out_nat = sb("out_nat", [P, NT, E])
        out_t = sb("out_t", [P, 2, S])
        probs = sb("probs", [P, 2, GH, BANK])
        v = sb("v", [P, NT, H, 2 * HD])
        op_q, op_k = sb("op_q", [P, SLOTS, GH, S], F32R), sb("op_k", [P, SLOTS, GH, S], F32R)
        parts = sb("parts", [P, 2, 2, BANK])
        h_t = sb("h_t_a", [P, 2, S])
        rope = sb("rope", [P, 4, 2, BANK])
        latent = sb("latent", [P, S])
        raw = sb("raw", [P, 2, BANK])
        out_raw = sb("out_raw", [P, BANK])
        inv_sum = sb("inv_sum", [P, CT * GH])
        stats, mean_var = sb("stats", [P, NT, 6]), sb("mean_var", [P, NT, 2])
        rstd = sb("rstd", [P, NT])
        neg_max, neg_max_parts = sb("neg_max", [P, GH * NT]), sb("neg_max_parts", [P, 2, GH * NT])
        max_rows = sb("max_rows", [2 * GH * NT, P])
        mod = sb("mod", [P, 4, 2])
        gate, gate_bias = sb("gate", [P, E]), sb("gate_bias", [P, E])
        proj = sb("proj", [P, 2, E])

        scratch = nc.dram_tensor("qk_parts", [2, 2, E, S], F32, kind="Internal").ap()

        w_loaded, w_set = sem("w_loaded"), sem("w_set")
        pads_set = sem("pads_set")
        pool_set = sem("pool_set")
        ticks = [sem(f"tick_a{i}") for i in range(4)]
        res_loaded = cnt("res_loaded", 16)
        x_loaded, stats_chain = cnt("x_loaded", 16), cnt("stats_chain", 2)
        mod_ready, gate_ready = cnt("mod_ready", 1), cnt("gate_ready", 1)
        var_ready, rstd_ready, xhat_ready = cnt("var_ready", 1), cnt("rstd_ready", 1), cnt("xhat_ready", NT)
        xt_done, ht_ready = cnt("xt_done", 4), cnt("ht_ready", 4)
        lat_done, lat_ready = cnt("lat_done", NC), cnt("lat_ready", NC)
        qk_done, raw_ready = cnt("qk_done", 8), cnt("raw_ready", 8)
        rope_terms, rope_ready = cnt("rope_terms", 8), cnt("rope_ready", 4)
        lo_ready = cnt("lo_ready", 8)
        parts_stored = [cnt(f"parts_stored{i}", 64) for i in range(2)]
        ops_loaded = [cnt(f"ops_loaded{s}", 256) for s in range(SLOTS)]
        v_done, v_ready = cnt("v_done", NT), cnt("v_ready", NT)
        score_done, max_done = cnt("score_done", G * GH * NT), cnt("max_done", G * GH * NT)
        m_chain, m_split = cnt("m_chain", G), cnt("m_split", G)
        mt_done, mt_ready, m_loaded = cnt("mt_done", G), cnt("mt_ready", G), cnt("m_loaded", 32 * G)
        st_done, prob_ready = cnt("st_done", G * UNITS), cnt("prob_ready", G * UNITS)
        pv_done = cnt("pv_done", G * NS)
        raw_out_ready, raw_out_turned = cnt("raw_out_ready", G * NC), cnt("raw_out_turned", G * NC)
        inv_ready, out_ready = cnt("inv_ready", G * NC), cnt("out_ready", G * NC)
        out_turned, out_t_ready = cnt("out_turned", 2 * NC), cnt("out_t_ready", 2 * NC)
        gate_bias_ready, xb_ready = cnt("gate_bias_ready", 1), cnt("xb_ready", 1)
        proj_done, proj_scaled, x1_ready = cnt("proj_done", NT), cnt("proj_scaled", NT), cnt("x1_ready", NT)
        x1_stored = cnt("x1_stored", 16)

        N_WLOAD = 8 + 2 + 4 + 2 + 2

        def first(turn):
            return isinstance(turn, int) and turn == 0

        start_counters(nc, counters)
        block = ctx.enter_context(nc.Block())

        @block.sync
        def _(sp):
            sp.wait_ge(w_set, 1)

            def load(dst, src):
                sp.dma_start(dst, src).then_inc(w_loaded, 16)

            load(w_lat[:, :, 0:64], d["wq"].rearrange("(k p) n -> p k n", p=P))
            load(w_lat[:, :, 64:128], d["wkv"].rearrange("(k p) n -> p k n", p=P))
            load(w_qr[:], d["wqr"].rearrange("(k p) n -> p k n", p=P))
            load(w_kr[:], d["wkr"].rearrange("(k p) n -> p k n", p=P))
            load(w_c[0:64, 0, :], d["wqc"])
            load(w_c[64:128, 1, :], d["wkc"])
            load(w_v[64:128, :], d["wv"])
            load(w_o[:], d["wo"].rearrange("(k p) n -> p k n", p=P))
            load(bias[0:64, 0:1], d["bq"].unsqueeze(1))
            load(bias[64:128, 0:1], d["bkv"].unsqueeze(1))
            for i, n in enumerate(("bqc", "bkc", "bqr", "bkr")):
                load(bias[:, 1 + i:2 + i], d[n].unsqueeze(1))
            load(bv_row[:], d["bv"].unsqueeze(0).broadcast_to([P, E]))
            load(bo_row[:], d["bo"].unsqueeze(0).broadcast_to([P, E]))
            load(cos_t[:], d["cos"])
            load(sin_t[:], d["sin"])

            sp.dma_start(x_hat[:], d["x"][0:1].rearrange("o (t p) e -> p (o t) e", p=P)).then_inc(x_loaded.sem, 16)

            def store_parts(turn, n):
                kind, c = qk_item(n)
                sp.wait_ge(lo_ready.sem, lo_ready.at(turn, n + 1))
                sp.sem_inc(ticks[2], 1)
                if n == 0:
                    for s in range(SLOTS):
                        sp.wait_ge(ops_loaded[s].sem, ops_loaded[s].at(turn, 0))
                        sp.sem_inc(ticks[2], 1)
                dst = scratch[kind % 2, :, P * (kind // 2):P * (kind // 2) + P, c * BANK:(c + 1) * BANK]
                sp.dma_start(dst.rearrange("a p s -> p a s"), parts[:, n % 2]).then_inc(parts_stored[n % 2].sem, 16)

            def load_operands(g):
                slot = g % SLOTS
                features = slice(g * GH * HD, (g + 1) * GH * HD)
                for n in range(2 * 2):
                    rows = slice(HD * n, HD * (n + 1))
                    k_src = scratch[1, n % 2, features, :].rearrange("(h d) s -> d h s", d=HD)
                    q_src = scratch[0, n // 2, features, :].rearrange("(h d) s -> d h s", d=HD)
                    sp.dma_start(op_k[rows, slot, :, :].bitcast(F32), k_src).then_inc(ops_loaded[slot].sem, 16)
                    sp.dma_start(op_q[rows, slot, :, :].bitcast(F32), q_src).then_inc(ops_loaded[slot].sem, 16)

            def load_max_rows(turn, g):
                sp.wait_ge(mt_ready.sem, mt_ready.at(turn, g + 1))
                n = GH * NT
                for r in range(2):
                    dst = op_q[ROWS + r:ROWS + r + 1, g % SLOTS, :, :].bitcast(F32)
                    sp.dma_start(dst.rearrange("p h (t s) -> p (h t) s", s=P), max_rows[n * r:n * r + n, :]).then_inc(
                        m_loaded.sem, 16)

            def parts_out(turn):
                for n in range(4):
                    store_parts(turn, n)
                for i in range(2):
                    sp.wait_ge(parts_stored[i].sem, parts_stored[i].at(turn, 32))
                    sp.sem_inc(ticks[2], 1)
                if not first(turn):
                    sp.wait_ge(st_done.sem, st_done.before(turn, -UNITS))
                sp.sem_inc(ticks[2], 1)
                load_operands(0)
                sp.wait_ge(st_done.sem, st_done.at(turn, 0))
                sp.sem_inc(ticks[2], 1)
                load_operands(1)
                for n in range(4, 8):
                    store_parts(turn, n)

            def image(turn, last):
                load_max_rows(turn, 0)
                sp.wait_ge(x1_stored.sem, x1_stored.at(turn, 0))
                sp.sem_inc(ticks[2], 1)
                sp.dma_start(x[:], d["x"][bass.ds(turn, 1)].rearrange("o (t p) e -> p (o t) e", p=P)).then_inc(
                    res_loaded.sem, 16)
                if not last:
                    sp.wait_ge(xt_done.sem, xt_done.at(turn, 4))
                    sp.sem_inc(ticks[2], 1)
                    sp.dma_start(x_hat[:], d["x"][bass.ds(turn + 1, 1)].rearrange(
                        "o (t p) e -> p (o t) e", p=P)).then_inc(x_loaded.sem, 16)
                load_max_rows(turn, 1)
                for i in range(2):
                    sp.wait_ge(parts_stored[i].sem, parts_stored[i].at(turn, 64))
                    sp.sem_inc(ticks[2], 1)
                for g in range(2, G):
                    sp.wait_ge(st_done.sem, st_done.at(turn, UNITS * (g - 1)))
                    sp.sem_inc(ticks[2], 1)
                    load_operands(g)
                    load_max_rows(turn, g)
                if not last:
                    parts_out(turn + 1)
                sp.wait_ge(x1_ready.sem, x1_ready.at(turn, NT))
                sp.sem_inc(ticks[2], 1)
                sp.dma_start(d["x1"][bass.ds(turn, 1)].rearrange("o (t p) e -> p (o t) e", p=P), x[:]).then_inc(
                    x1_stored.sem, 16)

            parts_out(0)
            with sp.Fori(0, B - 1) as b:
                image(b, False)
            image(B - 1, True)
            sp.wait_ge(x1_stored.sem, x1_stored.at(B, 0))

        @block.gpsimd
        def _(pool):
            nc.gpsimd.memset(op_q[PARTS:ROWS, 0].bitcast(F32), 0.0).then_inc(pool_set, 1)
            pool.wait_ge(pool_set, 1)
            nc.gpsimd.memset(v[:], 1.0).then_inc(pool_set, 1)
            pool.wait_ge(pool_set, 2)
            pool.wait_ge(w_set, 1)

            def inverse_deviation(turn):
                pool.wait_ge(var_ready.sem, var_ready.at(turn, 1))
                nc.gpsimd.tensor_tensor(rstd[:], rstd[:], neg_half[:], ALU.pow).then_inc(rstd_ready.sem, 1)

            def lo_part(turn, n):
                pool.wait_ge(raw_ready.sem, raw_ready.at(turn, n + 1))
                nc.gpsimd.tensor_tensor(parts[:, n % 2, 1, :].bitcast(F32R), raw[:, n % 2, :], parts[:, n % 2, 0, :],
                                        ALU.subtract).then_inc(lo_ready.sem, 1)

            def rope_sum(turn, r):
                pool.wait_ge(rope_terms.sem, rope_terms.at(turn, 2 * r + 2))
                nc.gpsimd.tensor_tensor(rope[:, r, 0, :], rope[:, r, 0, :], rope[:, r, 1, :],
                                        ALU.add).then_inc(rope_ready.sem, 1)

            def image(turn, last):
                pool.wait_ge(gate_ready.sem, gate_ready.at(turn, 1))
                nc.gpsimd.tensor_tensor(gate_bias[:], gate[:], bo_row[:], ALU.mult).then_inc(gate_bias_ready.sem, 1)
                pool.wait_ge(gate_bias_ready.sem, gate_bias_ready.at(turn, 1))
                pool.wait_ge(res_loaded.sem, res_loaded.at(turn, 16))
                nc.gpsimd.tensor_tensor(x[:], x[:], gate_bias[:].unsqueeze(1).broadcast_to([P, NT, E]),
                                        ALU.add).then_inc(xb_ready.sem, 1)
                if not last:
                    inverse_deviation(turn + 1)
                    for n in range(4):
                        lo_part(turn + 1, n)
                    for r in range(4):
                        rope_sum(turn + 1, r)
                    lo_part(turn + 1, 4)
                    lo_part(turn + 1, 5)
                pool.wait_ge(xb_ready.sem, xb_ready.at(turn, 1))
                for t in range(NT):
                    pool.wait_ge(proj_scaled.sem, proj_scaled.at(turn, t + 1))
                    nc.gpsimd.tensor_tensor(x[:, t, :], x[:, t, :], proj[:, t % 2, :], ALU.add).then_inc(
                        x1_ready.sem, 1)
                if not last:
                    lo_part(turn + 1, 6)
                    lo_part(turn + 1, 7)

            inverse_deviation(0)
            for n in range(4):
                lo_part(0, n)
            for r in range(4):
                rope_sum(0, r)
            for n in range(4, 8):
                lo_part(0, n)
            with pool.Fori(0, B - 1) as b:
                image(b, False)
            image(B - 1, True)

        @block.scalar
        def _(act):
            act.wait_ge(w_set, 2)
            n = SLOTS * GH * S
            nc.scalar.activation(op_k[PARTS:ROWS_M].rearrange("p a h s -> p (a h s)"),
                                 pad[PARTS:ROWS_M].broadcast_to([ROWS_M - PARTS, n]), ACT.Copy).then_inc(pads_set, 1)
            n = (SLOTS - 1) * GH * S
            nc.scalar.activation(op_q[PARTS:ROWS, 1:SLOTS].rearrange("p a h s -> p (a h s)"),
                                 pad[PARTS:ROWS].broadcast_to([ROWS - PARTS, n]), ACT.Copy).then_inc(pads_set, 1)
            act.wait_ge(w_loaded, 16 * N_WLOAD)

            def evacuate_x(turn, c):
                if c == 0:
                    act.wait_ge(mod_ready.sem, mod_ready.at(turn, 1))
                    act.wait_ge(qk_done.sem, qk_done.at(turn, 0))
                for f in range(2):
                    act.wait_ge(xt_done.sem, xt_done.at(turn, 2 * c + f + 1))
                    nc.scalar.activation(h_t[:, f, c * BANK:(c + 1) * BANK], ps[:, 2 * c + f, :], ACT.Identity,
                                         bias=mod[:, 0, f:f + 1], scale=mod[:, 1, f:f + 1]).then_inc(ht_ready.sem, 1)

            def gelu_latents(turn):
                act.wait_ge(v_done.sem, v_done.at(turn, 0))
                for c in range(NC):
                    act.wait_ge(lat_done.sem, lat_done.at(turn, c + 1))
                    nc.scalar.activation(latent[:, c * BANK:(c + 1) * BANK], ps[:, c, :], ACT.Gelu,
                                         bias=bias[:, 0:1]).then_inc(lat_ready.sem, 1)

            def gelu_qk(turn, n):
                kind, c = qk_item(n)
                if n < 4:
                    act.wait_ge(qk_done.sem, qk_done.at(turn, n + 1))
                    src, col = ps[:, n % 4, :], bias[:, 1 + kind:2 + kind]
                else:
                    act.wait_ge(rope_ready.sem, rope_ready.at(turn, n - 3))
                    src, col = rope[:, n - 4, 0, :], 0.0
                act.wait_ge(parts_stored[n % 2].sem, parts_stored[n % 2].at(turn, 16 * (n // 2)))
                nc.scalar.activation(parts[:, n % 2, 0, :].bitcast(F32R), src, ACT.Gelu, bias=col)
                act.wait_ge(lo_ready.sem, lo_ready.at(turn, n - 1))
                nc.scalar.activation(raw[:, n % 2, :], src, ACT.Gelu, bias=col).then_inc(raw_ready.sem, 1)

            def copy_out(turn, g, c):
                act.wait_ge(pv_done.sem, pv_done.at(turn, g * NS + (CT if c == 0 else NS)))
                act.wait_ge(raw_out_turned.sem, raw_out_turned.at(turn, g * NC + c))
                nc.scalar.activation(out_raw[:], ps[:, OUT_BANK + c, :], ACT.Copy).then_inc(raw_out_ready.sem, 1)

            def evacuate_out(turn, c):
                if c == 0:
                    act.wait_ge(proj_done.sem, proj_done.at(turn, 0))
                for f in range(2):
                    act.wait_ge(out_turned.sem, out_turned.at(turn, 2 * c + f + 1))
                    nc.scalar.activation(out_t[:, f, c * BANK:(c + 1) * BANK], ps[:, OUT_BANK + f, :],
                                         ACT.Copy).then_inc(out_t_ready.sem, 1)

            def image(turn, last):
                for g in range(G):
                    for s in range(NS):
                        n = g * NS + s
                        for h in range(GH):
                            u = GH * n + h
                            act.wait_ge(st_done.sem, st_done.at(turn, u + 1))
                            if h == 0:
                                act.wait_ge(pv_done.sem, pv_done.at(turn, n - 1))
                            w = width(s)
                            nc.scalar.activation(probs[:, n % 2, h, 0:w], ps[:, ST_BANK + u % 2, 0:w], ACT.Exp,
                                                 scale=float(HD) ** -0.5).then_inc(prob_ready.sem, 1)
                        if s == 1 and g > 0:
                            copy_out(turn, g - 1, 1)
                        if s == 5:
                            copy_out(turn, g, 0)
                        if not last:
                            for c in range(NC):
                                if HT_AT[c] == (g, s):
                                    evacuate_x(turn + 1, c)
                            if GELU_LAT_AT == (g, s):
                                gelu_latents(turn + 1)
                            for n in range(4):
                                if GELU_QK_AT[n] == (g, s):
                                    gelu_qk(turn + 1, n)
                copy_out(turn, G - 1, 1)
                if not last:
                    gelu_qk(turn + 1, 4)
                    gelu_qk(turn + 1, 5)
                for c in range(NC):
                    evacuate_out(turn, c)
                if not last:
                    gelu_qk(turn + 1, 6)
                    gelu_qk(turn + 1, 7)

            for c in range(NC):
                evacuate_x(0, c)
            gelu_latents(0)
            for n in range(8):
                gelu_qk(0, n)
            with act.Fori(0, B - 1) as b:
                image(b, False)
            image(B - 1, True)

        @block.vector
        def _(dve):
            nc.vector.memset(w_c[:], 0.0)
            nc.vector.memset(w_v[:], 0.0)
            nc.vector.memset(neg_half[:], -0.5)
            nc.vector.memset(pad[:], 0.0).then_inc(w_set, 1)
            dve.wait_ge(w_set, 1)
            nc.vector.memset(pad[ROWS:ROWS_M], 1.0).then_inc(w_set, 1)

            def layer_norm(turn):
                dve.wait_ge(x_loaded.sem, x_loaded.at(turn, 16))
                for t in range(NT):
                    last = nc.vector.bn_stats(stats[:, t, :], x_hat[:, t, :])
                last.then_inc(stats_chain.sem, 1)
                dve.wait_ge(stats_chain.sem, stats_chain.at(turn, 1))
                dve.sem_inc(ticks[3], 1)
                for t in range(NT):
                    last = nc.vector.bn_aggr(mean_var[:, t, :], stats[:, t, :])
                last.then_inc(stats_chain.sem, 1)
                dve.wait_ge(stats_chain.sem, stats_chain.at(turn, 2))
                nc.vector.tensor_scalar(rstd[:], mean_var[:, :, 1], EPS, None, ALU.add).then_inc(var_ready.sem, 1)

            def normalise_input(turn):
                dve.wait_ge(rstd_ready.sem, rstd_ready.at(turn, 1))
                for t in range(NT):
                    nc.vector.tensor_scalar(x_hat[:, t, :], x_hat[:, t, :], mean_var[:, t, 0:1], rstd[:, t:t + 1],
                                            ALU.subtract, ALU.mult).then_inc(xhat_ready.sem, 1)

            layer_norm(0)
            nc.vector.tensor_copy(causal[:], d["causal_sb"][:, 0, :])
            nc.vector.tensor_copy(causal_t[:], d["causal_sb"][:, 1, :])
            nc.vector.tensor_copy(ident_b[:], ident[:]).then_inc(w_set, 1)
            normalise_input(0)
            dve.wait_ge(w_loaded, 16 * N_WLOAD)

            def load_mod(turn):
                dve.wait_ge(ht_ready.sem, ht_ready.at(turn, 0))
                nc.vector.tensor_copy(mod[:].unsqueeze(1), mod_all[:, bass.ds(turn, 1), :, :]).then_inc(mod_ready.sem, 1)

            def rope_mult(turn, r):
                n = 4 + r
                kind, c = qk_item(n)
                dve.wait_ge(qk_done.sem, qk_done.at(turn, n + 1))
                if r == 0:
                    dve.wait_ge(raw_ready.sem, raw_ready.at(turn, 0))
                cols = slice(c * BANK, (c + 1) * BANK)
                y, bcol = ps[:, n % 4, :], bias[:, 1 + kind:2 + kind]
                nc.vector.scalar_tensor_tensor(rope[:, r, 0, :], y, bcol, cos_t[:, cols], ALU.add, ALU.mult)
                for lo, hi in ((0, 64), (64, 0)):
                    nc.vector.scalar_tensor_tensor(rope[hi:hi + 64, r, 1, :], y[lo:lo + 64], bcol[lo:lo + 64],
                                                   sin_t[lo:lo + 64, cols], ALU.add,
                                                   ALU.mult).then_inc(rope_terms.sem, 1)

            def add_value_bias(turn, t):
                if t == 0:
                    dve.wait_ge(pv_done.sem, pv_done.at(turn, 0))
                dve.wait_ge(v_done.sem, v_done.at(turn, t + 1))
                src = ps[:, OUT_BANK + t % 2, 0:E].rearrange("p (h e) -> p h e", e=HD)
                nc.vector.tensor_tensor(v[:, t, :, 0:HD], src, bv_row[:].rearrange("p (h e) -> p h e", e=HD),
                                        ALU.add).then_inc(v_ready.sem, 1)

            def row_max(turn, g, tile):
                t = g * GH * NT + tile
                dve.wait_ge(score_done.sem, score_done.at(turn, t + 1))
                w = P * (tile % NT + 1)
                bank = score_bank(tile % 2)
                src = ps[:, bank:bank + 2, :].rearrange("p a n -> p (a n)")[:, 0:w]
                nc.vector.tensor_reduce(neg_max[:, tile:tile + 1], src, AX.X, ALU.max,
                                        negate=True).then_inc(max_done.sem, 1)

            def split_max(turn, g):
                dve.wait_ge(max_done.sem, max_done.at(turn, GH * NT * (g + 1)))
                nc.vector.tensor_copy(neg_max_parts[:, 0, :].bitcast(F32R), neg_max[:]).then_inc(m_chain.sem, 1)
                dve.wait_ge(m_chain.sem, m_chain.at(turn, g + 1))
                nc.vector.tensor_tensor(neg_max_parts[:, 1, :].bitcast(F32R), neg_max[:], neg_max_parts[:, 0, :],
                                        ALU.subtract).then_inc(m_split.sem, 1)

            def max_to_rows(turn, g):
                dve.wait_ge(mt_done.sem, mt_done.at(turn, g + 1))
                dve.wait_ge(m_loaded.sem, m_loaded.at(turn, 32 * g))
                nc.vector.tensor_copy(max_rows[:], ps[0:2 * GH * NT, 0, 0:P]).then_inc(mt_ready.sem, 1)

            def normalise(turn, g, c):
                n = g * NC + c
                dve.wait_ge(raw_out_turned.sem, raw_out_turned.at(turn, n + 1))
                src = ps[:, OUT_BANK + c, :].rearrange("p (t h e) -> p t h e", h=GH, e=2 * HD)
                inv = inv_sum[:].rearrange("p (t h) -> p t h", h=GH)
                if n == 0:
                    dve.wait_ge(out_turned.sem, out_turned.at(turn, 0))
                dve.wait_ge(out_ready.sem, out_ready.at(turn, n))
                nc.vector.reciprocal(inv, src[:, :, :, HD]).then_inc(inv_ready.sem, 1)
                dve.wait_ge(inv_ready.sem, inv_ready.at(turn, n + 1))
                for t in range(CT):
                    dst = out_nat[:, c * CT + t, g * GH * HD:(g + 1) * GH * HD].rearrange("p (h e) -> p h e", e=HD)
                    last = nc.vector.tensor_tensor(dst, src[:, t, :, 0:HD],
                                                   inv[:, t, :].unsqueeze(2).broadcast_to([P, GH, HD]), ALU.mult)
                last.then_inc(out_ready.sem, 1)

            def project_out(turn, t):
                dve.wait_ge(proj_done.sem, proj_done.at(turn, t + 1))
                dve.wait_ge(x1_ready.sem, x1_ready.at(turn, t - 1))
                nc.vector.tensor_tensor(proj[:, t % 2, :], ps[:, ST_BANK + t % 2, 0:E], gate[:], ALU.mult).then_inc(
                    proj_scaled.sem, 1)

            def image(turn, last):
                dve.wait_ge(gate_bias_ready.sem, gate_bias_ready.at(turn, 0))
                nc.vector.tensor_copy(gate[:].unsqueeze(1), gate_all[:, 0, bass.ds(turn, 1), :]).then_inc(
                    gate_ready.sem, 1)
                for g in range(G):
                    for s in range(NS):
                        if g + 1 < G and s == MAX_STEPS:
                            max_to_rows(turn, g + 1)
                        for tile in MAX_IN_STEP[g][s]:
                            row_max(turn, g + 1, tile)
                        if g + 1 < G and s + 1 == MAX_STEPS:
                            split_max(turn, g + 1)
                        if s == 3 and g > 0:
                            normalise(turn, g - 1, 1)
                        if s == 7:
                            normalise(turn, g, 0)
                        if not last:
                            if (g, s) == LN_AT[0]:
                                layer_norm(turn + 1)
                                load_mod(turn + 1)
                            if (g, s) == LN_AT[1]:
                                normalise_input(turn + 1)
                            for r in range(4):
                                if ROPE_AT[r] == (g, s):
                                    rope_mult(turn + 1, r)
                first_lead, lead = (0, 0) if last else LEAD
                for tile in range(first_lead):
                    row_max(turn + 1, 0, tile)
                normalise(turn, G - 1, 1)
                for tile in range(first_lead, lead):
                    row_max(turn + 1, 0, tile)
                for t in range(NT):
                    project_out(turn, t)
                    if not last:
                        add_value_bias(turn + 1, t)
                        for tile in tiles_beside(t):
                            row_max(turn + 1, 0, tile)
                if not last:
                    split_max(turn + 1, 0)
                    max_to_rows(turn + 1, 0)

            load_mod(0)
            for r in range(4):
                rope_mult(0, r)
            for t in range(NT):
                add_value_bias(0, t)
            for tile in range(GH * NT):
                row_max(0, 0, tile)
            split_max(0, 0)
            max_to_rows(0, 0)
            with dve.Fori(0, B - 1) as b:
                image(b, False)
            image(B - 1, True)

        @block.tensor
        def _(pe):
            pe.wait_ge(w_loaded, 16 * N_WLOAD)
            pe.wait_ge(w_set, 3)
            pe.wait_ge(pads_set, 2)
            pe.wait_ge(pool_set, 2)

            def transpose_x(turn, c):
                pe.wait_ge(mt_ready.sem, mt_ready.at(turn, 0))
                for t in range(c * CT, (c + 1) * CT):
                    pe.wait_ge(xhat_ready.sem, xhat_ready.at(turn, t + 1))
                    for f in range(2):
                        o = P * (t % CT)
                        last = nc.tensor.transpose(ps[:, 2 * c + f, o:o + P], x_hat[:, t, f * P:(f + 1) * P], ident[:])
                        if t % CT == CT - 1:
                            last.then_inc(xt_done.sem, 1)

            def latents(turn, c):
                pe.wait_ge(ht_ready.sem, ht_ready.at(turn, 2 * c + 2))
                for f in range(2):
                    last = nc.tensor.matmul(ps[:, c, :], w_lat[:, f, :], h_t[:, f, c * BANK:(c + 1) * BANK],
                                            start=(f == 0), stop=(f == 1))
                last.then_inc(lat_done.sem, 1)

            def features(turn, n):
                kind, c = qk_item(n)
                cols = slice(c * BANK, (c + 1) * BANK)
                if n < 4:
                    pe.wait_ge(lat_ready.sem, lat_ready.at(turn, 2))
                    pe.wait_ge(ht_ready.sem, ht_ready.at(turn, 4))
                    last = nc.tensor.matmul(ps[:, n % 4, :], w_c[:, kind, :], latent[:, cols], start=True, stop=True)
                else:
                    pe.wait_ge(raw_ready.sem, raw_ready.at(turn, n - 3))
                    w = (w_qr, w_kr)[kind - 2]
                    for f in range(2):
                        last = nc.tensor.matmul(ps[:, n % 4, :], w[:, f, :], h_t[:, f, cols],
                                                start=(f == 0), stop=(f == 1))
                last.then_inc(qk_done.sem, 1)

            def values(turn, t):
                if t == 0:
                    pe.wait_ge(out_t_ready.sem, out_t_ready.at(turn, 0))
                pe.wait_ge(v_ready.sem, v_ready.at(turn, t - 1))
                nc.tensor.matmul(ps[:, OUT_BANK + t % 2, 0:E], latent[:, t * P:(t + 1) * P], w_v[:],
                                 start=True, stop=True).then_inc(v_done.sem, 1)

            def scores(turn, g, tile):
                h, i, slot, t = tile // NT, tile % NT, g % SLOTS, g * GH * NT + tile
                if tile == 0:
                    pe.wait_ge(ops_loaded[slot].sem, ops_loaded[slot].at(turn, 128 * (g // SLOTS + 1)))
                if tile < 2:
                    if g == 0:
                        pe.wait_ge(rope_terms.sem, rope_terms.at(turn, 8))
                    else:
                        pe.wait_ge(mt_ready.sem, mt_ready.at(turn, g))
                pe.wait_ge(max_done.sem, max_done.at(turn, t - 1))
                bank = score_bank(tile % 2)
                q = op_q[0:ROWS, slot, h, i * P:(i + 1) * P]
                for k0 in range(0, P * (i + 1), BANK):
                    k1 = min(k0 + BANK, P * (i + 1))
                    last_piece = k1 == P * (i + 1)
                    nc.tensor.matmul(ps[:, bank + k0 // BANK, 0:k1 - k0], q, op_k[0:ROWS, slot, h, k0:k1],
                                     start=True, stop=not last_piece)
                o = P * i % BANK
                nc.tensor.matmul(ps[:, bank + P * i // BANK, o:o + P], ident_b[:], causal[:], start=False,
                                 stop=True).then_inc(score_done.sem, 1)

            def transpose_max(turn, g):
                pe.wait_ge(m_split.sem, m_split.at(turn, g + 1))
                pe.sem_inc(ticks[1], 1)
                nc.tensor.transpose(ps[0:2 * GH * NT, 0, 0:P],
                                    neg_max_parts[:].rearrange("p a n -> p (a n)"), ident[:]).then_inc(
                                        mt_done.sem, 1)

            def scores_t(turn, g, s, h):
                c, j = STEPS[s]
                slot, u = g % SLOTS, (g * NS + s) * GH + h
                if s == 0 and h == 0:
                    pe.wait_ge(m_loaded.sem, m_loaded.at(turn, 32 * (g + 1)))
                    if g == 0:
                        pe.wait_ge(proj_scaled.sem, proj_scaled.at(turn, 0))
                pe.wait_ge(prob_ready.sem, prob_ready.at(turn, u - 1))
                q0, w = first_query(s), width(s)
                last = nc.tensor.matmul(ps[:, ST_BANK + u % 2, 0:w], op_k[0:ROWS_M, slot, h, j * P:(j + 1) * P],
                                        op_q[0:ROWS_M, slot, h, q0:q0 + w], start=True, stop=not DIAG[s])
                if DIAG[s]:
                    last = nc.tensor.matmul(ps[:, ST_BANK + u % 2, 0:P], ident_b[:], causal_t[:], start=False,
                                            stop=True)
                last.then_inc(st_done.sem, 1)

            def weigh_values(turn, g, s):
                c, j = STEPS[s]
                n = g * NS + s
                pe.wait_ge(prob_ready.sem, prob_ready.at(turn, GH * (n + 1)))
                if j == 0:
                    pe.wait_ge(v_ready.sem, v_ready.at(turn, NT))
                    pe.wait_ge(out_ready.sem, out_ready.at(turn, (g - 1) * NC + c + 1))
                o, w = first_query(s) - c * BANK, width(s)
                for h in range(GH):
                    last = nc.tensor.matmul(ps[32 * h:32 * h + 32, OUT_BANK + c, o:o + w], v[:, j, g * GH + h, :],
                                            probs[:, n % 2, h, 0:w], start=(j == 0), stop=(o + P == BANK))
                last.then_inc(pv_done.sem, 1)

            def turn_out(turn, g, c):
                pe.wait_ge(raw_out_ready.sem, raw_out_ready.at(turn, g * NC + c + 1))
                for t in range(CT):
                    last = nc.tensor.transpose(ps[:, OUT_BANK + c, t * P:(t + 1) * P], out_raw[:, t * P:(t + 1) * P],
                                               ident[:])
                last.then_inc(raw_out_turned.sem, 1)

            def turn_out_all(turn, c):
                pe.wait_ge(out_ready.sem, out_ready.at(turn, G * NC))
                if c > 0:
                    pe.wait_ge(out_t_ready.sem, out_t_ready.at(turn, 2))
                for f in range(2):
                    for t in range(CT):
                        last = nc.tensor.transpose(ps[:, OUT_BANK + f, t * P:(t + 1) * P],
                                                   out_nat[:, c * CT + t, f * P:(f + 1) * P], ident[:])
                    last.then_inc(out_turned.sem, 1)

            def project_out(turn, t):
                pe.wait_ge(proj_scaled.sem, proj_scaled.at(turn, t - 1))
                if t % CT == 0:
                    pe.wait_ge(out_t_ready.sem, out_t_ready.at(turn, 2 * (t // CT) + 2))
                for f in range(2):
                    last = nc.tensor.matmul(ps[:, ST_BANK + t % 2, 0:E], out_t[:, f, t * P:(t + 1) * P], w_o[:, f, :],
                                            start=(f == 0), stop=(f == 1))
                last.then_inc(proj_done.sem, 1)

            def image(turn, last):
                for g in range(G):
                    for s in range(NS):
                        tiles = MAX_IN_STEP[g][s]
                        places = [tiles[len(tiles) * i // 4:len(tiles) * (i + 1) // 4] for i in range(4)]
                        scores_t(turn, g, s, 0)
                        scores_t(turn, g, s, 1)
                        for tile in places[0]:
                            scores(turn, g + 1, tile)
                        if s > 0:
                            weigh_values(turn, g, s - 1)
                        elif g > 0:
                            weigh_values(turn, g - 1, NS - 1)
                        for tile in places[1]:
                            scores(turn, g + 1, tile)
                        scores_t(turn, g, s, 2)
                        for tile in places[2]:
                            scores(turn, g + 1, tile)
                        scores_t(turn, g, s, 3)
                        if s == MAX_STEPS and g + 1 < G:
                            transpose_max(turn, g + 1)
                        for tile in places[3]:
                            scores(turn, g + 1, tile)
                        if s == 2 and g > 0:
                            turn_out(turn, g - 1, 1)
                        if s == 6:
                            turn_out(turn, g, 0)
                        if not last:
                            for c in range(NC):
                                if XT_AT[c] == (g, s):
                                    transpose_x(turn + 1, c)
                                if LAT_AT == (g, s):
                                    latents(turn + 1, c)
                            for n in range(8):
                                if QK_AT[n] == (g, s):
                                    features(turn + 1, n)
                weigh_values(turn, G - 1, NS - 1)
                first_lead, lead = (0, 0) if last else LEAD
                for tile in range(first_lead):
                    scores(turn + 1, 0, tile)
                turn_out(turn, G - 1, 1)
                for tile in range(first_lead, min(lead, first_lead + 2)):
                    scores(turn + 1, 0, tile)
                turn_out_all(turn, 0)
                turn_out_all(turn, 1)
                for tile in range(min(lead, first_lead + 2), lead):
                    scores(turn + 1, 0, tile)
                pe.wait_ge(prob_ready.sem, prob_ready.at(turn, G * UNITS))
                pe.sem_inc(ticks[1], 1)
                for t in range(NT):
                    project_out(turn, t)
                    if not last:
                        values(turn + 1, t)
                        for tile in tiles_beside(t):
                            scores(turn + 1, 0, tile)
                if not last:
                    transpose_max(turn + 1, 0)

            for c in range(NC):
                transpose_x(0, c)
            for c in range(NC):
                latents(0, c)
            for n in range(8):
                features(0, n)
            for t in range(NT):
                values(0, t)
            for tile in range(GH * NT):
                scores(0, 0, tile)
            transpose_max(0, 0)
            with pe.Fori(0, B - 1) as b:
                image(b, False)
            image(B - 1, True)


def qk_item(n):
    return (n % 2 + (2 if n >= 4 else 0)), (n // 2) % 2


def stage_b(nc, d, ident, gate_all, mod_all, out):
    with ExitStack() as ctx:
        sb = lambda n, s, t=F32: ctx.enter_context(nc.sbuf_tensor(n, s, t))
        sem = lambda n: ctx.enter_context(nc.semaphore(n))
        counters = []

        def cnt(name, per_turn):
            counters.append(Counter(ctx, nc, name, per_turn))
            return counters[-1]

        ps = ctx.enter_context(nc.psum_tensor("ps_ffn", [P, 8, BANK], F32))
        OUT_BANK, FRONT_BANK = 4, 6

        w_in = sb("w_in", [P, 2, 2, NF * 2 * HID], F32R)
        w_out = sb("w_out", [P, 2, NF * E], F32R)
        staged = sb("staged", [P, 4, 3, E])
        w_router = sb("w_router", [P, 2, NE])
        lower = sb("lower", [P, NE, NE])
        neg_half = sb("neg_half_b", [P, CT])
        x1 = sb("x1_b", [P, 2, CT, E])
        res = sb("res", [P, 2, CT, E])
        x_hat = sb("x_hat_b", [P, CT, E])
        h_t = sb("h_t", [P, 2, CH])
        h_parts = sb("h_parts", [P, 2, 2, 2, CH], F32R)
        stats, mean_var, rstd = sb("stats_b", [P, CT, 6]), sb("mean_var_b", [P, CT, 2]), sb("rstd_b", [P, CT])
        logits_t = sb("logits_t", [NE, CH])
        ex = sb("ex", [P, CT, NE])
        prob = sb("prob", [P, CT, NE])
        beats, ties = sb("beats", [P, CT, NE, NE]), sb("ties", [P, CT, NE, NE])
        rank = sb("rank", [P, CT, NE])
        combine = sb("combine", [P, CT, NE])
        total, inv = sb("total", [P, CT]), sb("inv", [P, CT])
        combine_t = sb("combine_t", [NE, CH])
        share = sb("share", [P, 2, NE, CH])
        act_g = sb("act_g", [P, 3, CH])
        hidden = sb("hidden", [P, 2, CH])
        hid_parts = sb("hid_parts", [P, 3, 2, CH], F32R)
        scaled = sb("scaled", [P, 2, BANK])
        y = sb("y", [P, 2, CT, E])
        mod = sb("mod_b", [P, 2, 4, 2])
        gate = sb("gate_b", [P, 2, E])
        combine_d = nc.dram_tensor("combine_d", [2, NE, CH], F32, kind="Internal").ap()

        raw_loaded = [sem(f"raw_loaded{i}") for i in range(4)]
        small_loaded = sem("small_loaded")
        w_hi, w_lo = sem("w_hi"), sem("w_lo")
        ticks = [sem(f"tick_b{i}") for i in range(3)]
        x1_loaded = [cnt(f"x1_loaded{i}", 16) for i in range(2)]
        res_loaded = [cnt(f"res_loaded_b{i}", 16) for i in range(2)]
        chain = cnt("chain_b", 2 * CHAIN)
        mod_ready = cnt("mod_ready_b", 2)
        var_ready, rstd_ready, xhat_ready = cnt("var_ready_b", 2), cnt("rstd_ready_b", 2), cnt("xhat_ready_b", 2 * CT)
        xt_done, ht_ready = cnt("xt_done_b", 4), cnt("ht_ready_b", 4)
        h_hi, h_lo = cnt("h_hi", 2), cnt("h_lo", 2)
        logit_done, logit_ready = cnt("logit_done", 2), cnt("logit_ready", 2)
        logit_t_done, exp_ready = cnt("logit_t_done", 2), cnt("exp_ready", 2)
        combine_ready, ct_done, ct_ready = cnt("combine_ready", 2), cnt("ct_done", 2), cnt("ct_ready", 2)
        combine_stored = cnt("combine_stored", 32)
        share_loaded = [cnt(f"share_loaded{i}", 16) for i in range(2)]
        gu_done, silu_ready, weighed = cnt("gu_done", 2 * NF), cnt("silu_ready_b", 2 * NF), cnt("weighed", 2 * NE)
        hid_ready, hid_hi, hid_lo = cnt("hid_ready", 2 * NF), cnt("hid_hi", 2 * NF), cnt("hid_lo", 2 * NF)
        down_done, scaled_ready = cnt("down_done", 2 * NF), cnt("scaled_ready", 4)
        y_ready = cnt("y_ready", 4)
        y_stored = [cnt(f"y_stored{i}", 16) for i in range(2)]

        def first(turn):
            return isinstance(turn, int) and turn == 0

        start_counters(nc, counters)
        block = ctx.enter_context(nc.Block())

        def parts_of(e, half):
            o = 2 * HID * e
            return w_in[:, :, half, o:o + 2 * HID], w_out[:, half, e * E:(e + 1) * E]

        @block.sync
        def _(sp):
            sp.dma_start(w_router[:], d["gate_w_t"].rearrange("(k p) e -> p k e", p=P)).then_inc(small_loaded, 16)
            sp.dma_start(lower[:], d["lower"].unsqueeze(0).broadcast_to([P, NE, NE])).then_inc(small_loaded, 16)

            def chunk_of_x1(turn, i):
                return d["x1"][bass.ds(turn, 1), i * CH:(i + 1) * CH, :].rearrange("o (t p) e -> p (o t) e", p=P)

            def front(turn, i):
                if not first(turn):
                    sp.wait_ge(xhat_ready.sem, xhat_ready.before(turn, CT * (i + 1) - 2 * CT))
                sp.sem_inc(ticks[0], 1)
                sp.dma_start(x1[:, i], chunk_of_x1(turn, i)).then_inc(x1_loaded[i].sem, 16)

            def load_residual(turn, i):
                sp.wait_ge(y_ready.sem, y_ready.at(turn, 2 * i))
                sp.sem_inc(ticks[0], 1)
                sp.dma_start(res[:, i], chunk_of_x1(turn, i)).then_inc(res_loaded[i].sem, 16)

            def combine_weights(turn, i):
                sp.wait_ge(ct_ready.sem, ct_ready.at(turn, i + 1))
                sp.dma_start(combine_d[i], combine_t[:]).then_inc(combine_stored.sem, 16)
                sp.wait_ge(combine_stored.sem, combine_stored.at(turn, 16 * (i + 1)))
                sp.sem_inc(ticks[0], 1)
                if not first(turn):
                    sp.wait_ge(weighed.sem, weighed.before(turn, NE * (i + 1) - 2 * NE))
                sp.dma_start(share[:, i], combine_d[i:i + 1].broadcast_to([P, NE, CH])).then_inc(
                    share_loaded[i].sem, 16)

            def store(turn, i):
                sp.wait_ge(y_ready.sem, y_ready.at(turn, 2 * i + 2))
                sp.sem_inc(ticks[0], 1)
                sp.dma_start(out[bass.ds(turn, 1), i * CH:(i + 1) * CH, :].rearrange("o (t p) e -> p (o t) e", p=P),
                             y[:, i]).then_inc(y_stored[i].sem, 16)

            front(0, 0)
            for e in range(NF):
                if e >= 4:
                    sp.wait_ge(w_lo, e - 3)
                o = 2 * HID * e
                sp.dma_start(staged[:, e % 4, 0:2, :], d["w_in_t"][:, :, o:o + 2 * HID].rearrange(
                    "k p n -> p k n")).then_inc(raw_loaded[e % 4], 16)
                sp.dma_start(staged[:, e % 4, 2, :], d["w_out_t"][:, e * E:(e + 1) * E]).then_inc(raw_loaded[e % 4], 16)
                if e == 0:
                    front(0, 1)
            combine_weights(0, 0)

            def turn_body(turn, last):
                load_residual(turn, 0)
                if not last:
                    front(turn + 1, 0)
                combine_weights(turn, 1)
                store(turn, 0)
                load_residual(turn, 1)
                if not last:
                    front(turn + 1, 1)
                    combine_weights(turn + 1, 0)
                store(turn, 1)

            with sp.Fori(0, B - 1) as t:
                turn_body(t, False)
            turn_body(B - 1, True)
            for i in range(2):
                sp.wait_ge(y_stored[i].sem, y_stored[i].at(B, 0))

        @block.gpsimd
        def _(pool):
            def front_1(turn, i):
                pool.wait_ge(var_ready.sem, var_ready.at(turn, i + 1))
                nc.gpsimd.tensor_tensor(rstd[:], rstd[:], neg_half[:], ALU.pow).then_inc(rstd_ready.sem, 1)

            def front_2(turn, i):
                pool.wait_ge(h_hi.sem, h_hi.at(turn, i + 1))
                nc.gpsimd.tensor_tensor(h_parts[:, i, 1], h_t[:], h_parts[:, i, 0].bitcast(F32),
                                        ALU.subtract).then_inc(h_lo.sem, 1)

            def weigh(turn, i, e):
                n, x_ = i * NF + e, e - 2
                pool.wait_ge(silu_ready.sem, silu_ready.at(turn, n + 1))
                if x_ == 0:
                    pool.wait_ge(share_loaded[i].sem, share_loaded[i].at(turn, 16))
                nc.gpsimd.tensor_tensor(act_g[:, n % 3, :], act_g[:, n % 3, :], share[:, i, x_, :],
                                        ALU.mult).then_inc(weighed.sem, 1)

            def lo_part(turn, i, e):
                n = i * NF + e
                pool.wait_ge(hid_hi.sem, hid_hi.at(turn, n + 1))
                pool.wait_ge(down_done.sem, down_done.at(turn, n - 2))
                nc.gpsimd.tensor_tensor(hid_parts[:, n % 3, 1, :], hidden[:, n % 2, :],
                                        hid_parts[:, n % 3, 0, :].bitcast(F32), ALU.subtract).then_inc(hid_lo.sem, 1)

            for e in range(NF):
                pool.wait_ge(w_hi, e + 1)
                for lo, hi, raw in ((parts_of(e, 1)[0], parts_of(e, 0)[0], staged[:, e % 4, 0:2, :]),
                                    (parts_of(e, 1)[1], parts_of(e, 0)[1], staged[:, e % 4, 2, :])):
                    last = nc.gpsimd.tensor_tensor(lo, raw, hi.bitcast(F32), ALU.subtract)
                last.then_inc(w_lo, 1)
                if e == 0:
                    front_1(0, 0)
                if e == 2:
                    front_2(0, 0)

            def turn_body(turn, last):
                for i in range(2):
                    nxt = (turn, 1) if i == 0 else (turn + 1, 0)
                    for e in range(NF):
                        if e >= 2:
                            weigh(turn, i, e)
                        if e >= 1:
                            lo_part(turn, i, e - 1)
                        if not (i and last):
                            if e == FRONT_AT[0]:
                                front_1(*nxt)
                            if e == FRONT_AT[1]:
                                front_2(*nxt)
                    lo_part(turn, i, NF - 1)

            with pool.Fori(0, B - 1) as t:
                turn_body(t, False)
            turn_body(B - 1, True)

        @block.scalar
        def _(act):
            def router_exp(turn, i):
                act.wait_ge(logit_t_done.sem, logit_t_done.at(turn, i + 1))
                act.wait_ge(combine_ready.sem, combine_ready.at(turn, i))
                nc.scalar.activation(ex[:], ps[:, FRONT_BANK + 1, 0:CT * NE].rearrange("p (t e) -> p t e", e=NE),
                                     ACT.Exp, scale=-1.0).then_inc(exp_ready.sem, 1)

            router_exp(0, 0)

            def turn_body(turn, last):
                for i in range(2):
                    nxt = (turn, 1) if i == 0 else (turn + 1, 0)
                    for e in range(NF):
                        n = i * NF + e
                        act.wait_ge(gu_done.sem, gu_done.at(turn, n + 1))
                        act.wait_ge(hid_ready.sem, hid_ready.at(turn, n - 2))
                        nc.scalar.activation(act_g[:, n % 3, :], ps[:, 2 * (n % 2), :],
                                             ACT.Silu).then_inc(silu_ready.sem, 1)
                        if e == FRONT_AT[2] and not (i and last):
                            router_exp(*nxt)

            with act.Fori(0, B - 1) as t:
                turn_body(t, False)
            turn_body(B - 1, True)

        @block.vector
        def _(dve):
            nc.vector.memset(neg_half[:], -0.5)

            def front_1(turn, i):
                if i == 0:
                    dve.wait_ge(ht_ready.sem, ht_ready.at(turn, 0))
                src = mod_all[:, turn:turn + 1] if isinstance(turn, int) else mod_all[:, bass.ds(turn, 1)]
                gsrc = gate_all[:, 1, turn:turn + 1] if isinstance(turn, int) else gate_all[:, 1, bass.ds(turn, 1)]
                nc.vector.tensor_copy(mod[:, i:i + 1], src)
                nc.vector.tensor_copy(gate[:, i:i + 1], gsrc).then_inc(mod_ready.sem, 1)
                dve.wait_ge(x1_loaded[i].sem, x1_loaded[i].at(turn, 16))
                for t in range(CT):
                    last = nc.vector.bn_stats(stats[:, t, :], x1[:, i, t, :])
                last.then_inc(chain.sem, 1)
                dve.wait_ge(chain.sem, chain.at(turn, CHAIN * i + 1))
                dve.sem_inc(ticks[2], 1)
                for t in range(CT):
                    last = nc.vector.bn_aggr(mean_var[:, t, :], stats[:, t, :])
                last.then_inc(chain.sem, 1)
                dve.wait_ge(chain.sem, chain.at(turn, CHAIN * i + 2))
                nc.vector.tensor_scalar(rstd[:], mean_var[:, :, 1], EPS, None, ALU.add).then_inc(var_ready.sem, 1)

            def front_2(turn, i):
                dve.wait_ge(rstd_ready.sem, rstd_ready.at(turn, i + 1))
                dve.wait_ge(xt_done.sem, xt_done.at(turn, 2 * i))
                for t in range(CT):
                    nc.vector.tensor_scalar(x_hat[:, t, :], x1[:, i, t, :], mean_var[:, t, 0:1], rstd[:, t:t + 1],
                                            ALU.subtract, ALU.mult).then_inc(xhat_ready.sem, 1)

            def front_3(turn, i):
                dve.wait_ge(mod_ready.sem, mod_ready.at(turn, i + 1))
                dve.wait_ge(h_lo.sem, h_lo.at(turn, i))
                dve.wait_ge(logit_done.sem, logit_done.at(turn, i))
                dve.wait_ge(xt_done.sem, xt_done.at(turn, 2 * i + 2))
                for f in range(2):
                    nc.vector.tensor_scalar(h_t[:, f, :], ps[:, FRONT_BANK + f, :], mod[:, i, 3, f:f + 1],
                                            mod[:, i, 2, f:f + 1], ALU.mult, ALU.add).then_inc(ht_ready.sem, 1)
                dve.wait_ge(ht_ready.sem, ht_ready.at(turn, 2 * i + 2))
                if not first(turn):
                    dve.wait_ge(gu_done.sem, gu_done.before(turn, NF * (i + 1) - 2 * NF))
                nc.vector.tensor_copy(h_parts[:, i, 0], h_t[:]).then_inc(h_hi.sem, 1)

            def front_4(turn, i):
                dve.wait_ge(logit_done.sem, logit_done.at(turn, i + 1))
                nc.vector.tensor_copy(logits_t[:], ps[0:NE, FRONT_BANK, :]).then_inc(logit_ready.sem, 1)

            def front_5(turn, i):
                dve.wait_ge(exp_ready.sem, exp_ready.at(turn, i + 1))
                nc.vector.tensor_scalar(prob[:], ex[:], 1.0, None, ALU.add).then_inc(chain.sem, 1)
                dve.wait_ge(chain.sem, chain.at(turn, CHAIN * i + 3))
                nc.vector.reciprocal(prob[:], prob[:]).then_inc(chain.sem, 1)
                dve.wait_ge(chain.sem, chain.at(turn, CHAIN * i + 4))
                mine = prob[:].unsqueeze(3).broadcast_to([P, CT, NE, NE])
                other = prob[:].unsqueeze(2).broadcast_to([P, CT, NE, NE])
                nc.vector.tensor_tensor(beats[:], other, mine, ALU.is_gt)
                nc.vector.tensor_tensor(ties[:], other, mine, ALU.is_equal).then_inc(chain.sem, 1)
                dve.wait_ge(chain.sem, chain.at(turn, CHAIN * i + 5))
                nc.vector.tensor_tensor(ties[:], ties[:], lower[:].unsqueeze(1).broadcast_to([P, CT, NE, NE]),
                                        ALU.mult).then_inc(chain.sem, 1)
                dve.wait_ge(chain.sem, chain.at(turn, CHAIN * i + 6))
                nc.vector.tensor_tensor(beats[:], beats[:], ties[:], ALU.add).then_inc(chain.sem, 1)
                dve.wait_ge(chain.sem, chain.at(turn, CHAIN * i + 7))
                nc.vector.tensor_reduce(rank[:], beats[:], AX.X, ALU.add).then_inc(chain.sem, 1)
                dve.wait_ge(chain.sem, chain.at(turn, CHAIN * i + 8))
                nc.vector.scalar_tensor_tensor(combine[:], rank[:], TOPK - 0.5, prob[:], ALU.is_lt, ALU.mult).then_inc(
                    chain.sem, 1)
                dve.wait_ge(chain.sem, chain.at(turn, CHAIN * i + 9))
                nc.vector.tensor_reduce(total[:], combine[:], AX.X, ALU.add).then_inc(chain.sem, 1)
                dve.wait_ge(chain.sem, chain.at(turn, CHAIN * i + 10))
                nc.vector.tensor_scalar(total[:], total[:], 1e-20, None, ALU.add).then_inc(chain.sem, 1)
                dve.wait_ge(chain.sem, chain.at(turn, CHAIN * i + 11))
                nc.vector.reciprocal(inv[:], total[:]).then_inc(chain.sem, 1)
                dve.wait_ge(chain.sem, chain.at(turn, CHAIN * i + 12))
                nc.vector.tensor_scalar(inv[:], inv[:], ROUTE_SCALE, None, ALU.mult).then_inc(chain.sem, 1)
                dve.wait_ge(chain.sem, chain.at(turn, CHAIN * i + 13))
                nc.vector.tensor_tensor(combine[:], combine[:], inv[:].unsqueeze(2).broadcast_to([P, CT, NE]),
                                        ALU.mult).then_inc(combine_ready.sem, 1)

            def front_6(turn, i):
                dve.wait_ge(ct_done.sem, ct_done.at(turn, i + 1))
                dve.wait_ge(combine_stored.sem, combine_stored.at(turn, 16 * i))
                nc.vector.tensor_copy(combine_t[:], ps[0:NE, FRONT_BANK, :]).then_inc(ct_ready.sem, 1)

            def hidden_tile(turn, i, e):
                n = i * NF + e
                dve.wait_ge(silu_ready.sem, silu_ready.at(turn, n + 1))
                dve.wait_ge(gu_done.sem, gu_done.at(turn, n + 1))
                if e >= 2:
                    dve.wait_ge(weighed.sem, weighed.at(turn, i * NE + e - 1))
                dve.wait_ge(hid_lo.sem, hid_lo.at(turn, n - 1))
                nc.vector.tensor_tensor(hidden[:, n % 2, :], ps[:, 2 * (n % 2) + 1, :], act_g[:, n % 3, :],
                                        ALU.mult).then_inc(hid_ready.sem, 1)
                dve.wait_ge(hid_ready.sem, hid_ready.at(turn, n + 1))
                dve.wait_ge(down_done.sem, down_done.at(turn, n - 2))
                nc.vector.tensor_copy(hid_parts[:, n % 3, 0, :], hidden[:, n % 2, :]).then_inc(hid_hi.sem, 1)

            def residual(turn, i):
                dve.wait_ge(down_done.sem, down_done.at(turn, NF * (i + 1)))
                dve.wait_ge(y_stored[i].sem, y_stored[i].at(turn, 0))
                dve.wait_ge(res_loaded[i].sem, res_loaded[i].at(turn, 16))
                for q in range(2):
                    k = 2 * i + q
                    dve.wait_ge(y_ready.sem, y_ready.at(turn, k))
                    nc.vector.tensor_tensor(scaled[:, q, :].rearrange("p (t e) -> p t e", e=E),
                                            ps[:, OUT_BANK + q, :].rearrange("p (t e) -> p t e", e=E),
                                            gate[:, i].unsqueeze(1).broadcast_to([P, 2, E]),
                                            ALU.mult).then_inc(scaled_ready.sem, 1)
                    dve.wait_ge(scaled_ready.sem, scaled_ready.at(turn, k + 1))
                    nc.vector.tensor_tensor(y[:, i, 2 * q:2 * q + 2, :], res[:, i, 2 * q:2 * q + 2, :],
                                            scaled[:, q, :].rearrange("p (t e) -> p t e", e=E),
                                            ALU.add).then_inc(y_ready.sem, 1)

            dve.wait_ge(small_loaded, 32)
            def split_weights(e):
                dve.wait_ge(raw_loaded[e % 4], 32 * (e // 4 + 1))
                w_in_hi, w_out_hi = parts_of(e, 0)
                nc.vector.tensor_copy(w_in_hi, staged[:, e % 4, 0:2, :])
                nc.vector.tensor_copy(w_out_hi, staged[:, e % 4, 2, :]).then_inc(w_hi, 1)

            front_1(0, 0)
            split_weights(0)
            front_2(0, 0)
            split_weights(1)
            front_3(0, 0)
            split_weights(2)
            front_4(0, 0)
            split_weights(3)
            front_5(0, 0)
            front_6(0, 0)
            for e in range(4, NF):
                split_weights(e)

            def turn_body(turn, last):
                for i in range(2):
                    nxt = (turn, 1) if i == 0 else (turn + 1, 0)
                    for e in range(NF):
                        if not (i and last):
                            if e == FRONT_AT[0]:
                                front_1(*nxt)
                            if e == FRONT_AT[0] + 1:
                                front_2(*nxt)
                            if e == FRONT_AT[1]:
                                front_3(*nxt)
                            if e == FRONT_AT[1] + 1:
                                front_4(*nxt)
                            if e == FRONT_AT[2] + 1:
                                front_5(*nxt)
                            if e == FRONT_AT[3] + 1:
                                front_6(*nxt)
                        hidden_tile(turn, i, e)
                        if i == 1 and e == LAG - 1:
                            residual(turn, 0)
                residual(turn, 1)

            with dve.Fori(0, B - 1) as t:
                turn_body(t, False)
            turn_body(B - 1, True)

        @block.tensor
        def _(pe):
            pe.wait_ge(small_loaded, 32)

            def front_transpose(turn, i):
                pe.wait_ge(ct_ready.sem, ct_ready.at(turn, i))
                for f in range(2):
                    for t in range(CT):
                        pe.wait_ge(xhat_ready.sem, xhat_ready.at(turn, CT * i + t + 1))
                        last = nc.tensor.transpose(ps[:, FRONT_BANK + f, t * P:(t + 1) * P],
                                                   x_hat[:, t, f * P:(f + 1) * P], ident[:])
                    last.then_inc(xt_done.sem, 1)

            def front_router(turn, i):
                pe.wait_ge(ht_ready.sem, ht_ready.at(turn, 2 * i + 2))
                for f in range(2):
                    last = nc.tensor.matmul(ps[0:NE, FRONT_BANK, :], w_router[:, f, :], h_t[:, f, :],
                                            start=(f == 0), stop=(f == 1))
                last.then_inc(logit_done.sem, 1)

            def front_logits(turn, i):
                pe.wait_ge(logit_ready.sem, logit_ready.at(turn, i + 1))
                pe.sem_inc(ticks[1], 1)
                for t in range(CT):
                    last = nc.tensor.transpose(ps[:, FRONT_BANK + 1, t * NE:(t + 1) * NE], logits_t[:, t * P:(t + 1) * P],
                                               ident[0:NE, 0:NE])
                last.then_inc(logit_t_done.sem, 1)

            def front_combine(turn, i):
                pe.wait_ge(combine_ready.sem, combine_ready.at(turn, i + 1))
                for t in range(CT):
                    last = nc.tensor.transpose(ps[0:NE, FRONT_BANK, t * P:(t + 1) * P], combine[:, t, :], ident[:])
                last.then_inc(ct_done.sem, 1)

            def products(dst, stationary, moving, start, stop):
                for k, (a, c) in enumerate(((0, 0), (0, 1), (1, 0))):
                    last = nc.tensor.matmul(dst, stationary(a), moving(c), start=start and k == 0, stop=stop and k == 2,
                                            skip_group_check=True)
                return last

            def gate_up(turn, i, e):
                n = i * NF + e
                if i == 0:
                    pe.wait_ge(w_lo, e + 1)
                if e == 0:
                    pe.wait_ge(h_hi.sem, h_hi.at(turn, i + 1))
                    pe.wait_ge(h_lo.sem, h_lo.at(turn, i + 1))
                pe.wait_ge(hid_ready.sem, hid_ready.at(turn, n - 1))
                for u in range(2):
                    for f in range(2):
                        o = (2 * e + u) * HID
                        last = products(ps[:, 2 * (n % 2) + u, :], lambda a: w_in[:, f, a, o:o + HID],
                                        lambda c: h_parts[:, i, c, f, :], f == 0, f == 1)
                last.then_inc(gu_done.sem, 1)

            def down(turn, i, e):
                n = i * NF + e
                if e == 0:
                    pe.wait_ge(scaled_ready.sem, scaled_ready.at(turn, 2 * i))
                pe.wait_ge(hid_hi.sem, hid_hi.at(turn, n + 1))
                pe.wait_ge(hid_lo.sem, hid_lo.at(turn, n + 1))
                for t in range(CT):
                    last = products(ps[:, OUT_BANK + t // 2, (t % 2) * E:(t % 2 + 1) * E],
                                    lambda a: hid_parts[:, n % 3, a, t * P:(t + 1) * P],
                                    lambda c: w_out[:, c, e * E:(e + 1) * E], e == 0 and t % 2 == 0,
                                    e == NF - 1)
                last.then_inc(down_done.sem, 1)

            front_transpose(0, 0)
            front_router(0, 0)
            front_logits(0, 0)
            front_combine(0, 0)

            def turn_body(turn, last):
                for i in range(2):
                    nxt = (turn, 1) if i == 0 else (turn + 1, 0)
                    for e in range(NF):
                        gate_up(turn, i, e)
                        if not (i and last):
                            if e == FRONT_AT[0] + 1:
                                front_transpose(*nxt)
                            if e == FRONT_AT[1]:
                                front_router(*nxt)
                            if e == FRONT_AT[2]:
                                front_logits(*nxt)
                            if e == FRONT_AT[3]:
                                front_combine(*nxt)
                        if e >= LAG:
                            down(turn, i, e - LAG)
                        elif i == 1:
                            down(turn, 0, NF - LAG + e)
                for e in range(NF - LAG, NF):
                    down(turn, 1, e)

            with pe.Fori(0, B - 1) as t:
                turn_body(t, False)
            turn_body(B - 1, True)


LAG = 2
CHAIN = 13
FRONT_AT = (2, 4, 6, 8)


def build(nc, ins, out):
    with ExitStack() as ctx:
        sb = lambda n, s, t=F32: ctx.enter_context(nc.sbuf_tensor(n, s, t))
        ident, causal_sb = sb("ident", [P, P]), sb("causal_sb", [P, 2, P])
        gate_all, mod_all = sb("gate_all", [P, 2, B, E]), sb("mod_all", [P, B, 4, 2])
        const_loaded = ctx.enter_context(nc.semaphore("const_loaded"))
        d = dict(ins)
        d["x1"] = nc.dram_tensor("x1", [B, S, E], F32, kind="Internal").ap()
        d["causal_sb"] = causal_sb
        with nc.Block() as block:
            @block.sync
            def _(sp):
                sp.dma_start(ident[:], d["ident"]).then_inc(const_loaded, 16)
                sp.dma_start(causal_sb[:], d["causal"].rearrange("a p n -> p a n")).then_inc(const_loaded, 16)
                sp.wait_ge(const_loaded, 32)
        stage_0(nc, d, gate_all, mod_all)
        stage_a(nc, d, ident, gate_all, mod_all)
        stage_b(nc, d, ident, gate_all, mod_all, out)


def kernel(**inputs):
    import concourse.bacc as bacc
    from concourse.bass_utils import run_bass_kernel_spmd

    a = {k.removeprefix("L0_").removeprefix("attn_").removeprefix("ffn_"): np.asarray(t) for k, t in inputs.items()}
    put = {n: a[n] for n in ("x", "wq", "bq", "wqc", "bqc", "wqr", "bqr", "wkv", "bkv", "wkr", "bkr", "wkc", "bkc",
                             "wv", "bv", "wo", "bo", "wmod")}
    put["cT"] = a["c"].T
    put["gate_w_t"] = a["gate_weight"].T
    w_g = np.concatenate([a["ws_gate"].reshape(2, HID, E), a["w_gate"]])
    w_u = np.concatenate([a["ws_up"].reshape(2, HID, E), a["w_up"]])
    w_in = np.stack([w_g, w_u], axis=1).transpose(3, 0, 1, 2).reshape(2, P, NF * 2 * HID)
    put["w_in_t"] = w_in
    w_d = np.concatenate([a["ws_down"].reshape(E, 2, HID).transpose(1, 2, 0), a["w_down"].transpose(0, 2, 1)])
    put["w_out_t"] = w_d.transpose(1, 0, 2).reshape(HID, NF * E)
    inv_freq = (np.float32(1) / np.float32(10000) ** (np.arange(0, DR, 2, dtype=np.float32) / np.float32(DR)))
    angle = (np.arange(S, dtype=np.float32)[:, None] * inv_freq[None, :]).T
    angle = np.concatenate([angle, angle]).astype(np.float32)
    put["cos"] = np.cos(angle)
    put["sin"] = np.sin(angle) * np.where(np.arange(DR) < DR // 2, 1, -1).astype(np.float32)[:, None]
    put["ident"] = np.eye(P, dtype=np.float32)
    later = np.arange(P)[None, :] > np.arange(P)[:, None]
    put["causal"] = np.where(np.stack([later, later.T]), np.float32(NEG), np.float32(0))
    put["lower"] = (np.arange(NE)[None, :] < np.arange(NE)[:, None]).astype(np.float32)

    nc = bacc.Bacc("TRN2", target_bir_lowering=False, num_devices=1)
    ins, arrays = {}, {}
    for n, t in put.items():
        t = np.ascontiguousarray(t)
        arrays["in_" + n] = t
        ins[n] = nc.dram_tensor("in_" + n, t.shape, mybir.dt.from_np(t.dtype), kind="ExternalInput").ap()
    out = nc.dram_tensor("out", [B, S, E], F32, kind="ExternalOutput").ap()
    build(nc, ins, out)
    r = run_bass_kernel_spmd(nc, [arrays], core_ids=[0])
    return np.asarray(r.results[0]["out"])
```
